# Optimizing a Trainium2 kernel written in Bass

```python
import numpy as np
import jax
import jax.numpy as jnp

def _softmax(x, axis=-1):
    return jax.nn.softmax(x, axis=axis)

def _gelu(x):
    return jax.nn.gelu(x, approximate=True)

def _silu(x):
    return jax.nn.silu(x)

def _sigmoid(x):
    return jax.nn.sigmoid(x)

def _layernorm(x, axis=-1, eps=1e-05):
    m = jnp.mean(x, axis=axis, keepdims=True)
    v = jnp.var(x, axis=axis, keepdims=True)
    return (x - m) / jnp.sqrt(v + eps)

def _scatter_add(tgt, idx, src, axis=0):
    return tgt.at[idx].add(src)

def _segment_sum(src, seg, n):
    return jax.ops.segment_sum(src, seg, n)
kernel_name = 'mk_gnn_ffn_d1_gnn_r8_2860dc'

def setup_inputs(seed: int=0):
    np.random.seed(seed)
    _w = jnp.asarray

    def _rec_inputs():
        import jax
        import jax.numpy as jnp
        _gk = jax.random.key(seed)
        x = -0.0003713 + 1 * jax.random.normal(jax.random.fold_in(_gk, 1), (6250, 256), jnp.float32)
        _s = jax.random.randint(jax.random.fold_in(_gk, 2), (50000,), 0, 6250, jnp.int32)
        _d = jax.random.randint(jax.random.fold_in(_gk, 3), (50000,), 0, 6250, jnp.int32)
        _loop = jnp.arange(6250, dtype=jnp.int32)
        src = jnp.concatenate([_s, _d, _loop])
        dst = jnp.concatenate([_d, _s, _loop])
        _o = jnp.argsort(dst, stable=True)
        src = src[_o]
        dst = dst[_o]
        return (x, src, dst)
    x, src, dst = _rec_inputs()

    def _L0_gnn_setup():
        import jax, jax.numpy as jnp
        import numpy as np
        N = 6250
        D = 256
        H = 4
        C = D // H
        E = 100000
        NEG_SLOPE = 0.2
        BN_EPS = 1e-05

        def _batchnorm(x, gamma, beta):
            mean = jnp.mean(x, axis=0)
            var = jnp.mean(jnp.square(x - mean), axis=0)
            return gamma * (x - mean) * jax.lax.rsqrt(var + BN_EPS) + beta
        key = jax.random.key(seed)
        ks = jax.random.split(key, 16)
        s = 0.05
        return {'x': jax.random.normal(ks[0], (N, D), dtype=jnp.float32), 'edge_index': jax.random.randint(ks[1], (2, E), 0, N, dtype=jnp.int64), 'W_l': jax.random.normal(ks[2], (D, H * C), dtype=jnp.float32) * s, 'W_r': jax.random.normal(ks[3], (D, H * C), dtype=jnp.float32) * s, 'att': jax.random.normal(ks[4], (H, C), dtype=jnp.float32) * s, 'bias': jnp.zeros((H * C,), dtype=jnp.float32), 'W1': jax.random.normal(ks[5], (D, D), dtype=jnp.float32) * s, 'b1': jnp.zeros((D,), dtype=jnp.float32), 'W2': jax.random.normal(ks[6], (D, D), dtype=jnp.float32) * s, 'b2': jnp.zeros((D,), dtype=jnp.float32), 'gamma1': jnp.ones((D,), dtype=jnp.float32), 'beta1': jnp.zeros((D,), dtype=jnp.float32), 'gamma2': jnp.ones((D,), dtype=jnp.float32), 'beta2': jnp.zeros((D,), dtype=jnp.float32)}
    _L0_gnn_all = _L0_gnn_setup()
    _L0_gnn_in = {k: v for k, v in _L0_gnn_all.items() if k in ('W_l', 'W_r', 'att', 'bias', 'W1', 'b1', 'W2', 'b2', 'gamma1', 'beta1', 'gamma2', 'beta2')}
    del _L0_gnn_all

    def _L0_ffn_setup():
        import jax, jax.numpy as jnp
        import numpy as np
        B, S, D, E, H, K = (4, 512, 256, 8, 512, 2)
        key = jax.random.key(seed)
        ks = jax.random.split(key, 6)
        x = jax.random.normal(ks[0], (B, S, D), jnp.float32)
        Wg = jax.random.normal(ks[1], (D, E), jnp.float32) * 0.02
        bg = jnp.zeros((E,), jnp.float32)
        W1 = jax.random.normal(ks[2], (E, D, H), jnp.float32) * 0.02
        b1 = jnp.zeros((E, H), jnp.float32)
        W2 = jax.random.normal(ks[3], (E, H, D), jnp.float32) * 0.02
        b2 = jnp.zeros((E, D), jnp.float32)
        return {'x': x, 'Wg': Wg, 'bg': bg, 'W1': W1, 'b1': b1, 'W2': W2, 'b2': b2}
    _L0_ffn_all = _L0_ffn_setup()
    _L0_ffn_in = {k: v for k, v in _L0_ffn_all.items() if k in ('Wg', 'bg', 'W1', 'b1', 'W2', 'b2')}
    del _L0_ffn_all
    return {'x': x, 'src': src, 'dst': dst, 'L0_gnn_W_l': _L0_gnn_in['W_l'], 'L0_gnn_W_r': _L0_gnn_in['W_r'], 'L0_gnn_att': _L0_gnn_in['att'], 'L0_gnn_bias': _L0_gnn_in['bias'], 'L0_gnn_W1': _L0_gnn_in['W1'], 'L0_gnn_b1': _L0_gnn_in['b1'], 'L0_gnn_W2': _L0_gnn_in['W2'], 'L0_gnn_b2': _L0_gnn_in['b2'], 'L0_gnn_gamma1': _L0_gnn_in['gamma1'], 'L0_gnn_beta1': _L0_gnn_in['beta1'], 'L0_gnn_gamma2': _L0_gnn_in['gamma2'], 'L0_gnn_beta2': _L0_gnn_in['beta2'], 'L0_ffn_Wg': _L0_ffn_in['Wg'], 'L0_ffn_bg': _L0_ffn_in['bg'], 'L0_ffn_W1': _L0_ffn_in['W1'], 'L0_ffn_b1': _L0_ffn_in['b1'], 'L0_ffn_W2': _L0_ffn_in['W2'], 'L0_ffn_b2': _L0_ffn_in['b2']}

def reference(x, src, dst, L0_gnn_W_l, L0_gnn_W_r, L0_gnn_att, L0_gnn_bias, L0_gnn_W1, L0_gnn_b1, L0_gnn_W2, L0_gnn_b2, L0_gnn_gamma1, L0_gnn_beta1, L0_gnn_gamma2, L0_gnn_beta2, L0_ffn_Wg, L0_ffn_bg, L0_ffn_W1, L0_ffn_b1, L0_ffn_W2, L0_ffn_b2):
    import jax
    import jax.numpy as jnp

    def _L0_gnn_ref(x, edge_index, W_l, W_r, att, bias, W1, b1, W2, b2, gamma1, beta1, gamma2, beta2):
        import jax, jax.numpy as jnp
        import numpy as np
        N = 6250
        D = 256
        H = 4
        C = D // H
        E = 100000
        NEG_SLOPE = 0.2
        BN_EPS = 1e-05

        def _batchnorm(x, gamma, beta):
            mean = jnp.mean(x, axis=0)
            var = jnp.mean(jnp.square(x - mean), axis=0)
            return gamma * (x - mean) * jax.lax.rsqrt(var + BN_EPS) + beta
        n = x.shape[0]
        loop = jnp.arange(n, dtype=edge_index.dtype)
        src = jnp.concatenate([edge_index[0], loop])
        dst = jnp.concatenate([edge_index[1], loop])
        xl = (x @ W_l).reshape(n, H, C)
        xr = (x @ W_r).reshape(n, H, C)
        feat = xl[src] + xr[dst]
        feat = jnp.where(feat >= 0, feat, NEG_SLOPE * feat)
        logits = jnp.einsum('ehc,hc->eh', feat, att)
        seg_max = jax.ops.segment_max(logits, dst, num_segments=n)
        ex = jnp.exp(logits - seg_max[dst])
        seg_sum = jax.ops.segment_sum(ex, dst, num_segments=n)
        alpha = ex / (seg_sum[dst] + 1e-16)
        msg = alpha[:, :, None] * xl[src]
        out = jax.ops.segment_sum(msg, dst, num_segments=n)
        x_attn = out.reshape(n, H * C) + bias
        h = _batchnorm(x_attn + x, gamma1, beta1)
        ffn = jax.nn.relu(h @ W1 + b1) @ W2 + b2
        return _batchnorm(ffn + h, gamma2, beta2)

    def _L0_ffn_ref(x, Wg, bg, W1, b1, W2, b2):
        import jax, jax.numpy as jnp
        import numpy as np
        B, S, D, E, H, K = (4, 512, 256, 8, 512, 2)
        Bv, Sv, Dv = x.shape
        gate_scores = x @ Wg + bg
        _, idx = jax.lax.top_k(gate_scores, K)
        mask = jax.nn.one_hot(idx, E, dtype=x.dtype).sum(axis=-2)
        xf = x.reshape(-1, Dv)
        mf = mask.reshape(-1, E)
        h = jax.nn.gelu(jnp.einsum('td,edh->teh', xf, W1) + b1[None], approximate=False)
        y = jnp.einsum('teh,ehd->ted', h, W2) + b2[None]
        out = jnp.einsum('ted,te->td', y, mf)
        return out.reshape(Bv, Sv, Dv)
    edge_index = jnp.stack([src, dst])
    x = x + _L0_gnn_ref(_layernorm(x, axis=-1), edge_index, L0_gnn_W_l, L0_gnn_W_r, L0_gnn_att, L0_gnn_bias, L0_gnn_W1, L0_gnn_b1, L0_gnn_W2, L0_gnn_b2, L0_gnn_gamma1, L0_gnn_beta1, L0_gnn_gamma2, L0_gnn_beta2)
    x = x + _L0_ffn_ref(_layernorm(x, axis=-1)[None], L0_ffn_Wg, L0_ffn_bg, L0_ffn_W1, L0_ffn_b1, L0_ffn_W2, L0_ffn_b2)[0]
    return x

_drawn_inputs = setup_inputs


def setup_inputs(seed=0):
    import zlib

    import numpy as np

    out = dict(_drawn_inputs(seed))
    spreads = {'L0_gnn_bias': (0.0, 2.0),
     'L0_gnn_b1': (0.0, 0.329),
     'L0_gnn_b2': (0.0, 2.0),
     'L0_gnn_gamma1': (1.0, 0.2),
     'L0_gnn_beta1': (0.0, 0.415),
     'L0_gnn_gamma2': (1.0, 0.2),
     'L0_gnn_beta2': (0.0, 0.1),
     'L0_ffn_bg': (0.0, 0.1),
     'L0_ffn_b1': (0.0, 0.448),
     'L0_ffn_b2': (0.0, 0.1)}
    factors = {'L0_gnn_W_r': 34.394}
    for name, (base, spread) in spreads.items():
        noise = np.random.default_rng([zlib.crc32(name.encode()), seed]).standard_normal(out[name].shape)
        drawn = base * np.exp(spread * noise) if base else spread * noise
        out[name] = jnp.asarray(drawn.astype(out[name].dtype))
    for name, factor in factors.items():
        out[name] = (out[name] * factor).astype(out[name].dtype)
    return out
```

```python
from contextlib import ExitStack

import concourse.bass as bass
import numpy as np
from concourse import mybir

F32 = mybir.dt.float32
BF16 = mybir.dt.bfloat16
I32 = mybir.dt.int32
U32 = mybir.dt.uint32
ALU = mybir.AluOpType
ACT = mybir.ActivationFunctionType
AX = mybir.AxisListType

P = 128
N = 6250
D = 256
DH = D // P
H = 4
C = D // H
SLOPE = 0.2
EPS = 1e-5
SEG_EPS = 1e-16
NEG = 2.0 ** 100

EDGES = 106250
NT = (N + P - 1) // P
NTAIL = N - (NT - 1) * P
NTP = NT + 1
COLS = NTP * P
ET = (EDGES + P - 1) // P
T = 32
NCH = (ET + T - 1) // T
ETL = NCH * T
Q = (ETL + P - 1) // P
ETP = Q * P
FULLQ = EDGES // (P * P)
ROWS_LAST = (EDGES - FULLQ * P * P) // P
EDGES_LAST = EDGES - FULLQ * P * P - ROWS_LAST * P
GATES = 2 * H * (T + 1) + 2 * H * T
XW = D + 8

E = 8
HID = 512
HC = HID // P
K = 2
R = 125
TILES = N // R
W = 2 * R
CHUNKS = N // W
REGION = NT * P + P
SLOT_TILES = (K * N + E * (P - 1)) // P
SLOT_TILES += SLOT_TILES % 2
ZW = D + 1
NO_ROW = 4 * COLS


def link_on(engine, semaphore):
    count = [0]

    def link(ins):
        count[0] += 1
        ins.then_inc(semaphore, 1)
        engine.wait_ge(semaphore, count[0])

    return link


def tiles(engine, n, front, unroll, body):
    for t in range(front):
        body(t, t % unroll)
    rounds = (n - front) // unroll
    if rounds:
        with engine.Fori(0, rounds) as i:
            for u in range(unroll):
                body(i * unroll + (front + u), (front + u) % unroll)
    for t in range(front + rounds * unroll, n):
        body(t, t % unroll)


def wait_past(engine, semaphore, value):
    if isinstance(value, int) and value <= 0:
        return
    engine.wait_ge(semaphore, value)


def gate_views(row):
    f, b = H * (T + 1), H * T
    cut = lambda at, n: row[:, at:at + n].rearrange("p (h t) -> p h t", h=H)
    return cut(0, f), cut(f, f), cut(2 * f, b), cut(2 * f + b, b)


class Program:
    pass


def prepare_edges(nc, k):
    with ExitStack() as ctx:
        sb = lambda name, shape, dt=F32: ctx.enter_context(nc.sbuf_tensor(name, shape, dt))
        sem = lambda name: ctx.enter_context(nc.semaphore(name))
        src_ps = ctx.enter_context(nc.psum_tensor("p_src_ps", [P, 2, 512], F32))
        rel_ps = ctx.enter_context(nc.psum_tensor("p_rel_ps", [P, 2, 512], F32))
        rows_i = sb("p_rows_i", [P, 2, Q, P], I32)
        rows_f = sb("p_rows_f", [P, 2, Q, P])
        rel = sb("p_rel", [P, Q, P])
        rel_bf = sb("p_rel_bf", [P, Q, P], BF16)
        ends = sb("p_ends", [P, 2, Q])
        ints = sb("p_ints", [P, P + 1], I32)
        first = sb("p_first", [NCH, T + 2])
        last = sb("p_last", [NCH, T + 2])
        go_on = sb("p_go_on", [NCH, T + 1])
        single = sb("p_single", [NCH, T + 1])
        gates = sb("p_gates", [NCH, GATES], BF16)
        blank = sb("p_blank", [1, 2])
        padded, loaded, iotas, chain = sem("p_padded"), sem("p_loaded"), sem("p_iotas"), sem("p_chain")
        rows_ready, rel_ready, turned = sem("p_rows"), sem("p_rel_s"), sem("p_turned")
        ends_ready, stored, ends_in, gates_ready = sem("p_ends_s"), sem("p_stored"), sem("p_ends_in"), sem("p_gates_s")

        with nc.Block() as block:

            @block.sync
            def _(sp):
                for a, name in enumerate((k.dst, k.src)):
                    sp.dma_start(rows_i[:, a, 0:FULLQ, :],
                                 name[0:FULLQ * P * P].rearrange("(q p e) -> p q e", p=P, e=P)).then_inc(loaded, 16)
                sp.wait_ge(padded, 2)
                for a, name in enumerate((k.dst, k.src)):
                    at = FULLQ * P * P
                    if ROWS_LAST:
                        sp.dma_start(rows_i[0:ROWS_LAST, a, FULLQ, :],
                                     name[at:at + ROWS_LAST * P].rearrange("(p e) -> p e", e=P)).then_inc(loaded, 16)
                        at += ROWS_LAST * P
                    if EDGES_LAST:
                        sp.dma_start(rows_i[ROWS_LAST:ROWS_LAST + 1, a, FULLQ, 0:EDGES_LAST],
                                     name[at:EDGES].rearrange("(p e) -> p e", p=1)).then_inc(loaded, 16)
                sp.wait_ge(ends_ready, 1)
                with nc.allow_non_contiguous_dma(reason="one number of each tile"):
                    sp.dma_start(k.first_rows[1:1 + ETP].rearrange("(q p) -> p q", p=P), ends[:, 0]).then_inc(stored, 16)
                    sp.dma_start(k.last_rows[1:1 + ETP].rearrange("(q p) -> p q", p=P), ends[:, 1]).then_inc(stored, 16)
                    sp.dma_start(k.base_rows[0].rearrange("(q p) -> p q", p=P),
                                 rows_i[:, 0, :, 0]).then_inc(stored, 16)
                sp.dma_start(k.first_rows[0:1], blank[0:1, 0:1]).then_inc(stored, 16)
                sp.dma_start(k.last_rows[0:1], blank[0:1, 1:2]).then_inc(stored, 16)
                sp.wait_ge(rel_ready, 2)
                sp.dma_start(k.rel_rows.rearrange("(q p e) -> p q e", p=P, e=P), rel_bf[:, :, :]).then_inc(stored, 16)
                sp.wait_ge(stored, 96)
                for rows, out in ((k.first_rows, first), (k.last_rows, last)):
                    overlapping = bass.AP(tensor=rows.tensor, offset=0, ap=[[T, NCH], [1, T + 2]])
                    sp.dma_start(out[:, :], overlapping).then_inc(ends_in, 16)
                sp.wait_ge(gates_ready, 1)
                sp.dma_start(k.gate_rows, gates[:, :]).then_inc(stored, 16)
                sp.dma_start(k.go_on_rows, go_on[:, 0:T]).then_inc(stored, 16)
                sp.wait_ge(stored, 128)

            @block.gpsimd
            def _(pool):
                nc.gpsimd.iota(ints[:, 0:P], [[1, P]], base=0, channel_multiplier=0).then_inc(iotas, 1)
                nc.gpsimd.iota(ints[:, P:P + 1], [[0, 1]], base=0, channel_multiplier=1).then_inc(iotas, 1)

            @block.vector
            def _(dve):
                link = link_on(dve, chain)
                nc.vector.memset(rows_i[:, 0, FULLQ:Q, :], N).then_inc(padded, 1)
                nc.vector.memset(rows_i[:, 1, FULLQ:Q, :], 0).then_inc(padded, 1)
                nc.vector.memset(blank[:, :], -1.0)
                nc.vector.memset(k.one[:, :], 1.0)
                link(nc.vector.memset(k.head_rows[:, :, :], 0.0))
                for h in range(H):
                    nc.vector.memset(k.head_rows[:, h, h:2 * H:H], 1.0)
                for h in range(2):
                    nc.vector.memset(k.head_rows[:, H + h, h * C:(h + 1) * C], 1.0)
                dve.wait_ge(iotas, 2)
                link(nc.vector.tensor_copy(k.iota_row[:, :], ints[:, 0:P]))
                link(nc.vector.tensor_copy(k.iota_col[:, :], ints[:, P:P + 1]))
                link(nc.vector.tensor_scalar(k.neg_col[:, :], k.iota_col[:, :], -1.0, None, ALU.mult))
                link(nc.vector.tensor_scalar(k.ident[:, :], k.iota_row[:, :], k.iota_col[:, 0:1], None, ALU.is_equal))
                dve.wait_ge(loaded, 32 * (1 + (ROWS_LAST > 0) + (EDGES_LAST > 0)))
                link(nc.vector.tensor_copy(rows_f[:, 0], rows_i[:, 0]))
                nc.vector.tensor_copy(rows_f[:, 1], rows_i[:, 1]).then_inc(rows_ready, 1)
                nc.vector.tensor_copy(ends[:, 0], rows_f[:, 0, :, 0])
                nc.vector.tensor_copy(ends[:, 1], rows_f[:, 0, :, P - 1]).then_inc(ends_ready, 1)
                nc.vector.tensor_tensor(rel[:, :, :], rows_f[:, 0], rows_f[:, 0, :, 0:1].to_broadcast([P, Q, P]),
                                        ALU.subtract).then_inc(rel_ready, 1)
                dve.wait_ge(rel_ready, 1)
                nc.vector.tensor_copy(rel_bf[:, :, :], rel[:, :, :]).then_inc(rel_ready, 1)
                for g in range((Q + 3) // 4):
                    n = min(4, Q - 4 * g)
                    dve.wait_ge(turned, 2 * g + 2)
                    at = slice(4 * g * P, (4 * g + n) * P)
                    nc.vector.tensor_copy(k.src_e[:, at], src_ps[:, g, 0:n * P])
                    nc.vector.tensor_scalar(k.neg_rel[:, at], rel_ps[:, g, 0:n * P], -1.0, None, ALU.mult)
                dve.wait_ge(ends_in, 32)
                j = T + 1
                link(nc.vector.tensor_tensor(go_on[:, :], first[:, 1:j + 1], last[:, 0:j], ALU.is_equal))
                link(nc.vector.tensor_tensor(single[:, :], first[:, 0:j], last[:, 0:j], ALU.is_equal))
                g_in, g_pass, b_in, b_pass = gate_views(gates[:, :])
                link(nc.vector.memset(gates[:, :], -NEG))
                for h in range(H):
                    nc.vector.tensor_scalar(g_in[:, h, 0:T], go_on[:, 0:T], 1.0, NEG, ALU.subtract, ALU.mult)
                    nc.vector.memset(g_in[:, h, T:j], 0.0)
                    nc.vector.tensor_scalar(g_pass[:, h, T:j], single[:, T:j], 1.0, NEG, ALU.subtract, ALU.mult)
                    nc.vector.tensor_scalar(b_in[:, h, 0:T - 1], go_on[:, 1:T], 1.0, NEG, ALU.subtract, ALU.mult)
                link(nc.vector.tensor_tensor(last[:, 0:T], go_on[:, 0:T], single[:, 0:T], ALU.mult))
                for h in range(H):
                    nc.vector.tensor_scalar(g_pass[:, h, 1:T], last[:, 1:T], 1.0, NEG, ALU.subtract, ALU.mult)
                link(nc.vector.tensor_tensor(first[:, 0:T - 1], go_on[:, 1:T], single[:, 2:T + 1], ALU.mult))
                for h in range(H):
                    link(nc.vector.tensor_scalar(b_pass[:, h, 0:T - 1], first[:, 0:T - 1], 1.0, NEG, ALU.subtract,
                                                 ALU.mult))
                nc.vector.memset(blank[:, :], -1.0).then_inc(gates_ready, 1)

            @block.tensor
            def _(pe):
                pe.wait_ge(rows_ready, 1)
                pe.wait_ge(chain, 5)
                pe.wait_ge(rel_ready, 1)
                for g in range((Q + 3) // 4):
                    for out, rows in ((src_ps, rows_f[:, 1]), (rel_ps, rel[:, :, :])):
                        for q in range(4 * g, min(4 * g + 4, Q)):
                            last = nc.tensor.transpose(out[:, g, (q % 4) * P:(q % 4 + 1) * P], rows[:, q, :],
                                                       k.ident[:, :])
                        last.then_inc(turned, 1)


def inverse_root(nc, link, out, var, root):
    link(nc.vector.reciprocal(out, root))
    link(nc.vector.tensor_tensor(root, out, out, ALU.mult))
    link(nc.vector.scalar_tensor_tensor(root, root, -0.5, var, ALU.mult, ALU.mult))
    link(nc.vector.scalar_tensor_tensor(out, root, 1.5, out, ALU.add, ALU.mult))


def norm_scale(nc, link, st, mean, rstd, tmp, eps_sqrt):
    half = D // 2
    link(nc.vector.tensor_tensor(tmp[:, 0, :], st[:, :, 1], st[:, :, 4], ALU.subtract))
    link(nc.vector.tensor_tensor(tmp[:, 0, :], tmp[:, 0, :], tmp[:, 0, :], ALU.mult))
    link(nc.vector.tensor_tensor(tmp[:, 1, :], st[:, :, 2], st[:, :, 5], ALU.add))
    link(nc.vector.tensor_scalar(tmp[:, 0, :], tmp[:, 0, :], 0.25, None, ALU.mult))
    link(nc.vector.scalar_tensor_tensor(tmp[:, 0, :], tmp[:, 1, :], 0.5 / half, tmp[:, 0, :], ALU.mult, ALU.add))
    link(nc.vector.tensor_tensor(mean, st[:, :, 1], st[:, :, 4], ALU.add))
    link(nc.vector.tensor_scalar(mean, mean, 0.5, None, ALU.mult))
    eps_sqrt(tmp[:, 0, :], tmp[:, 1, :])
    inverse_root(nc, link, rstd, tmp[:, 0, :], tmp[:, 1, :])


def project_nodes(nc, k):
    with ExitStack() as ctx:
        sb = lambda name, shape, dt=F32: ctx.enter_context(nc.sbuf_tensor(name, shape, dt))
        pb = lambda name, shape: ctx.enter_context(nc.psum_tensor(name, shape, F32))
        sem = lambda name: ctx.enter_context(nc.semaphore(name))
        x_all = sb("x_all", [P, NTP, D])
        stats = sb("ln_stats", [P, NTP, 6])
        mean = sb("ln_mean", [P, NTP])
        rstd = sb("ln_rstd", [P, NTP])
        tmp = sb("ln_tmp", [P, 2, NTP])
        w_ext = sb("w_ext", [P, 2, 2, XW])
        w_att = sb("w_att", [P, 2, 2, D])
        att_all = sb("att_all", [P, D])
        z_sb = sb("z_sb", [P, 2, D])
        zt_sb = sb("zt_sb", [P, 2, 2, P])
        xl_sb = sb("xl_sb", [P, 2, XW])
        xr_sb = sb("xr_sb", [P, 2, XW])
        f_sb = sb("f_sb", [P, 2, D])
        g_sb = sb("g_sb", [P, 2, D])
        lin = sb("lin", [P, 2, H])
        red = sb("red", [P, 2, H])
        zt_ps = pb("zt_ps", [P, 2, 512])
        xl_ps = pb("xl_ps", [P, 2, 512])
        xr_ps = pb("xr_ps", [P, 2, 512])
        blank, x_in, w_in = sem("n_blank"), sem("n_x_in"), sem("n_w_in")
        stat_done, var_ready, root_ready, chain, w_ready = (sem("n_stat"), sem("n_var"), sem("n_root"), sem("n_chain"),
                                                            sem("n_w_ready"))
        z_ready, zt_done, zt_taken = sem("n_z"), sem("n_zt"), sem("n_zt_taken")
        zt_kept = [sem("n_zt_kept0"), sem("n_zt_kept1")]
        mm_done, xl_ready, xr_ready, xr_full = sem("n_mm"), sem("n_xl"), sem("n_xr"), sem("n_xr_full")
        f_ready, g_ready, red_ready, lin_ready = sem("n_f"), sem("n_g"), sem("n_red"), sem("n_lin")
        stored = [sem("n_stored0"), sem("n_stored1")]

        with nc.Block() as block:

            @block.sync
            def _(sp):
                sp.dma_start(att_all[:, :], k.att.rearrange("h c -> (h c)").partition_broadcast(P)).then_inc(w_in, 16)
                for a, w in enumerate((k.W_l, k.W_r)):
                    sp.dma_start(w_ext[:, a, :, 0:D], w.rearrange("(h p) n -> p h n", p=P)).then_inc(w_in, 16)
                step = NT // 2
                for t in range(0, NT - 1, step):
                    sp.dma_start(x_all[:, t:t + step, :],
                                 k.x[t * P:(t + step) * P, :].rearrange("(t p) d -> p t d", p=P)).then_inc(x_in, 16)
                sp.wait_ge(blank, 1)
                sp.dma_start(x_all[0:NTAIL, NT - 1, :], k.x[(NT - 1) * P:N, :]).then_inc(x_in, 16)

                def store(t, s):
                    sp.wait_ge(xr_full, t + 1)
                    row = t * P
                    sp.dma_start(k.xl_rows[bass.ds(row, P), :], xl_sb[:, s, :]).then_inc(stored[s], 16)
                    sp.dma_start(k.xr_rows[bass.ds(row, P), :], xr_sb[:, s, :]).then_inc(stored[s], 16)

                tiles(sp, NTP, 2, 2, store)
                for s in range(2):
                    sp.wait_ge(stored[s], 16 * NTP)

            @block.gpsimd
            def _(pool):
                nc.gpsimd.memset(k.acc[:, :, :], 0.0)

                def keep(t, s):
                    pool.wait_ge(zt_taken, t + 1)
                    pool.dma_start(k.zt_cols[:, :, bass.ds(t * P, P)], zt_sb[:, s]).then_inc(zt_kept[s], 16)

                tiles(pool, NTP, 2, 2, keep)
                for s in range(2):
                    pool.wait_ge(zt_kept[s], 8 * NTP)

            @block.vector
            def _(dve):
                link = link_on(dve, chain)
                nc.vector.memset(x_all[:, NT - 1:NTP, :], 0.0).then_inc(blank, 1)
                dve.wait_ge(w_in, 48)
                for a in range(2):
                    for h in range(2):
                        link(nc.vector.scalar_tensor_tensor(w_att[:, a, h, :], w_ext[:, a, h, 0:D], SLOPE,
                                                            att_all[:, :], ALU.mult, ALU.mult))
                        nc.vector.memset(w_ext[:, a, h, D + H:XW], 0.0)
                        link(nc.vector.tensor_reduce(w_ext[:, a, h, D:D + H],
                                                     w_att[:, a, h, :].rearrange("p (h c) -> p h c", c=C), AX.X,
                                                     ALU.add))
                nc.vector.tensor_scalar(k.att_pos[:, :], att_all[:, :], 1.0 - SLOPE, None, ALU.mult).then_inc(w_ready, 1)
                dve.wait_ge(x_in, 16 * (2 + 1))
                with dve.Fori(0, NTP // 2) as i:
                    for u in range(2):
                        nc.vector.bn_stats(stats[:, bass.ds(i * 2 + u, 1), :],
                                           x_all[:, bass.ds(i * 2 + u, 1), :]).then_inc(stat_done, 1)
                dve.wait_ge(stat_done, NTP)

                def root(var, out):
                    nc.vector.tensor_scalar(var, var, EPS, None, ALU.add).then_inc(var_ready, 1)
                    dve.wait_ge(root_ready, 1)

                norm_scale(nc, link, stats, mean[:, :], rstd[:, :], tmp, root)

                def normalise(t, s):
                    wait_past(dve, zt_done, t - 1)
                    nc.vector.tensor_scalar(z_sb[:, s, :], x_all[:, bass.ds(t, 1), :], mean[:, bass.ds(t, 1)],
                                            rstd[:, bass.ds(t, 1)], ALU.subtract, ALU.mult).then_inc(z_ready, 1)

                def self_logits(t, s):
                    dve.wait_ge(xr_ready, t + 1)
                    nc.vector.tensor_tensor(f_sb[:, s, :], xr_ps[:, s, 0:D], xl_sb[:, s, 0:D], ALU.add).then_inc(f_ready, 1)
                    nc.vector.tensor_tensor(lin[:, s, :], xr_ps[:, s, D:D + H], xl_sb[:, s, D:D + H],
                                            ALU.add).then_inc(lin_ready, 1)
                    dve.wait_ge(f_ready, t + 1)
                    nc.vector.scalar_tensor_tensor(g_sb[:, s, :], f_sb[:, s, :], 0.0, k.att_pos[:, :], ALU.max,
                                                   ALU.mult).then_inc(g_ready, 1)
                    dve.wait_ge(g_ready, t + 1)
                    nc.vector.tensor_reduce(red[:, s, :], g_sb[:, s, :].rearrange("p (h c) -> p h c", c=C), AX.X,
                                            ALU.add).then_inc(red_ready, 1)
                    dve.wait_ge(red_ready, t + 1)
                    dve.wait_ge(lin_ready, t + 1)
                    if not isinstance(t, int) or t >= 2:
                        dve.wait_ge(stored[s], (t - s) * 16)
                    nc.vector.tensor_tensor(xr_sb[:, s, D + H:XW], red[:, s, :], lin[:, s, :], ALU.add).then_inc(xr_full, 1)

                normalise(0, 0)
                normalise(1, 1)

                def both(t, s):
                    normalise(t + 2, s)
                    self_logits(t, s)

                dve.wait_ge(w_ready, 1)
                tiles(dve, NTP - 2, 2, 2, both)
                for t in range(NTP - 2, NTP):
                    self_logits(t, t % 2)

            @block.scalar
            def _(act):
                act.wait_ge(var_ready, 1)
                nc.scalar.activation(tmp[:, 1, :], tmp[:, 0, :], ACT.Sqrt).then_inc(root_ready, 1)

                def take_zt(t, s):
                    act.wait_ge(zt_done, t + 1)
                    wait_past(act, mm_done, t - 1)
                    if not isinstance(t, int) or t >= 2:
                        act.wait_ge(zt_kept[s], (t - s) * 8)
                    nc.scalar.copy(zt_sb[:, s], zt_ps[:, s, 0:D].rearrange("p (h n) -> p h n", h=2)).then_inc(zt_taken, 1)

                def take_x(t, s):
                    act.wait_ge(mm_done, t + 1)
                    if not isinstance(t, int) or t >= 2:
                        act.wait_ge(stored[s], (t - s) * 16)
                    nc.scalar.copy(xl_sb[:, s, :], xl_ps[:, s, 0:XW]).then_inc(xl_ready, 1)
                    nc.scalar.copy(xr_sb[:, s, 0:D + H], xr_ps[:, s, 0:D + H]).then_inc(xr_ready, 1)

                take_zt(0, 0)

                def both(t, s):
                    take_zt(t + 1, 1 - s)
                    take_x(t, s)

                tiles(act, NTP - 2, 2, 2, both)
                both(NTP - 2, 0)
                take_x(NTP - 1, 1)

            @block.tensor
            def _(pe):
                def turn(t, s):
                    pe.wait_ge(z_ready, t + 1)
                    wait_past(pe, zt_taken, t - 1)
                    for h in range(2):
                        last = nc.tensor.transpose(zt_ps[:, s, h * P:(h + 1) * P], z_sb[:, s, h * P:(h + 1) * P],
                                                   k.ident[:, :])
                    last.then_inc(zt_done, 1)

                def project(t, s):
                    pe.wait_ge(zt_taken, t + 1)
                    wait_past(pe, xr_ready, t - 1)
                    wait_past(pe, lin_ready, t - 1)
                    for a, out in enumerate((xl_ps, xr_ps)):
                        for h in range(2):
                            last = nc.tensor.matmul(out[:, s, 0:XW], zt_sb[:, s, h, :], w_ext[:, a, h, :],
                                                    start=(h == 0), stop=(h == 1))
                    last.then_inc(mm_done, 1)

                pe.wait_ge(w_ready, 1)
                turn(0, 0)

                def both(t, s):
                    turn(t + 1, 1 - s)
                    project(t, s)

                tiles(pe, NTP - 2, 2, 2, both)
                both(NTP - 2, 0)
                project(NTP - 1, 1)


def load_bases(nc, k, engine, at, n):
    return nc.values_load_multi_w_load_instructions(k.bases[:, bass.ds(at, n)], engines=[engine], min_val=0, max_val=N)[1]


def attend(nc, k):
    QT = 4
    QUADS = T // QT
    PAIRS = T // 2
    LAG = 4
    LEAD = QUADS - LAG
    AHEAD = 6
    SOFT = 22
    EX = 2 * P
    assert NCH % 2 == 0
    with ExitStack() as ctx:
        sb = lambda name, shape, dt=F32: ctx.enter_context(nc.sbuf_tensor(name, shape, dt))
        pb = lambda name, shape: ctx.enter_context(nc.psum_tensor(name, shape, F32))
        sem = lambda name: ctx.enter_context(nc.semaphore(name))
        idx = sb("a_idx", [P, QUADS, QT], I32)
        xl_e = sb("a_xl_e", [P, 2 * T, XW])
        xr_w = sb("a_xr_w", [P, 2, QT, XW])
        rel_bc = sb("a_rel_bc", [P, 2, QT, P], BF16)
        far = sb("a_far", [P, QT, P])
        hot_n = sb("a_hot_n", [P, 2, QT, P])
        hot_e = sb("a_hot_e", [P, 2, QT, P])
        pos = sb("a_pos", [P, 2, D])
        red = sb("a_red", [P, 2, 2 * H])
        lg = sb("a_lg", [P, 2, 2, H, T])
        msg = sb("a_msg", [P, QT, D])
        exs = sb("a_exs", [P, 2, T, 2 * H])
        rel_r = sb("a_rel_r", [P, NCH, P], BF16)
        fresh = sb("a_fresh", [P, NCH])
        cut = sb("a_cut", [P, P + 1], BF16)
        lgr = sb("a_lgr", [P, 2, P])
        run = sb("a_run", [P, P])
        top = sb("a_top", [P, P])
        peak = sb("a_peak", [P, P])
        side = sb("a_side", [P, 2, P])
        begin = run
        expo = sb("a_expo", [P, 2, P])
        gate = sb("a_gate", [1, 2, GATES], BF16)
        carry = sb("a_carry", [1, H])
        into = sb("a_into", [1, H, T + 1])
        reach = sb("a_reach", [1, H, T + 1])
        reach_t = sb("a_reach_t", [1, H, T])
        back = sb("a_back", [1, H, T])
        reach_b = sb("a_reach_b", [1, H, T])
        fade = sb("a_fade", [1, H])
        faded = sb("a_faded", [1, H])
        f_ps = pb("a_f_ps", [P, 2, 2, 512])
        o_ps = pb("a_o_ps", [P, 2, 512])
        sm_ps = pb("a_sm_ps", [P, 2, 512])

        fixed, bases_in, masks, may_gather = sem("a_fixed"), sem("a_bases_in"), sem("a_masks"), sem("a_may_gather")
        idx_ready, far_n, hot_n_ready, far_e, hot_e_ready = (sem("a_idx_s"), sem("a_far_n"), sem("a_hot_n_s"),
                                                             sem("a_far_e"), sem("a_hot_e_s"))
        xl_in = [sem(f"a_xl_in{q}") for q in range(2 * QUADS)]
        xr_in = [sem(f"a_xr_in{q}") for q in range(2)]
        rel_in = [sem(f"a_rel_in{q}") for q in range(2)]
        gate_in = [sem(f"a_gate_in{q}") for q in range(2)]
        f_done, pos_ready, red_ready, lg_ready = sem("a_f_s"), sem("a_pos_s"), sem("a_red_s"), sem("a_lg_s")
        rows_done, rows_taken, soft, ends_done = sem("a_rows"), sem("a_rows_taken"), sem("a_soft"), sem("a_ends")
        reach_done, peak_done, expo_ready, faded_ready = sem("a_reach_c"), sem("a_peak_s"), sem("a_expo_s"), sem("a_faded_s")
        turned, exs_ready, msg_ready, sum_done, added = (sem("a_turned"), sem("a_exs_s"), sem("a_msg_s"), sem("a_sum_s"),
                                                         sem("a_added"))

        def steps(engine, step):
            late = [(2, QUADS - LAG + j) for j in range(LAG)]
            soon = [(1, j) for j in range(QUADS - LAG)]
            step(0, 0, True, [None] * QUADS)
            step(1, 1, True, [None] * LAG + soon)
            with engine.Fori(0, NCH // 2 - 2) as r:
                step(r * 2 + 2, 0, True, late + soon)
                step(r * 2 + 3, 1, True, late + soon)
            step(NCH - 2, 0, True, late + soon)
            step(NCH - 1, 1, True, late + soon)
            step(NCH, 0, False, late + soon)
            step(NCH + 1, 1, False, late)

        def softmax_in(c):
            return not isinstance(c, int) or 1 <= c <= NCH

        with nc.Block() as block:

            @block.gpsimd
            def _(pool):
                def gather(c, p, j):
                    pool.wait_ge(idx_ready, c * QUADS + (j + 1))
                    pool.sem_inc(may_gather, 1)
                    for u in range(QT):
                        nc.gpsimd.indirect_dma_start(
                            xl_e[:, p * T + j * QT + u, :], None, k.xl_rows,
                            bass.IndirectOffsetOnAxis(ap=idx[:, j, u:u + 1], axis=0)
                        ).then_inc(xl_in[p * QUADS + j], 16)

                def messages(cc, pp, jj):
                    pool.wait_ge(exs_ready, cc + 1)
                    for g in range(2):
                        t = jj * QT + 2 * g
                        wait_past(pool, sum_done, cc * T + (t - 2))
                        nc.gpsimd.tensor_tensor(
                            msg[:, 2 * g:2 * g + 2, :].rearrange("p t (h c) -> p t h c", c=C),
                            xl_e[:, pp * T + t:pp * T + t + 2, 0:D].rearrange("p t (h c) -> p t h c", c=C),
                            exs[:, pp, t:t + 2, 0:H][:, :, :, None].to_broadcast([P, 2, H, C]),
                            ALU.mult).then_inc(msg_ready, 1)

                def step(c, p, logits, sums):
                    for j in range(QUADS):
                        if sums[j:j + 1] and sums[j]:
                            b, jj = sums[j]
                            messages(c - b, (p + b) % 2, jj)
                        more = j + LEAD >= QUADS
                        at = c + more
                        if logits and not (isinstance(at, int) and at >= NCH):
                            wait_past(pool, msg_ready, c * PAIRS + (2 * (j + LEAD + 1) - 2 * PAIRS))
                            gather(at, (p + more) % 2, (j + LEAD) % QUADS)

                for j in range(LEAD):
                    gather(0, 0, j)
                steps(pool, step)

            @block.sync
            def _(sp):
                with nc.allow_non_contiguous_dma(reason="one number of each tile"):
                    sp.dma_start(k.bases[:, :], k.base_rows[:, 0:ETL]).then_inc(bases_in, 16)
                    for h in range(H):
                        sp.dma_start(rel_r[h * T:(h + 1) * T], k.rel_rows[0:ETL * P].rearrange(
                            "(c t e) -> t c e", t=T, e=P)).then_inc(fixed, 16)
                        sp.dma_start(fresh[h * T:(h + 1) * T], k.go_on_rows.rearrange("c t -> t c")).then_inc(fixed, 16)

                def loads(c, p):
                    if not isinstance(c, int) or c >= 2:
                        sp.wait_ge(soft, (c - 1) * SOFT)
                    sp.dma_start(gate[:, p], k.gate_rows[bass.ds(c, 1), :]).then_inc(gate_in[p], 16)
                    for j in range(QUADS):
                        at = c * T + j * QT
                        if j % 2 == 0:
                            bases = load_bases(nc, k, mybir.EngineType.SP, at, 2 * QT)
                        wait_past(sp, far_n, c * QUADS + (j - 1))
                        sp.dma_start(rel_bc[:, j % 2].rearrange("p t e -> p (t e)"),
                                     k.rel_rows[bass.ds(at * P, QT * P)].partition_broadcast(P)).then_inc(rel_in[j % 2], 16)
                        wait_past(sp, f_done, c * PAIRS + (2 * (j - 1)))
                        for u in range(QT):
                            sp.dma_start(xr_w[:, j % 2, u, :], k.xr_rows[bass.ds(bases[j % 2 * QT + u], P), :]).then_inc(xr_in[j % 2], 16)

                sp.wait_ge(bases_in, 16)
                loads(0, 0)
                loads(1, 1)
                with sp.Fori(0, NCH // 2 - 1) as r:
                    loads(r * 2 + 2, 0)
                    loads(r * 2 + 3, 1)

            @block.scalar
            def _(act):
                def indices(q, slot):
                    nc.scalar.copy(idx[:, slot, :], k.src_e[:, bass.ds(q * QT, QT)]).then_inc(idx_ready, 1)

                for q in range(AHEAD):
                    indices(q, q)

                def hot_nodes(c, j):
                    quad = c * QUADS + j
                    act.wait_ge(rel_in[j % 2], c * (8 * QUADS) + (j // 2 + 1) * 16)
                    nc.scalar.activation(far[:, :, :], rel_bc[:, j % 2], ACT.Abs, bias=k.neg_col[:, 0:1]).then_inc(far_n, 1)
                    act.wait_ge(far_n, quad + 1)
                    wait_past(act, f_done, c * PAIRS + 2 * (j - 1))
                    nc.scalar.activation(hot_n[:, j % 2], far[:, :, :], ACT.Relu, scale=-1.0,
                                         bias=k.one[:, 0:1]).then_inc(hot_n_ready, 1)
                    act.wait_ge(hot_n_ready, quad + 1)

                def hot_edges(c, j):
                    for u in range(QT):
                        nc.scalar.activation(far[:, u, :], k.iota_row[:, :], ACT.Abs,
                                             bias=k.neg_rel[:, bass.ds(c * T + (j * QT + u), 1)]).then_inc(far_e, 1)
                    act.wait_ge(far_e, c * T + (j + 1) * QT)
                    wait_past(act, sum_done, c * T + (j - 1) * QT)
                    nc.scalar.activation(hot_e[:, j % 2], far[:, :, :], ACT.Relu, scale=-1.0,
                                         bias=k.one[:, 0:1]).then_inc(hot_e_ready, 1)
                    act.wait_ge(hot_e_ready, c * QUADS + (j + 1))

                def step(c, p, logits, sums):
                    for j in range(QUADS):
                        quad = c * QUADS + j
                        if logits:
                            if not isinstance(c, int) or c * QUADS + j >= 2:
                                cc, pp, jj = (c, p, j - 2) if j >= 2 else (c - 1, 1 - p, j - 2 + QUADS)
                                act.wait_ge(xl_in[pp * QUADS + jj], (cc - pp) * (8 * QT) + 16 * QT)
                            indices(quad + AHEAD, (j + AHEAD) % QUADS)
                        following = c + (j + 1 == QUADS)
                        if logits and not (isinstance(following, int) and following >= NCH):
                            hot_nodes(following, (j + 1) % QUADS)
                        back = following - (2 if (j + 1) % QUADS < LAG else 1)
                        if not isinstance(back, int) or 0 <= back < NCH:
                            hot_edges(back, (j + 1 - LAG) % QUADS)
                        if not softmax_in(c):
                            continue
                        if j == 0:
                            act.wait_ge(rows_done, c)
                            nc.scalar.copy(lgr[:, :, :], sm_ps[:, 1 - p, 0:EX].rearrange("p (a e) -> p a e", a=2)
                                           ).then_inc(rows_taken, 1)
                        if j == 2:
                            act.wait_ge(soft, (c - 1) * SOFT + 19)
                            nc.scalar.activation(expo[:, :, :], lgr[:, :, :], ACT.Exp).then_inc(expo_ready, 1)
                        if j == 3:
                            act.wait_ge(soft, (c - 1) * SOFT + 20)
                            nc.scalar.activation(faded[:, :], fade[:, :], ACT.Exp).then_inc(faded_ready, 1)
                            act.wait_ge(turned, c)
                            wait_past(act, sum_done, (c - 2) * T + 1)
                            nc.scalar.copy(exs[:, 1 - p].rearrange("p t k -> p k t"),
                                           sm_ps[:, 1 - p, EX:EX + 2 * P].rearrange("p (k t) -> p k t", t=T)
                                           ).then_inc(exs_ready, 1)

                hot_nodes(0, 0)
                steps(act, step)

            @block.vector
            def _(dve):
                dve.wait_ge(fixed, 32 * H)
                nc.vector.memset(cut[:, 0:1], -NEG)
                nc.vector.memset(cut[:, P:P + 1], -NEG)
                nc.vector.memset(red[:, :, :], 0.0)
                nc.vector.memset(carry[:, :], -NEG)
                nc.vector.memset(back[:, :, :], -NEG)
                nc.vector.memset(o_ps[:, :, :], 0.0)
                nc.vector.tensor_scalar(fresh[:, :], fresh[:, :], -1.0, 1.0, ALU.mult, ALU.add).then_inc(masks, 1)
                dve.wait_ge(masks, 1)

                att = k.att_pos[:, None, :].to_broadcast([P, 2, D])

                def logits_of(c, p, j, g, between):
                    n = c * PAIRS + (2 * j + g + 1)
                    at = slice(j * QT + 2 * g, j * QT + 2 * g + 2)
                    dve.wait_ge(f_done, n)
                    nc.vector.scalar_tensor_tensor(pos[:, :, :], f_ps[:, g, :, 0:D], 0.0, att, ALU.max,
                                                   ALU.mult).then_inc(pos_ready, 1)
                    between(0)
                    dve.wait_ge(pos_ready, n)
                    nc.vector.tensor_reduce(red[:, :, 0:H], pos[:, :, :].rearrange("p t (h c) -> p t h c", c=C), AX.X,
                                            ALU.add).then_inc(red_ready, 1)
                    between(1)
                    dve.wait_ge(red_ready, n)
                    nc.vector.tensor_tensor(lg[:, p, :, :, at].rearrange("p a h t -> p t (a h)"), red[:, :, :],
                                            f_ps[:, g, :, D:XW], ALU.add).then_inc(lg_ready, 1)

                def add_up(cc, jj, u, base):
                    n = cc * T + (jj * QT + u)
                    dve.wait_ge(sum_done, n + 1)
                    if jj == 0 and u == 0:
                        dve.wait_ge(soft, (cc + 1) * SOFT)
                    wait_past(dve, added, n)
                    window = k.acc[:, :, bass.ds(base, P)]
                    nc.vector.tensor_tensor(window, o_ps[:, u % 2, 0:3 * P].rearrange("p (b n) -> p b n", b=3), window,
                                            ALU.add).then_inc(added, 1)

                def softmax(cc, pp, part, node=None):
                    did = cc * SOFT

                    def done(i, ins):
                        ins.then_inc(soft, 1)

                    def after(i):
                        wait_past(dve, soft, did + i)

                    g_in, g_pass, b_in, b_pass = gate_views(gate[:, pp])
                    rel = rel_r[:, bass.ds(cc, 1), :].rearrange("p o e -> p (o e)")
                    if part == 0:
                        done(1, nc.vector.tensor_tensor(cut[:, 1:P], rel[:, 1:P], rel[:, 0:P - 1], ALU.not_equal))
                        after(1)
                        done(2, nc.vector.tensor_scalar(cut[:, 1:P], cut[:, 1:P], -NEG, None, ALU.mult))
                        done(3, nc.vector.tensor_scalar(side[:, 0], rel, rel[:, 0:1], -NEG, ALU.not_equal, ALU.mult))
                        done(4, nc.vector.tensor_scalar(side[:, 1], rel, rel[:, P - 1:P], -NEG, ALU.not_equal, ALU.mult))
                        dve.wait_ge(rows_taken, cc + 1)
                        done(5, nc.vector.tensor_tensor(peak[:, :], lgr[:, 0], lgr[:, 1], ALU.max))
                        after(5)
                        done(6, nc.vector.tensor_tensor_scan(run[:, :], cut[:, 0:P], peak[:, :], -NEG, ALU.add, ALU.max))
                        after(6)
                        done(7, nc.vector.tensor_tensor_scan(top[:, ::-1], cut[:, P:0:-1], run[:, ::-1], -NEG, ALU.add,
                                                             ALU.max))
                        after(7)
                        done(8, nc.vector.tensor_scalar(begin[:, :], cut[:, 0:P], -1.0 / NEG, None, ALU.mult))
                        after(8)
                        done(9, nc.vector.tensor_copy(begin[:, 0:1], fresh[:, bass.ds(cc, 1)]))
                    if part == 1:
                        dve.wait_ge(ends_done, cc + 1)
                        dve.wait_ge(gate_in[pp], (cc - pp) * 8 + 16)
                        ends = sm_ps[0:1, pp, 0:EX].rearrange("p (a h t) -> p a h t", a=2, t=T)
                        done(10, nc.vector.tensor_tensor(into[:, :, 1:T + 1], ends[:, 1], g_in[:, :, 1:T + 1], ALU.add))
                        after(10)
                        done(11, nc.vector.tensor_tensor(into[:, :, 0], carry[:, :], g_in[:, :, 0], ALU.add))
                        done(12, nc.vector.tensor_tensor(back[:, :, 0:T - 1], ends[:, 0, :, 1:T], b_in[:, :, 0:T - 1],
                                                         ALU.add))
                        after(12)
                        flat = lambda a: a.rearrange("p h t -> p (h t)")
                        done(13, nc.vector.tensor_tensor_scan(flat(reach[:, :, :]), flat(g_pass), flat(into[:, :, :]),
                                                              -NEG, ALU.add, ALU.max))
                        done(14, nc.vector.tensor_tensor_scan(flat(reach_b[:, :, :])[:, ::-1], flat(b_pass)[:, ::-1],
                                                              flat(back[:, :, :])[:, ::-1], -NEG, ALU.add, ALU.max))
                        after(14)
                        done(15, nc.vector.tensor_copy(reach_t[:, :, :], reach[:, :, 0:T]))
                        done(16, nc.vector.tensor_copy(carry[:, :], reach[:, :, T]))
                    if part == 2:
                        dve.wait_ge(reach_done, cc + 1)
                        done(17, nc.vector.scalar_tensor_tensor(peak[:, :], side[:, 0], sm_ps[:, pp, 0:1], top[:, :],
                                                                ALU.add, ALU.max))
                        after(17)
                        done(18, nc.vector.scalar_tensor_tensor(peak[:, :], side[:, 1], sm_ps[:, pp, 1:2], peak[:, :],
                                                                ALU.add, ALU.max))
                        after(18)
                        done(19, nc.vector.tensor_tensor(lgr[:, :, :], lgr[:, :, :],
                                                         peak[:, None, :].to_broadcast([P, 2, P]), ALU.subtract))
                    if part == 3:
                        dve.wait_ge(peak_done, cc + 1)
                        first = sm_ps[0:1, pp, P:2 * P].rearrange("p (h t) -> p h t", t=T)[:, :, 0]
                        done(20, nc.vector.tensor_tensor(fade[:, :], into[:, :, 0], first, ALU.subtract))
                        dve.wait_ge(expo_ready, cc + 1)
                        done(21, nc.vector.tensor_tensor(expo[:, 1], expo[:, 1], begin[:, :], ALU.mult))
                    if part == 4:
                        dve.wait_ge(exs_ready, cc + 1)
                        wait_past(dve, added, cc * T)
                        column = k.acc[:, :, bass.ds(node, 1)]
                        done(22, nc.vector.tensor_tensor(column, column, sm_ps[:, pp, 2:5][:, :, None], ALU.mult))

                def step(c, p, logits, sums):
                    def soften(parts, j):
                        if softmax_in(c) and j in parts:
                            softmax(c - 1, 1 - p, parts[j])

                    for j in range(QUADS):
                        b, jj = sums[j] if sums[j:j + 1] and sums[j] else (0, 0)
                        if b:
                            bases = load_bases(nc, k, mybir.EngineType.DVE, (c - b) * T + jj * QT, QT)
                        if j == LAG and softmax_in(c):
                            softmax(c - 1, 1 - p, 4, bases[0])
                        soften({1: 0, 2: 1, 3: 3}, j)
                        for g in range(2):
                            def between(u):
                                if b:
                                    add_up(c - b, jj, 2 * g + u, bases[2 * g + u])

                            if logits:
                                logits_of(c, p, j, g, between)
                            else:
                                between(0)
                                between(1)
                            if g == 0:
                                soften({2: 2}, j)

                steps(dve, step)

            @block.tensor
            def _(pe):
                def logits_of(c, p, j, g):
                    if g == 0:
                        pe.wait_ge(hot_n_ready, c * QUADS + (j + 1))
                        pe.wait_ge(xr_in[j % 2], c * (QUADS * 8 * QT) + (j // 2 + 1) * (16 * QT))
                        pe.wait_ge(xl_in[p * QUADS + j], (c - p) * (8 * QT) + 16 * QT)
                    wait_past(pe, lg_ready, c * PAIRS + (2 * j + g - 1))
                    for u in range(2 * g, 2 * g + 2):
                        out = f_ps[:, g, u % 2, 0:XW]
                        nc.tensor.matmul(out, hot_n[:, j % 2, u, :], xr_w[:, j % 2, u, :], start=True, stop=False)
                        last = nc.tensor.matmul(out, k.ident[:, :], xl_e[:, p * T + j * QT + u, :], start=False, stop=True)
                    last.then_inc(f_done, 1)

                def sums_of(cc, pp, jj, g):
                    if g == 0:
                        pe.wait_ge(hot_e_ready, cc * QUADS + (jj + 1))
                    pe.wait_ge(msg_ready, cc * PAIRS + (2 * jj + g + 1))
                    for u in range(2 * g, 2 * g + 2):
                        t = jj * QT + u
                        wait_past(pe, added, cc * T + (t - 1))
                        one_hot = hot_e[:, jj % 2, u, :]
                        for h in range(2):
                            nc.tensor.matmul(o_ps[:, u % 2, h * P:(h + 1) * P], msg[:, u, h * P:(h + 1) * P], one_hot,
                                             start=True, stop=True)
                        nc.tensor.matmul(o_ps[0:2 * H, u % 2, 2 * P:3 * P], exs[:, pp, t, :], one_hot,
                                         start=True, stop=True).then_inc(sum_done, 1)

                def softmax(cc, pp, part):
                    did = cc * SOFT
                    sm = sm_ps[:, pp]
                    if part == 0:
                        pe.wait_ge(lg_ready, (cc + 1) * PAIRS)
                        for a in range(2):
                            last = nc.tensor.transpose(sm[:, a * P:(a + 1) * P], lg[:, pp, a].rearrange("p h t -> p (h t)"),
                                                       k.ident[:, :])
                        last.then_inc(rows_done, 1)
                    if part == 1:
                        pe.wait_ge(soft, did + 7)
                        nc.tensor.transpose(sm[0:1, 0:P], top[:, 0:1], k.ident[:, :])
                        nc.tensor.transpose(sm[0:1, P:2 * P], top[:, P - 1:P], k.ident[:, :]).then_inc(ends_done, 1)
                    if part == 2:
                        pe.wait_ge(soft, did + 15)
                        nc.tensor.matmul(sm[:, 0:1], reach_t[:, :, :].rearrange("p h t -> p (h t)"), k.one[0:1, 0:1], start=True, stop=True)
                        nc.tensor.matmul(sm[:, 1:2], reach_b[:, :, :].rearrange("p h t -> p (h t)"), k.one[0:1, 0:1], start=True,
                                         stop=True).then_inc(reach_done, 1)
                    if part == 3:
                        pe.wait_ge(soft, did + 18)
                        nc.tensor.transpose(sm[0:1, P:2 * P], peak[:, 0:1], k.ident[:, :]).then_inc(peak_done, 1)
                    if part == 4:
                        pe.wait_ge(soft, did + 21)
                        for a in range(2):
                            nc.tensor.transpose(sm[:, EX + a * P:EX + (a + 1) * P], expo[:, a], k.ident[:, :])
                        pe.wait_ge(faded_ready, cc + 1)
                        for b, heads in enumerate(((0, 1), (2, 3), range(H))):
                            for h in heads:
                                last = nc.tensor.matmul(sm[:, 2 + b:3 + b], k.head_rows[:, h if b == 2 else H + h % 2, :],
                                                        faded[0:1, h:h + 1], start=(h == heads[0]), stop=(h == heads[-1]))
                        last.then_inc(turned, 1)

                def step(c, p, logits, sums):
                    def soften(parts, j):
                        if softmax_in(c) and j in parts:
                            softmax(c - 1, 1 - p, parts[j])

                    for j in range(QUADS):
                        b, jj = sums[j] if sums[j:j + 1] and sums[j] else (0, 0)
                        for g in range(2):
                            if logits:
                                logits_of(c, p, j, g)
                            soften(({2: 2}, {0: 0, 1: 1, 2: 3, 3: 4})[g], j)
                            if b:
                                sums_of(c - b, (p + b) % 2, jj, g)

                pe.wait_ge(masks, 1)
                steps(pe, step)


def batch_scale(nc, link, stats, par, scale, tmp, eps_sqrt):
    for h in range(DH):
        link(nc.vector.bn_aggr(tmp[:, h, 0:2], stats[:, h]))
    link(nc.vector.tensor_copy(tmp[:, :, 2], tmp[:, :, 1]))
    eps_sqrt(tmp[:, :, 2], tmp[:, :, 3])
    inverse_root(nc, link, tmp[:, :, 1], tmp[:, :, 2], tmp[:, :, 3])
    link(nc.vector.tensor_tensor(scale[:, 0], par[:, 0], tmp[:, :, 1], ALU.mult))
    link(nc.vector.tensor_tensor(tmp[:, :, 0], tmp[:, :, 0], scale[:, 0], ALU.mult))
    link(nc.vector.tensor_tensor(scale[:, 1], par[:, 1], tmp[:, :, 0], ALU.subtract))


def join_heads(nc, k):
    with ExitStack() as ctx:
        sb = lambda name, shape, dt=F32: ctx.enter_context(nc.sbuf_tensor(name, shape, dt))
        pb = lambda name, shape: ctx.enter_context(nc.psum_tensor(name, shape, F32))
        sem = lambda name: ctx.enter_context(nc.semaphore(name))
        head_of = sb("j_head_of", [2 * H, DH, P])
        pick = sb("j_pick", [2 * H, 2, DH, P])
        tiny = sb("j_tiny", [P, 1])
        par = sb("j_par", [P, 2, DH])
        bias = sb("j_bias", [P, DH])
        xl = sb("j_xl", [R, 2, 2, D])
        zt = sb("j_zt", [P, 2, DH, W])
        own = sb("j_own", [P, 2, DH, W])
        den = sb("j_den", [P, 2, DH, W])
        stats = sb("j_stats", [P, DH, CHUNKS, 6])
        tmp = sb("j_tmp", [P, DH, 4])
        den_ps = pb("j_den_ps", [P, 2, 2, 256])
        own_ps = pb("j_own_ps", [P, 2, 2, 256])
        xl_ps = pb("j_xl_ps", [P, 2, 2, 256])
        par_in, picked, chain, var_ready, root_ready = sem("j_par_in"), sem("j_picked"), sem("j_chain"), sem("j_var"), sem("j_root")
        xl_in = [sem("j_xl_in0"), sem("j_xl_in1")]
        zt_in = [sem("j_zt_in0"), sem("j_zt_in1")]
        spread, taken, did = sem("j_spread"), sem("j_taken"), sem("j_did")
        STEPS = 8
        XL_READ = 2

        with nc.Block() as block:

            @block.sync
            def _(sp):
                with nc.allow_non_contiguous_dma(reason="one number of each feature"):
                    for i, v in enumerate((k.gamma1, k.beta1)):
                        sp.dma_start(par[:, i], v.rearrange("(h p) -> p h", p=P)).then_inc(par_in, 16)
                    sp.dma_start(bias[:, :], k.bias.rearrange("(h p) -> p h", p=P)).then_inc(par_in, 16)

                def load(c, s):
                    wait_past(sp, did, (c - 1) * STEPS)
                    sp.dma_start(xl[:, s], k.xl_rows[bass.ds(c * W, W), 0:D].rearrange("(u p) d -> p u d", p=R)
                                 ).then_inc(xl_in[s], 16)
                    sp.dma_start(zt[:, s], k.zt_cols[:, :, bass.ds(c * W, W)]).then_inc(zt_in[s], 16)

                tiles(sp, CHUNKS, 2, 2, load)

            @block.vector
            def _(dve):
                link = link_on(dve, chain)
                nc.vector.memset(tiny[:, :], SEG_EPS)
                for h in range(DH):
                    for q in range(2):
                        link(nc.vector.memset(head_of[:, h, q * C:(q + 1) * C], float(2 * h + q)))
                link(nc.vector.tensor_scalar(pick[:, 0], head_of[:, :, :], k.iota_col[0:2 * H, 0:1], None, ALU.is_equal))
                link(nc.vector.tensor_scalar(pick[:, 1], head_of[:, :, :], float(H), k.iota_col[0:2 * H, 0:1], ALU.add,
                                             ALU.is_equal))
                nc.vector.tensor_tensor(pick[:, 0], pick[:, 0], pick[:, 1], ALU.add).then_inc(picked, 1)
                dve.wait_ge(par_in, 48)

                def join(c, s):
                    def step(i, ins):
                        ins.then_inc(did, 1)
                        dve.wait_ge(did, c * STEPS + i)

                    acc = k.acc[:, 0:DH, bass.ds(c * W, W)]
                    dve.wait_ge(taken, c + 1)
                    step(1, nc.vector.reciprocal(den[:, s], den[:, s]))
                    step(2, nc.vector.tensor_tensor(own[:, s], xl_ps[:, s, :, 0:W], own[:, s], ALU.mult))
                    step(3, nc.vector.tensor_tensor(own[:, s], own[:, s], acc, ALU.add))
                    step(4, nc.vector.tensor_tensor(own[:, s], own[:, s], den[:, s], ALU.mult))
                    dve.wait_ge(zt_in[s], (c - s) * 8 + 16)
                    for h in range(DH):
                        step(5 + h, nc.vector.scalar_tensor_tensor(k.acc[:, h, bass.ds(c * W, W)], own[:, s, h], bias[:, h:h + 1],
                                                                   zt[:, s, h], ALU.add, ALU.add))
                    for h in range(DH):
                        step(7 + h, nc.vector.bn_stats(stats[:, h, bass.ds(c, 1), :], k.acc[:, h, bass.ds(c * W, W)]))

                tiles(dve, CHUNKS, 2, 2, join)

                def root(var, out):
                    nc.vector.tensor_scalar(var, var, EPS, None, ALU.add).then_inc(var_ready, 1)
                    dve.wait_ge(root_ready, 1)

                batch_scale(nc, link, stats, par, k.norm1, tmp, root)

            @block.scalar
            def _(act):
                def take(c, s):
                    act.wait_ge(spread, c + 1)
                    wait_past(act, did, (c - 2) * STEPS + 6)
                    nc.scalar.copy(own[:, s], own_ps[:, s, :, 0:W])
                    nc.scalar.activation(den[:, s], den_ps[:, s, :, 0:W], ACT.Identity, bias=tiny[:, 0:1]).then_inc(taken, 1)

                act.wait_ge(picked, 1)
                tiles(act, CHUNKS, 2, 2, take)
                act.wait_ge(var_ready, 1)
                nc.scalar.activation(tmp[:, :, 3], tmp[:, :, 2], ACT.Sqrt).then_inc(root_ready, 1)

            @block.tensor
            def _(pe):
                def spread_heads(c, s):
                    wait_past(pe, taken, c - 1)
                    wait_past(pe, did, (c - 2) * STEPS + XL_READ)
                    for h in range(DH):
                        for out, i in ((den_ps, 0), (own_ps, 1)):
                            nc.tensor.matmul(out[:, s, h, 0:W], pick[:, i, h, :], k.acc[0:2 * H, DH, bass.ds(c * W, W)],
                                             start=True, stop=True)
                    pe.wait_ge(xl_in[s], (c - s) * 8 + 16)
                    for h in range(DH):
                        for u in range(2):
                            last = nc.tensor.transpose(xl_ps[:, s, h, u * R:(u + 1) * R], xl[:, s, u, h * P:(h + 1) * P],
                                                       k.ident[0:R, 0:R])
                    last.then_inc(spread, 1)

                pe.wait_ge(picked, 1)
                tiles(pe, CHUNKS, 2, 2, spread_heads)


def feed_forward(nc, k):
    with ExitStack() as ctx:
        sb = lambda name, shape, dt=F32: ctx.enter_context(nc.sbuf_tensor(name, shape, dt))
        pb = lambda name, shape: ctx.enter_context(nc.psum_tensor(name, shape, F32))
        sem = lambda name: ctx.enter_context(nc.semaphore(name))
        w1 = sb("f_w1", [P, DH, D])
        w2 = sb("f_w2", [P, DH, D])
        b1 = sb("f_b1", [P, DH])
        b2 = sb("f_b2", [P, DH])
        par = sb("f_par", [P, 2, DH])
        hid = sb("f_hid", [P, 2, DH, W])
        stats = sb("f_stats", [P, DH, CHUNKS, 6])
        tmp = sb("f_tmp", [P, DH, 4])
        up_ps = pb("f_up_ps", [P, 2, 2, 256])
        down_ps = pb("f_down_ps", [P, 2, 2, 256])
        w_in, chain, var_ready, root_ready = sem("f_w_in"), sem("f_chain"), sem("f_var"), sem("f_root")
        normed, up_done, hid_ready, down_done, summed, measured = (sem("f_normed"), sem("f_up"), sem("f_hid_s"), sem("f_down"),
                                                                   sem("f_summed"), sem("f_measured"))

        with nc.Block() as block:

            @block.sync
            def _(sp):
                for w, v in ((w1, k.W1), (w2, k.W2)):
                    sp.dma_start(w[:, :, :], v.rearrange("(h p) n -> p h n", p=P)).then_inc(w_in, 16)
                with nc.allow_non_contiguous_dma(reason="one number of each feature"):
                    for out, v in ((b1[:, :], k.b1), (b2[:, :], k.b2), (par[:, 0], k.gamma2), (par[:, 1], k.beta2)):
                        sp.dma_start(out, v.rearrange("(h p) -> p h", p=P)).then_inc(w_in, 16)
                for e in range(E):
                    sp.dma_start(k.we1[:, e], k.We1[e].rearrange("(h p) n -> p h n", p=P)).then_inc(k.experts_in, 16)
                    sp.dma_start(k.we2[:, e], k.We2[e].rearrange("(h p) n -> p h n", p=P)).then_inc(k.experts_in, 16)

            @block.vector
            def _(dve):
                link = link_on(dve, chain)
                dve.wait_ge(w_in, 96)

                def add(c, s):
                    dve.wait_ge(down_done, c + 1)
                    dve.wait_ge(normed, 2 * c + 2)
                    for h in range(DH):
                        at = k.acc[:, h, bass.ds(c * W, W)]
                        nc.vector.scalar_tensor_tensor(at, down_ps[:, s, h, 0:W], b2[:, h:h + 1], at, ALU.add,
                                                       ALU.add).then_inc(summed, 1)
                    for h in range(DH):
                        dve.wait_ge(summed, 2 * c + (h + 1))
                        nc.vector.bn_stats(stats[:, h, bass.ds(c, 1), :],
                                           k.acc[:, h, bass.ds(c * W, W)]).then_inc(measured, 1)

                tiles(dve, CHUNKS, 2, 2, add)
                dve.wait_ge(measured, 2 * CHUNKS)

                def root(var, out):
                    nc.vector.tensor_scalar(var, var, EPS, None, ALU.add).then_inc(var_ready, 1)
                    dve.wait_ge(root_ready, 1)

                batch_scale(nc, link, stats, par, k.norm2, tmp, root)

            @block.scalar
            def _(act):
                act.wait_ge(w_in, 96)

                def norm(c, s):
                    for h in range(DH):
                        at = k.acc[:, h, bass.ds(c * W, W)]
                        nc.scalar.activation(at, at, ACT.Identity, scale=k.norm1[:, 0, h:h + 1],
                                             bias=k.norm1[:, 1, h:h + 1]).then_inc(normed, 1)

                def act_up(c, s):
                    act.wait_ge(up_done, c + 1)
                    wait_past(act, down_done, c - 1)
                    for h in range(DH):
                        nc.scalar.activation(hid[:, s, h], up_ps[:, s, h, 0:W], ACT.Relu,
                                             bias=b1[:, h:h + 1]).then_inc(hid_ready, 1)

                norm(0, 0)
                norm(1, 1)

                def both(c, s):
                    norm(c + 2, s)
                    act_up(c, s)

                tiles(act, CHUNKS - 2, 3, 2, both)
                for c in range(CHUNKS - 2, CHUNKS):
                    act_up(c, c % 2)
                act.wait_ge(var_ready, 1)
                nc.scalar.activation(tmp[:, :, 3], tmp[:, :, 2], ACT.Sqrt).then_inc(root_ready, 1)

            @block.tensor
            def _(pe):
                def up(c, s):
                    pe.wait_ge(normed, 2 * c + 2)
                    wait_past(pe, hid_ready, 2 * c - 2)
                    for o in range(DH):
                        for h in range(DH):
                            last = nc.tensor.matmul(up_ps[:, s, o, 0:W], w1[:, h, o * P:(o + 1) * P],
                                                    k.acc[:, h, bass.ds(c * W, W)], start=(h == 0), stop=(h == DH - 1))
                    last.then_inc(up_done, 1)

                def down(c, s):
                    pe.wait_ge(hid_ready, 2 * c + 2)
                    wait_past(pe, summed, 2 * c - 2)
                    for o in range(DH):
                        for h in range(DH):
                            last = nc.tensor.matmul(down_ps[:, s, o, 0:W], w2[:, h, o * P:(o + 1) * P], hid[:, s, h],
                                                    start=(h == 0), stop=(h == DH - 1))
                    last.then_inc(down_done, 1)

                pe.wait_ge(w_in, 96)
                up(0, 0)

                def both(c, s):
                    up(c + 1, 1 - s)
                    down(c, s)

                tiles(pe, CHUNKS - 1, 2, 2, both)
                down(CHUNKS - 1, (CHUNKS - 1) % 2)


def route_tokens(nc, k):
    with ExitStack() as ctx:
        sb = lambda name, shape, dt=F32: ctx.enter_context(nc.sbuf_tensor(name, shape, dt))
        pb = lambda name, shape: ctx.enter_context(nc.psum_tensor(name, shape, F32))
        sem = lambda name: ctx.enter_context(nc.semaphore(name))
        space = [k.acc[:, DH, :], 0]

        def work(rows, shape):
            n = int(np.prod(shape))
            at = space[0][0:rows, space[1]:space[1] + n]
            space[1] += n
            names = "abcd"[:len(shape)]
            if len(shape) == 1:
                return at
            return at.rearrange(f"p ({' '.join(names)}) -> p {' '.join(names)}", **dict(zip(names[1:], shape[1:])))

        x_in_sb = work(R, (2, 2, D))
        y = sb("r_y", [P, 2, DH, W])
        z = work(R, (2, 2, D))
        zt = sb("r_zt", [P, 2, DH, W])
        zr = sb("r_zr", [R, 4, ZW])
        wg = sb("r_wg", [P, DH, E])
        bg = sb("r_bg", [1, E])
        ones = sb("r_ones", [P, P])
        below = sb("r_below", [R, R])
        stats = sb("r_stats", [R, TILES, 6])
        mean = sb("r_mean", [R, TILES])
        rstd = sb("r_rstd", [R, TILES])
        tmp = sb("r_tmp", [R, 2, TILES])
        score, equal, which, rank = (work(P, (TILES, E)) for _ in range(4))
        first, second = (work(R, (TILES, E)) for _ in range(2))
        best = sb("r_best", [R, TILES])
        total, before, opened = (work(P, (E, TILES)) for _ in range(3))
        place = work(R, (K, TILES))
        ids_i = sb("r_ids_i", [R, TILES, K], I32)
        ids = work(R, (TILES, K))
        idx = sb("r_idx", [R, 4], I32)
        expert = sb("r_expert", [P, E])
        pad = work(P, (ZW,))
        pad_f = sb("r_pad_f", [P, E])
        pad_i = sb("r_pad_i", [P, E], I32)
        count = sb("r_count", [P, E])
        nt = sb("r_nt", [1, E])
        end = sb("r_end", [1, E])
        jump = sb("r_jump", [1, E])
        steps_of = sb("r_steps_of", [1, NT])
        past = z[0:1].rearrange("p s u d -> p (s u d)")[:, 0:SLOT_TILES * E].rearrange("p (s e) -> p s e", e=E)
        slot_f = sb("r_slot_f", [1, 2, SLOT_TILES])
        y_ps = pb("r_y_ps", [R, 2, 2, D])
        zt_ps = pb("r_zt_ps", [P, 2, DH, 256])
        score_ps = pb("r_score_ps", [P, TILES, E])
        rank_ps = pb("r_rank_ps", [P, TILES, E])
        total_ps = pb("r_total_ps", [P, TILES, E])

        w_in, chain, var_ready, root_ready, iotas = sem("r_w_in"), sem("r_chain"), sem("r_var"), sem("r_root"), sem("r_iotas")
        x_in = [sem("r_x_in0"), sem("r_x_in1")]
        y_ready, y_turned, summed, measured = sem("r_y_s"), sem("r_y_turned"), sem("r_summed"), sem("r_measured")
        z_ready, z_turned, z_taken, scored = sem("r_z_s"), sem("r_z_turned"), sem("r_z_taken"), sem("r_scored")
        masked, ranked, row_ready, may_scatter = sem("r_masked"), sem("r_ranked"), sem("r_row_s"), sem("r_may")
        scattered = [sem(f"r_scattered{q}") for q in range(4)]
        pads_ready, pads_stored, blank_stored = sem("r_pads"), sem("r_pads_stored"), sem("r_blank_stored")

        with nc.Block() as block:

            @block.sync
            def _(sp):
                sp.dma_start(wg[:, :, :], k.Wg.rearrange("(h p) e -> p h e", p=P)).then_inc(w_in, 16)
                sp.dma_start(bg[:, :], k.bg.rearrange("(o e) -> o e", o=1)).then_inc(w_in, 16)

                def load(c, s):
                    wait_past(sp, summed, c - 1)
                    sp.dma_start(x_in_sb[:, s], k.x[bass.ds(c * W, W), :].rearrange("(u p) d -> p u d", p=R)
                                 ).then_inc(x_in[s], 16)

                tiles(sp, CHUNKS, 2, 2, load)
                sp.wait_ge(pads_ready, 1)
                sp.dma_start(k.disp_rows[E * REGION:E * REGION + P, :], pad[:, :]).then_inc(blank_stored, 16)
                sp.wait_ge(blank_stored, 16)
                sp.wait_ge(pads_stored, 16 * E)

            @block.scalar
            def _(act):
                def norm(c, s):
                    wait_past(act, y_turned, c - 1)
                    for h in range(DH):
                        nc.scalar.activation(y[:, s, h], k.acc[:, h, bass.ds(c * W, W)], ACT.Identity,
                                             scale=k.norm2[:, 0, h:h + 1], bias=k.norm2[:, 1, h:h + 1]).then_inc(y_ready, 1)

                tiles(act, CHUNKS, 2, 2, norm)
                act.wait_ge(var_ready, 1)
                nc.scalar.activation(tmp[:, 1, :], tmp[:, 0, :], ACT.Sqrt).then_inc(root_ready, 1)

                def take(c, s):
                    act.wait_ge(z_turned, c + 1)
                    wait_past(act, scored, c - 1)
                    nc.scalar.copy(zt[:, s], zt_ps[:, s, :, 0:W]).then_inc(z_taken, 1)

                tiles(act, CHUNKS, 2, 2, take)

            @block.tensor
            def _(pe):
                def turn_y(c, s):
                    pe.wait_ge(y_ready, 2 * c + 2)
                    wait_past(pe, summed, c - 1)
                    for u in range(2):
                        for h in range(DH):
                            last = nc.tensor.transpose(y_ps[:, s, u, h * P:(h + 1) * P], y[:, s, h, u * R:(u + 1) * R],
                                                       k.ident[:, :])
                    last.then_inc(y_turned, 1)

                tiles(pe, CHUNKS, 2, 2, turn_y)
                pe.wait_ge(w_in, 32)

                def turn_z(c, s):
                    pe.wait_ge(z_ready, 2 * c + 2)
                    wait_past(pe, z_taken, c - 1)
                    for h in range(DH):
                        for u in range(2):
                            last = nc.tensor.transpose(zt_ps[:, s, h, u * R:(u + 1) * R], z[:, s, u, h * P:(h + 1) * P],
                                                       k.ident[0:R, 0:R])
                    last.then_inc(z_turned, 1)

                def score_of(c, s):
                    pe.wait_ge(z_taken, c + 1)
                    for u in range(2):
                        out = score_ps[0:R, bass.ds(c * 2 + u, 1), :].rearrange("p o e -> p (o e)")
                        for h in range(DH):
                            nc.tensor.matmul(out, zt[:, s, h, u * R:(u + 1) * R], wg[:, h, :], start=(h == 0), stop=False)
                        last = nc.tensor.matmul(out, ones[0:1, 0:R], bg[:, :], start=False, stop=True)
                    last.then_inc(scored, 1)

                turn_z(0, 0)

                def both(c, s):
                    turn_z(c + 1, 1 - s)
                    score_of(c, s)

                tiles(pe, CHUNKS - 1, 2, 2, both)
                score_of(CHUNKS - 1, (CHUNKS - 1) % 2)
                pe.wait_ge(masked, 1)
                flat = equal[0:R].rearrange("p t e -> p (t e)")
                nc.tensor.matmul(rank_ps[0:R].rearrange("p t e -> p (t e)"), below[:, :], flat, start=True, stop=True)
                nc.tensor.matmul(total_ps[:, :, :].rearrange("p t e -> p (t e)"), ones[0:R, :], flat, start=True,
                                 stop=True).then_inc(ranked, 1)

            @block.vector
            def _(dve):
                link = link_on(dve, chain)
                link(nc.vector.memset(ones[:, :], 1.0))
                nc.vector.tensor_scalar(below[:, :], k.iota_row[0:R, 0:R], k.iota_col[0:R, 0:1], None, ALU.is_gt)
                nc.vector.tensor_scalar(expert[:, :], k.iota_row[:, 0:E], float(-E), None, ALU.add)
                nc.vector.tensor_scalar(steps_of[:, :], k.iota_row[0:1, 0:NT], float(P), None, ALU.mult)
                nc.vector.memset(pad[:, 0:D], 0.0)
                nc.vector.memset(pad[:, D:ZW], float(NO_ROW))
                nc.vector.memset(opened, 1.0)
                link(nc.vector.memset(best[:, :], 0.0))
                link(nc.vector.memset(opened[:, :, 0:1], 0.0))
                dve.wait_ge(iotas, 1)
                link(nc.vector.tensor_copy(ids[:, :, :], ids_i[:, :, :]))

                def add(c, s):
                    dve.wait_ge(y_turned, c + 1)
                    dve.wait_ge(x_in[s], (c - s) * 8 + 16)
                    nc.vector.tensor_tensor(k.x1[:, bass.ds(c * 2, 2), :], y_ps[:, s], x_in_sb[:, s], ALU.add).then_inc(summed, 1)
                    dve.wait_ge(summed, c + 1)
                    for u in range(2):
                        nc.vector.bn_stats(stats[:, bass.ds(c * 2 + u, 1), :],
                                           k.x1[:, bass.ds(c * 2 + u, 1), :]).then_inc(measured, 1)

                tiles(dve, CHUNKS, 2, 2, add)
                dve.wait_ge(measured, TILES)

                def root(var, out):
                    nc.vector.tensor_scalar(var, var, EPS, None, ALU.add).then_inc(var_ready, 1)
                    dve.wait_ge(root_ready, 1)

                norm_scale(nc, link, stats, mean[:, :], rstd[:, :], tmp, root)

                def normalise(out, t):
                    return nc.vector.tensor_scalar(out, k.x1[:, bass.ds(t, 1), :].rearrange("p o d -> p (o d)"),
                                                   mean[:, bass.ds(t, 1)], rstd[:, bass.ds(t, 1)], ALU.subtract, ALU.mult)

                def norm(c, s):
                    wait_past(dve, z_turned, c - 1)
                    for u in range(2):
                        normalise(z[:, s, u], c * 2 + u).then_inc(z_ready, 1)

                tiles(dve, CHUNKS, 2, 2, norm)

                dve.wait_ge(scored, CHUNKS)
                spread_e = lambda a: a[:, :, None].to_broadcast([R, TILES, E])
                experts = expert[0:R, None, :].to_broadcast([R, TILES, E])
                link(nc.vector.tensor_copy(score[0:R], score_ps[0:R]))
                for choice in (first, second):
                    link(nc.vector.tensor_reduce(best[:, :], score[0:R], AX.X, ALU.max))
                    link(nc.vector.tensor_tensor(equal[0:R], score[0:R], spread_e(best), ALU.is_ge))
                    link(nc.vector.tensor_tensor(which[0:R], equal[0:R], experts, ALU.mult))
                    link(nc.vector.tensor_reduce(best[:, :], which[0:R], AX.X, ALU.min))
                    link(nc.vector.tensor_tensor(choice, experts, spread_e(best), ALU.is_equal))
                    link(nc.vector.scalar_tensor_tensor(score[0:R], choice, -NEG, score[0:R], ALU.mult, ALU.add))
                nc.vector.tensor_tensor(equal[0:R], first, second, ALU.add).then_inc(masked, 1)

                dve.wait_ge(ranked, 1)
                flat = lambda a: a.rearrange("p e t -> p (e t)")
                link(nc.vector.tensor_copy(total, total_ps[:, :, :].rearrange("p t e -> p e t")))
                link(nc.vector.tensor_tensor_scan(flat(before), flat(opened), flat(total), 0.0, ALU.mult, ALU.add))
                link(nc.vector.tensor_copy(count[:, :], before[:, :, TILES - 1]))
                link(nc.vector.tensor_tensor(before, before, total, ALU.subtract))
                link(nc.vector.tensor_tensor(rank[0:R], rank_ps[0:R], before[0:R].rearrange("p e t -> p t e"), ALU.add))
                regions = k.iota_row[0:R, None, 0:E].to_broadcast([R, TILES, E])
                link(nc.vector.scalar_tensor_tensor(rank[0:R], regions, float(REGION), rank[0:R], ALU.mult, ALU.add))
                for i, choice in enumerate((first, second)):
                    link(nc.vector.tensor_tensor(which[0:R], rank[0:R], choice, ALU.mult))
                    link(nc.vector.tensor_reduce(place[:, i], which[0:R], AX.X, ALU.add))
                link(nc.vector.scalar_tensor_tensor(pad_f[:, :], k.iota_row[:, 0:E], float(REGION), count[:, :], ALU.mult, ALU.add))
                nc.vector.tensor_scalar(pad_i[:, :], pad_f[:, :], k.iota_col[:, 0:1], None, ALU.add).then_inc(pads_ready, 1)

                def row(t, s):
                    for i in range(K):
                        q = 2 * s + i
                        if not isinstance(t, int) or t >= 2:
                            dve.wait_ge(scattered[q], (t - s) * 8)
                        normalise(zr[:, q, 0:D], t)
                        nc.vector.tensor_copy(zr[:, q, D:ZW], ids[:, bass.ds(t, 1), i])
                        nc.vector.tensor_copy(idx[:, q:q + 1], place[:, i, bass.ds(t, 1)]).then_inc(row_ready, 1)

                tiles(dve, TILES, 2, 2, row)

                link(nc.vector.tensor_tensor(past[:, 0:E, 0:E], count[0:1, 0:E, None].to_broadcast([1, E, E]),
                                             steps_of[:, None, 0:E].to_broadcast([1, E, E]), ALU.is_gt))
                link(nc.vector.tensor_reduce(nt[:, :], past[:, 0:E, 0:E], AX.X, ALU.add))
                for j in range(E, NT):
                    link(nc.vector.scalar_tensor_tensor(nt[:, :], count[0:1, :], steps_of[:, j:j + 1], nt[:, :], ALU.is_gt, ALU.add))
                link(nc.vector.tensor_tensor_scan(end[:, :], ones[0:1, 0:E], nt[:, :], 0.0, ALU.mult, ALU.add))
                link(nc.vector.tensor_scalar(jump[:, :], nt[:, :], float(-P), float(REGION), ALU.mult, ALU.add))
                slots = k.iota_row[0:1, 0:SLOT_TILES]
                link(nc.vector.tensor_tensor(past[:, :, :], slots[:, :, None].to_broadcast([1, SLOT_TILES, E]),
                                             end[:, None, :].to_broadcast([1, SLOT_TILES, E]), ALU.is_ge))
                link(nc.vector.tensor_reduce(slot_f[:, 1], past[:, :, :], AX.X, ALU.add))
                link(nc.vector.tensor_tensor(past[:, :, :], past[:, :, :], jump[:, None, :].to_broadcast([1, SLOT_TILES, E]), ALU.mult))
                link(nc.vector.tensor_reduce(slot_f[:, 0], past[:, :, :], AX.X, ALU.add))
                link(nc.vector.scalar_tensor_tensor(slot_f[:, 0], slots, float(P), slot_f[:, 0], ALU.mult, ALU.add))
                link(nc.vector.tensor_scalar(k.slots[:, 0], slot_f[:, 0], float(E * REGION), None, ALU.min))
                link(nc.vector.tensor_scalar(k.slots[:, 1], slot_f[:, 1], float(E - 1), None, ALU.min))

            @block.gpsimd
            def _(pool):
                nc.gpsimd.iota(ids_i[:, :, :], [[2 * R, TILES], [1, K]], base=0, channel_multiplier=K).then_inc(iotas, 1)
                pool.wait_ge(pads_ready, 1)
                for e in range(E):
                    nc.gpsimd.indirect_dma_start(k.disp_rows, bass.IndirectOffsetOnAxis(ap=pad_i[:, e:e + 1], axis=0),
                                                 pad[:, :], None).then_inc(pads_stored, 16)

                def scatter(t, s):
                    for i in range(K):
                        q = 2 * s + i
                        pool.wait_ge(row_ready, t * K + (i + 1))
                        pool.sem_inc(may_scatter, 1)
                        nc.gpsimd.indirect_dma_start(k.disp_rows, bass.IndirectOffsetOnAxis(ap=idx[:, q:q + 1], axis=0),
                                                     zr[:, q, :], None).then_inc(scattered[q], 16)

                tiles(pool, TILES, 2, 2, scatter)
                for q in range(4):
                    pool.wait_ge(scattered[q], 8 * TILES)


def apply_experts(nc, k):
    RING = 4
    with ExitStack() as ctx:
        pb = lambda name, shape: ctx.enter_context(nc.psum_tensor(name, shape, F32))
        sb = lambda name, shape, dt=F32: ctx.enter_context(nc.sbuf_tensor(name, shape, dt))
        sem = lambda name: ctx.enter_context(nc.semaphore(name))
        space = [k.acc[:, 0:DH, :].rearrange("p h n -> p (h n)"), 0]

        def work(shape):
            n = int(np.prod(shape))
            at = space[0][:, space[1]:space[1] + n]
            space[1] += n
            names = "abcd"[:len(shape)]
            return at.rearrange(f"p ({' '.join(names)}) -> p {' '.join(names)}", **dict(zip(names[1:], shape[1:])))

        be1, be2 = work((E, HID)), work((E, D))
        z = work((RING, ZW))
        zt = work((2, DH, P))
        hid = work((2, HID))
        hid_t = work((2, HC, P))
        y = work((RING, D))
        idx = sb("x_idx", [P, RING], I32)
        zt_ps = pb("x_zt_ps", [P, 2, 512])
        hid_ps = pb("x_hid_ps", [P, 2, HID])
        hid_t_ps = pb("x_hid_t_ps", [P, 2, HC, P])
        y_ps = pb("x_y_ps", [P, 2, 512])
        bias_in = sem("x_bias_in")
        z_in = [sem(f"x_z_in{q}") for q in range(RING)]
        stored = [sem(f"x_stored{q}") for q in range(RING)]
        z_turned, zt_ready, up_done, hid_ready, gelu_done = sem("x_z_turned"), sem("x_zt"), sem("x_up"), sem("x_hid_s"), sem("x_gelu")
        hid_turned, hid_t_ready, down_done, y_ready, may_store = (sem("x_hid_turned"), sem("x_hid_t_s"), sem("x_down"), sem("x_y_s"),
                                                                  sem("x_may"))
        n_main = SLOT_TILES - 2

        with nc.Block() as block:

            @block.sync
            def _(sp):
                for e in range(E):
                    sp.dma_start(be1[:, e], k.be1[e].partition_broadcast(P)).then_inc(bias_in, 16)
                    sp.dma_start(be2[:, e], k.be2[e].partition_broadcast(P)).then_inc(bias_in, 16)

                def load(s, q):
                    row = nc.values_load_multi_w_load_instructions(k.slots[:, 0, bass.ds(s, 1)], engines=[mybir.EngineType.SP],
                                                                   min_val=0, max_val=E * REGION)[1][0]
                    wait_past(sp, y_ready, s - (RING - 1))
                    sp.dma_start(z[:, q], k.disp_rows[bass.ds(row, P), :]).then_inc(z_in[q], 16)

                tiles(sp, SLOT_TILES, RING, RING, load)

            @block.gpsimd
            def _(pool):
                def store(s, q):
                    pool.wait_ge(y_ready, s + 1)
                    pool.sem_inc(may_store, 1)
                    nc.gpsimd.indirect_dma_start(k.moe_rows, bass.IndirectOffsetOnAxis(ap=idx[:, q:q + 1], axis=0), y[:, q],
                                                 None, bounds_check=K * N - 1, oob_is_err=False).then_inc(stored[q], 16)

                tiles(pool, SLOT_TILES, RING, RING, store)
                for q in range(RING):
                    pool.wait_ge(stored[q], 16 * len(range(q, SLOT_TILES, RING)))

            @block.tensor
            def _(pe):
                def experts_of(s, n):
                    return nc.values_load_multi_w_load_instructions(k.slots[:, 1, bass.ds(s, n)], engines=[mybir.EngineType.PE],
                                                                    min_val=0, max_val=E - 1)[1]

                def turn_z(s, q):
                    pe.wait_ge(z_in[q % RING], (s - q % RING) * (16 // RING) + 16)
                    wait_past(pe, zt_ready, s - 1)
                    for h in range(DH):
                        last = nc.tensor.transpose(zt_ps[:, q % 2, h * P:(h + 1) * P], z[:, q % RING, h * P:(h + 1) * P],
                                                   k.ident[:, :])
                    last.then_inc(z_turned, 1)

                def up(s, q, e):
                    pe.wait_ge(zt_ready, s + 1)
                    wait_past(pe, hid_ready, s - 1)
                    for h in range(DH):
                        last = nc.tensor.matmul(hid_ps[:, q % 2], zt[:, q % 2, h], k.we1[:, bass.ds(e, 1), h, :].rearrange(
                            "p o n -> p (o n)"), start=(h == 0), stop=(h == DH - 1))
                    last.then_inc(up_done, 1)

                def turn_hid(s, q):
                    pe.wait_ge(gelu_done, s + 1)
                    wait_past(pe, hid_t_ready, s - 1)
                    for j in range(HC):
                        last = nc.tensor.transpose(hid_t_ps[:, q % 2, j], hid[:, q % 2, j * P:(j + 1) * P], k.ident[:, :])
                    last.then_inc(hid_turned, 1)

                def down(s, q, e):
                    pe.wait_ge(hid_t_ready, s + 1)
                    wait_past(pe, y_ready, s - 1)
                    for j in range(HC):
                        last = nc.tensor.matmul(y_ps[:, q % 2, 0:D], hid_t[:, q % 2, j], k.we2[:, bass.ds(e, 1), j, :].rearrange(
                            "p o n -> p (o n)"), start=(j == 0), stop=(j == HC - 1))
                    last.then_inc(down_done, 1)

                pe.wait_ge(k.experts_in, 32 * E)
                turn_z(0, 0)
                turn_z(1, 1)
                up(0, 0, experts_of(0, 1)[0])

                def step(s, q):
                    e = experts_of(s, 2)
                    turn_hid(s, q)
                    up(s + 1, q + 1, e[1])
                    turn_z(s + 2, q + 2)
                    down(s, q, e[0])

                tiles(pe, n_main, RING, RING, step)
                e = experts_of(n_main, 2)
                turn_hid(n_main, n_main % 2)
                up(n_main + 1, n_main + 1, e[1])
                down(n_main, n_main % 2, e[0])
                turn_hid(n_main + 1, n_main + 1)
                down(n_main + 1, n_main + 1, e[1])

            @block.scalar
            def _(act):
                def take_zt(s, q):
                    act.wait_ge(z_turned, s + 1)
                    wait_past(act, up_done, s - 1)
                    nc.scalar.copy(zt[:, q % 2], zt_ps[:, q % 2, 0:D].rearrange("p (h n) -> p h n", h=DH)).then_inc(zt_ready, 1)

                def gelu(s, q):
                    act.wait_ge(hid_ready, s + 1)
                    nc.scalar.activation(hid[:, q % 2], hid[:, q % 2], ACT.Gelu).then_inc(gelu_done, 1)

                take_zt(0, 0)
                take_zt(1, 1)

                def step(s, q):
                    gelu(s, q)
                    take_zt(s + 2, q)

                tiles(act, n_main, 2, 2, step)
                gelu(n_main, n_main)
                gelu(n_main + 1, n_main + 1)

            @block.vector
            def _(dve):
                def experts_of(s, n):
                    return nc.values_load_multi_w_load_instructions(k.slots[:, 1, bass.ds(s, n)], engines=[mybir.EngineType.DVE],
                                                                    min_val=0, max_val=E - 1)[1]

                def bias_up(s, q, e):
                    dve.wait_ge(up_done, s + 1)
                    wait_past(dve, hid_turned, s - 1)
                    nc.vector.tensor_tensor(hid[:, q % 2], hid_ps[:, q % 2], be1[:, bass.ds(e, 1), :].rearrange("p o n -> p (o n)"),
                                            ALU.add).then_inc(hid_ready, 1)

                def take_hid(s, q):
                    dve.wait_ge(hid_turned, s + 1)
                    wait_past(dve, down_done, s - 1)
                    nc.vector.tensor_copy(hid_t[:, q % 2], hid_t_ps[:, q % 2]).then_inc(hid_t_ready, 1)

                def bias_down(s, q, e):
                    if not isinstance(s, int) or s >= RING:
                        dve.wait_ge(stored[q % RING], (s - q % RING) * (16 // RING))
                    nc.vector.tensor_copy(idx[:, q % RING:q % RING + 1], z[:, q % RING, D:ZW])
                    dve.wait_ge(down_done, s + 1)
                    nc.vector.tensor_tensor(y[:, q % RING], y_ps[:, q % 2, 0:D], be2[:, bass.ds(e, 1), :].rearrange("p o n -> p (o n)"),
                                            ALU.add).then_inc(y_ready, 1)

                dve.wait_ge(bias_in, 32 * E)
                bias_up(0, 0, experts_of(0, 1)[0])

                def step(s, q):
                    e = experts_of(s, 2)
                    take_hid(s, q)
                    bias_up(s + 1, q + 1, e[1])
                    bias_down(s, q, e[0])

                tiles(dve, SLOT_TILES - 1, RING, RING, step)
                last = SLOT_TILES - 1
                e = experts_of(last, 1)
                take_hid(last, last % RING)
                bias_down(last, last % RING, e[0])


def combine(nc, k):
    STEP = 5
    ROUNDS = TILES // STEP
    with ExitStack() as ctx:
        sem = lambda name: ctx.enter_context(nc.semaphore(name))
        both = k.acc[0:R, 0:DH, :].rearrange("p h n -> p (h n)")[:, 0:2 * STEP * K * D].rearrange(
            "p (s t k d) -> p s t k d", s=2, t=STEP, k=K)
        rows_in = [sem("c_rows_in0"), sem("c_rows_in1")]
        first, summed, stored = sem("c_first"), sem("c_summed"), sem("c_stored")

        with nc.Block() as block:

            @block.sync
            def _(sp):
                def load(i, s):
                    wait_past(sp, summed, i - 1)
                    sp.dma_start(both[:, s], k.moe_rows[bass.ds(i * (STEP * R * K), STEP * R * K), :].rearrange(
                        "(t p k) d -> p t k d", p=R, k=K)).then_inc(rows_in[s], 16)

                tiles(sp, ROUNDS, 2, 2, load)

            @block.vector
            def _(dve):
                def add(i, s):
                    x1 = k.x1[:, bass.ds(i * STEP, STEP), :]
                    dve.wait_ge(rows_in[s], (i - s) * 8 + 16)
                    nc.vector.tensor_tensor(both[:, s, :, 0], both[:, s, :, 0], both[:, s, :, 1], ALU.add).then_inc(first, 1)
                    dve.wait_ge(first, i + 1)
                    nc.vector.tensor_tensor(x1, x1, both[:, s, :, 0], ALU.add).then_inc(summed, 1)

                tiles(dve, ROUNDS, 2, 2, add)

            @block.scalar
            def _(act):
                def store(i, s):
                    act.wait_ge(summed, i + 1)
                    act.dma_start(k.out[bass.ds(i * (STEP * R), STEP * R), :].rearrange("(t p) d -> p t d", p=R),
                                  k.x1[:, bass.ds(i * STEP, STEP), :]).then_inc(stored, 16)

                tiles(act, ROUNDS, 2, 2, store)
                act.wait_ge(stored, 16 * ROUNDS)


INS = ["x", "src", "dst", "L0_gnn_W_l", "L0_gnn_W_r", "L0_gnn_att", "L0_gnn_bias", "L0_gnn_W1", "L0_gnn_b1", "L0_gnn_W2",
       "L0_gnn_b2", "L0_gnn_gamma1", "L0_gnn_beta1", "L0_gnn_gamma2", "L0_gnn_beta2", "L0_ffn_Wg", "L0_ffn_bg", "L0_ffn_W1",
       "L0_ffn_b1", "L0_ffn_W2", "L0_ffn_b2"]


def graph_ffn_kernel(nc, *args):
    k = Program()
    *ins, k.out = args
    (k.x, k.src, k.dst, k.W_l, k.W_r, k.att, k.bias, k.W1, k.b1, k.W2, k.b2, k.gamma1, k.beta1, k.gamma2, k.beta2, k.Wg,
     k.bg, k.We1, k.be1, k.We2, k.be2) = ins
    dram = lambda name, shape, dt=F32: nc.dram_tensor(name, shape, dt).ap()
    k.first_rows = dram("first_rows", [ETP + 1])
    k.last_rows = dram("last_rows", [ETP + 1])
    k.base_rows = dram("base_rows", [1, ETP], I32)
    k.rel_rows = dram("rel_rows", [ETP * P], BF16)
    k.gate_rows = dram("gate_rows", [NCH, GATES], BF16)
    k.go_on_rows = dram("go_on_rows", [NCH, T])
    k.xl_rows = dram("xl_rows", [COLS, XW])
    k.xr_rows = dram("xr_rows", [COLS, XW])
    k.zt_cols = dram("zt_cols", [P, 2, COLS])
    k.disp_rows = dram("disp_rows", [E * REGION + P, ZW])
    k.moe_rows = dram("moe_rows", [K * N, D])

    with ExitStack() as ctx:
        keep = lambda name, shape, dt=F32: ctx.enter_context(nc.sbuf_tensor(name, shape, dt))
        k.iota_row = keep("iota_row", [P, P])
        k.iota_col = keep("iota_col", [P, 1])
        k.ident = keep("ident", [P, P])
        k.norm1 = keep("norm1", [P, 2, DH])
        k.norm2 = keep("norm2", [P, 2, DH])
        k.slots = keep("slots", [1, 2, SLOT_TILES], I32)
        k.acc = keep("acc", [P, DH + 1, COLS])
        k.experts_in = ctx.enter_context(nc.semaphore("experts_in"))
        with ExitStack() as edges:
            sb = lambda name, shape, dt=F32: edges.enter_context(nc.sbuf_tensor(name, shape, dt))
            k.neg_col = sb("neg_col", [P, 1])
            k.one = sb("one", [P, 1])
            k.head_rows = sb("head_rows", [1, H + 2, P])
            k.src_e = sb("src_e", [P, ETP], I32)
            k.neg_rel = sb("neg_rel", [P, ETP])
            k.att_pos = sb("att_pos", [P, D])
            k.bases = sb("bases", [1, ETL], I32)
            prepare_edges(nc, k)
            project_nodes(nc, k)
            attend(nc, k)
        join_heads(nc, k)
        k.we1 = keep("we1", [P, E, DH, HID])
        k.we2 = keep("we2", [P, E, HC, D])
        feed_forward(nc, k)
        k.x1 = keep("x1", [R, TILES, D])
        route_tokens(nc, k)
        apply_experts(nc, k)
        combine(nc, k)


def kernel(**inputs):
    import concourse.bacc as _bacc
    from concourse.bass_utils import run_bass_kernel_spmd as _run

    nc = _bacc.Bacc("TRN2", target_bir_lowering=False, num_devices=1)
    arrays, args = {}, []
    for name in INS:
        a = np.ascontiguousarray(inputs[name])
        arrays[f"in_{name}_dram"] = a
        args.append(nc.dram_tensor(f"in_{name}_dram", a.shape, mybir.dt.from_np(a.dtype), kind="ExternalInput").ap())
    args.append(nc.dram_tensor("out_dram", (N, D), F32, kind="ExternalOutput").ap())
    graph_ffn_kernel(nc, *args)
    r = _run(nc, [arrays], core_ids=[0])
    return r.results[0]["out_dram"]
```

```python
from contextlib import ExitStack

import concourse.bass as bass
import numpy as np
from concourse import mybir

F32 = mybir.dt.float32
BF16 = mybir.dt.bfloat16
I32 = mybir.dt.int32
U32 = mybir.dt.uint32
ALU = mybir.AluOpType
ACT = mybir.ActivationFunctionType
AX = mybir.AxisListType

P = 128
N = 6250
D = 256
DH = D // P
H = 4
C = D // H
SLOPE = 0.2
EPS = 1e-5
SEG_EPS = 1e-16
NEG = 2.0 ** 100

EDGES = 106250
NT = (N + P - 1) // P
NTAIL = N - (NT - 1) * P
NTP = NT + 1
COLS = NTP * P
ET = (EDGES + P - 1) // P
T = 32
NCH = (ET + T - 1) // T
ETL = NCH * T
Q = (ETL + P - 1) // P
ETP = Q * P
FULLQ = EDGES // (P * P)
ROWS_LAST = (EDGES - FULLQ * P * P) // P
EDGES_LAST = EDGES - FULLQ * P * P - ROWS_LAST * P
GATES = 2 * H * (T + 1) + 2 * H * T
XW = D + 8

E = 8
HID = 512
HC = HID // P
K = 2
R = 125
TILES = N // R
W = 2 * R
CHUNKS = N // W
REGION = NT * P + P
SLOT_TILES = (K * N + E * (P - 1)) // P
SLOT_TILES += SLOT_TILES % 2
ZW = D + 1
NO_ROW = 4 * COLS


def link_on(dve, k):

    def link(ins):
        k.linked += 1
        ins.then_inc(k.chain, 1)
        dve.wait_ge(k.chain, k.linked)

    return link


def ask_root(nc, k, dve, var):
    k.asked += 1
    nc.vector.tensor_scalar(var, var, EPS, None, ALU.add).then_inc(k.var_ready, 1)
    dve.wait_ge(k.root_ready, k.asked)


def give_root(nc, k, act, root, var):
    k.given += 1
    act.wait_ge(k.var_ready, k.given)
    nc.scalar.activation(root, var, ACT.Sqrt).then_inc(k.root_ready, 1)


def tiles(engine, n, front, unroll, body):
    for t in range(front):
        body(t, t % unroll)
    rounds = (n - front) // unroll
    if rounds:
        with engine.Fori(0, rounds) as i:
            for u in range(unroll):
                body(i * unroll + (front + u), (front + u) % unroll)
    for t in range(front + rounds * unroll, n):
        body(t, t % unroll)


def wait_past(engine, semaphore, value):
    if isinstance(value, int) and value <= 0:
        return
    engine.wait_ge(semaphore, value)


def gate_views(row):
    f, b = H * (T + 1), H * T
    cut = lambda at, n: row[:, at:at + n].rearrange("p (h t) -> p h t", h=H)
    return cut(0, f), cut(f, f), cut(2 * f, b), cut(2 * f + b, b)


class Program:
    pass


def prepare_edges(nc, k):
    with ExitStack() as ctx:
        sb = lambda name, shape, dt=F32: ctx.enter_context(nc.sbuf_tensor(name, shape, dt))
        sem = lambda name: ctx.enter_context(nc.semaphore(name))
        src_ps = ctx.enter_context(nc.psum_tensor("p_src_ps", [P, 2, 512], F32))
        rel_ps = ctx.enter_context(nc.psum_tensor("p_rel_ps", [P, 2, 512], F32))
        rows_i = sb("p_rows_i", [P, 2, Q, P], I32)
        rows_f = sb("p_rows_f", [P, 2, Q, P])
        rel = sb("p_rel", [P, Q, P])
        rel_bf = sb("p_rel_bf", [P, Q, P], BF16)
        ends = sb("p_ends", [P, 2, Q])
        ints = sb("p_ints", [P, P + 1], I32)
        first = sb("p_first", [NCH, T + 2])
        last = sb("p_last", [NCH, T + 2])
        go_on = sb("p_go_on", [NCH, T + 1])
        single = sb("p_single", [NCH, T + 1])
        gates = sb("p_gates", [NCH, GATES], BF16)
        blank = sb("p_blank", [1, 2])
        padded, loaded, iotas = sem("p_padded"), sem("p_loaded"), sem("p_iotas")
        rows_ready, rel_ready, turned = sem("p_rows"), sem("p_rel_s"), sem("p_turned")
        ends_ready, stored, ends_in, gates_ready = sem("p_ends_s"), sem("p_stored"), sem("p_ends_in"), sem("p_gates_s")

        with nc.Block() as block:

            @block.sync
            def _(sp):
                for a, name in enumerate((k.dst, k.src)):
                    sp.dma_start(rows_i[:, a, 0:FULLQ, :],
                                 name[0:FULLQ * P * P].rearrange("(q p e) -> p q e", p=P, e=P)).then_inc(loaded, 16)
                sp.wait_ge(padded, 2)
                for a, name in enumerate((k.dst, k.src)):
                    at = FULLQ * P * P
                    if ROWS_LAST:
                        sp.dma_start(rows_i[0:ROWS_LAST, a, FULLQ, :],
                                     name[at:at + ROWS_LAST * P].rearrange("(p e) -> p e", e=P)).then_inc(loaded, 16)
                        at += ROWS_LAST * P
                    if EDGES_LAST:
                        sp.dma_start(rows_i[ROWS_LAST:ROWS_LAST + 1, a, FULLQ, 0:EDGES_LAST],
                                     name[at:EDGES].rearrange("(p e) -> p e", p=1)).then_inc(loaded, 16)
                sp.wait_ge(ends_ready, 1)
                with nc.allow_non_contiguous_dma(reason="one number of each tile"):
                    sp.dma_start(k.first_rows[1:1 + ETP].rearrange("(q p) -> p q", p=P), ends[:, 0]).then_inc(stored, 16)
                    sp.dma_start(k.last_rows[1:1 + ETP].rearrange("(q p) -> p q", p=P), ends[:, 1]).then_inc(stored, 16)
                    sp.dma_start(k.base_rows[0].rearrange("(q p) -> p q", p=P),
                                 rows_i[:, 0, :, 0]).then_inc(stored, 16)
                sp.dma_start(k.first_rows[0:1], blank[0:1, 0:1]).then_inc(stored, 16)
                sp.dma_start(k.last_rows[0:1], blank[0:1, 1:2]).then_inc(stored, 16)
                sp.wait_ge(rel_ready, 2)
                sp.dma_start(k.rel_rows.rearrange("(q p e) -> p q e", p=P, e=P), rel_bf[:, :, :]).then_inc(stored, 16)
                sp.wait_ge(stored, 96)
                for rows, out in ((k.first_rows, first), (k.last_rows, last)):
                    overlapping = bass.AP(tensor=rows.tensor, offset=0, ap=[[T, NCH], [1, T + 2]])
                    sp.dma_start(out[:, :], overlapping).then_inc(ends_in, 16)
                sp.wait_ge(gates_ready, 1)
                sp.dma_start(k.gate_rows, gates[:, :]).then_inc(stored, 16)
                sp.dma_start(k.go_on_rows, go_on[:, 0:T]).then_inc(stored, 16)
                sp.wait_ge(stored, 128)

            @block.gpsimd
            def _(pool):
                nc.gpsimd.iota(ints[:, 0:P], [[1, P]], base=0, channel_multiplier=0).then_inc(iotas, 1)
                nc.gpsimd.iota(ints[:, P:P + 1], [[0, 1]], base=0, channel_multiplier=1).then_inc(iotas, 1)

            @block.vector
            def _(dve):
                link = link_on(dve, k)
                nc.vector.memset(rows_i[:, 0, FULLQ:Q, :], N).then_inc(padded, 1)
                nc.vector.memset(rows_i[:, 1, FULLQ:Q, :], 0).then_inc(padded, 1)
                nc.vector.memset(blank[:, :], -1.0)
                nc.vector.memset(k.one[:, :], 1.0)
                link(nc.vector.memset(k.head_rows[:, :, :], 0.0))
                for h in range(H):
                    nc.vector.memset(k.head_rows[:, h, h:2 * H:H], 1.0)
                for h in range(2):
                    nc.vector.memset(k.head_rows[:, H + h, h * C:(h + 1) * C], 1.0)
                dve.wait_ge(iotas, 2)
                link(nc.vector.tensor_copy(k.iota_row[:, :], ints[:, 0:P]))
                link(nc.vector.tensor_copy(k.iota_col[:, :], ints[:, P:P + 1]))
                link(nc.vector.tensor_scalar(k.neg_col[:, :], k.iota_col[:, :], -1.0, None, ALU.mult))
                link(nc.vector.tensor_scalar(k.ident[:, :], k.iota_row[:, :], k.iota_col[:, 0:1], None, ALU.is_equal))
                dve.wait_ge(loaded, 32 * (1 + (ROWS_LAST > 0) + (EDGES_LAST > 0)))
                link(nc.vector.tensor_copy(rows_f[:, 0], rows_i[:, 0]))
                nc.vector.tensor_copy(rows_f[:, 1], rows_i[:, 1]).then_inc(rows_ready, 1)
                nc.vector.tensor_copy(ends[:, 0], rows_f[:, 0, :, 0])
                nc.vector.tensor_copy(ends[:, 1], rows_f[:, 0, :, P - 1]).then_inc(ends_ready, 1)
                nc.vector.tensor_tensor(rel[:, :, :], rows_f[:, 0], rows_f[:, 0, :, 0:1].to_broadcast([P, Q, P]),
                                        ALU.subtract).then_inc(rel_ready, 1)
                dve.wait_ge(rel_ready, 1)
                nc.vector.tensor_copy(rel_bf[:, :, :], rel[:, :, :]).then_inc(rel_ready, 1)
                for g in range((Q + 3) // 4):
                    n = min(4, Q - 4 * g)
                    dve.wait_ge(turned, 2 * g + 2)
                    at = slice(4 * g * P, (4 * g + n) * P)
                    nc.vector.tensor_copy(k.src_e[:, at], src_ps[:, g, 0:n * P])
                    nc.vector.tensor_scalar(k.neg_rel[:, at], rel_ps[:, g, 0:n * P], -1.0, None, ALU.mult)
                dve.wait_ge(ends_in, 32)
                j = T + 1
                link(nc.vector.tensor_tensor(go_on[:, :], first[:, 1:j + 1], last[:, 0:j], ALU.is_equal))
                link(nc.vector.tensor_tensor(single[:, :], first[:, 0:j], last[:, 0:j], ALU.is_equal))
                g_in, g_pass, b_in, b_pass = gate_views(gates[:, :])
                link(nc.vector.memset(gates[:, :], -NEG))
                for h in range(H):
                    nc.vector.tensor_scalar(g_in[:, h, 0:T], go_on[:, 0:T], 1.0, NEG, ALU.subtract, ALU.mult)
                    nc.vector.memset(g_in[:, h, T:j], 0.0)
                    nc.vector.tensor_scalar(g_pass[:, h, T:j], single[:, T:j], 1.0, NEG, ALU.subtract, ALU.mult)
                    nc.vector.tensor_scalar(b_in[:, h, 0:T - 1], go_on[:, 1:T], 1.0, NEG, ALU.subtract, ALU.mult)
                link(nc.vector.tensor_tensor(last[:, 0:T], go_on[:, 0:T], single[:, 0:T], ALU.mult))
                for h in range(H):
                    nc.vector.tensor_scalar(g_pass[:, h, 1:T], last[:, 1:T], 1.0, NEG, ALU.subtract, ALU.mult)
                link(nc.vector.tensor_tensor(first[:, 0:T - 1], go_on[:, 1:T], single[:, 2:T + 1], ALU.mult))
                for h in range(H):
                    link(nc.vector.tensor_scalar(b_pass[:, h, 0:T - 1], first[:, 0:T - 1], 1.0, NEG, ALU.subtract,
                                                 ALU.mult))
                nc.vector.memset(blank[:, :], -1.0).then_inc(gates_ready, 1)

            @block.tensor
            def _(pe):
                pe.wait_ge(rows_ready, 1)
                pe.wait_ge(k.chain, 5)
                pe.wait_ge(rel_ready, 1)
                for g in range((Q + 3) // 4):
                    for out, rows in ((src_ps, rows_f[:, 1]), (rel_ps, rel[:, :, :])):
                        for q in range(4 * g, min(4 * g + 4, Q)):
                            last = nc.tensor.transpose(out[:, g, (q % 4) * P:(q % 4 + 1) * P], rows[:, q, :],
                                                       k.ident[:, :])
                        last.then_inc(turned, 1)


def inverse_root(nc, link, out, var, root):
    link(nc.vector.reciprocal(out, root))
    link(nc.vector.tensor_tensor(root, out, out, ALU.mult))
    link(nc.vector.scalar_tensor_tensor(root, root, -0.5, var, ALU.mult, ALU.mult))
    link(nc.vector.scalar_tensor_tensor(out, root, 1.5, out, ALU.add, ALU.mult))


def norm_scale(nc, link, st, mean, rstd, tmp, root):
    half = D // 2
    link(nc.vector.tensor_tensor(tmp[:, 0, :], st[:, :, 1], st[:, :, 4], ALU.subtract))
    link(nc.vector.tensor_tensor(tmp[:, 0, :], tmp[:, 0, :], tmp[:, 0, :], ALU.mult))
    link(nc.vector.tensor_tensor(tmp[:, 1, :], st[:, :, 2], st[:, :, 5], ALU.add))
    link(nc.vector.tensor_scalar(tmp[:, 0, :], tmp[:, 0, :], 0.25, None, ALU.mult))
    link(nc.vector.scalar_tensor_tensor(tmp[:, 0, :], tmp[:, 1, :], 0.5 / half, tmp[:, 0, :], ALU.mult, ALU.add))
    link(nc.vector.tensor_tensor(mean, st[:, :, 1], st[:, :, 4], ALU.add))
    link(nc.vector.tensor_scalar(mean, mean, 0.5, None, ALU.mult))
    root(tmp[:, 0, :])
    inverse_root(nc, link, rstd, tmp[:, 0, :], tmp[:, 1, :])


def project_nodes(nc, k):
    with ExitStack() as ctx:
        sb = lambda name, shape, dt=F32: ctx.enter_context(nc.sbuf_tensor(name, shape, dt))
        pb = lambda name, shape: ctx.enter_context(nc.psum_tensor(name, shape, F32))
        sem = lambda name: ctx.enter_context(nc.semaphore(name))
        x_all = sb("x_all", [P, NTP, D])
        stats = sb("ln_stats", [P, NTP, 6])
        mean = sb("ln_mean", [P, NTP])
        rstd = sb("ln_rstd", [P, NTP])
        tmp = sb("ln_tmp", [P, 2, NTP])
        w_ext = sb("w_ext", [P, 2, 2, XW])
        w_att = sb("w_att", [P, 2, 2, D])
        att_all = sb("att_all", [P, D])
        z_sb = sb("z_sb", [P, 2, D])
        zt_sb = sb("zt_sb", [P, 2, 2, P])
        xl_sb = sb("xl_sb", [P, 2, XW])
        xr_sb = sb("xr_sb", [P, 2, XW])
        f_sb = sb("f_sb", [P, 2, D])
        g_sb = sb("g_sb", [P, 2, D])
        lin = sb("lin", [P, 2, H])
        red = sb("red", [P, 2, H])
        zt_ps = pb("zt_ps", [P, 2, 512])
        xl_ps = pb("xl_ps", [P, 2, 512])
        xr_ps = pb("xr_ps", [P, 2, 512])
        blank, x_in, w_in = sem("n_blank"), sem("n_x_in"), sem("n_w_in")
        stat_done, w_ready = sem("n_stat"), sem("n_w_ready")
        z_ready, zt_done, zt_taken = sem("n_z"), sem("n_zt"), sem("n_zt_taken")
        z_kept = [sem("n_z_kept0"), sem("n_z_kept1")]
        mm_done, xl_ready, xr_ready, xr_full = sem("n_mm"), sem("n_xl"), sem("n_xr"), sem("n_xr_full")
        f_ready, g_ready, red_ready, lin_ready = sem("n_f"), sem("n_g"), sem("n_red"), sem("n_lin")
        stored = [sem("n_stored0"), sem("n_stored1")]

        with nc.Block() as block:

            @block.sync
            def _(sp):
                sp.dma_start(att_all[:, :], k.att.rearrange("h c -> (h c)").partition_broadcast(P)).then_inc(w_in, 16)
                for a, w in enumerate((k.W_l, k.W_r)):
                    sp.dma_start(w_ext[:, a, :, 0:D], w.rearrange("(h p) n -> p h n", p=P)).then_inc(w_in, 16)
                step = NT // 2
                for t in range(0, NT - 1, step):
                    sp.dma_start(x_all[:, t:t + step, :],
                                 k.x[t * P:(t + step) * P, :].rearrange("(t p) d -> p t d", p=P)).then_inc(x_in, 16)
                sp.wait_ge(blank, 1)
                sp.dma_start(x_all[0:NTAIL, NT - 1, :], k.x[(NT - 1) * P:N, :]).then_inc(x_in, 16)

                def store(t, s):
                    sp.wait_ge(xr_full, t + 1)
                    row = t * P
                    sp.dma_start(k.xl_rows[bass.ds(row, P), :], xl_sb[:, s, :]).then_inc(stored[s], 16)
                    sp.dma_start(k.xr_rows[bass.ds(row, P), :], xr_sb[:, s, :]).then_inc(stored[s], 16)

                tiles(sp, NTP, 2, 2, store)
                for s in range(2):
                    sp.wait_ge(stored[s], 16 * NTP)

            @block.gpsimd
            def _(pool):
                nc.gpsimd.memset(k.acc[:, :, :], 0.0)

                def keep(t, s):
                    pool.wait_ge(z_ready, t + 1)
                    pool.dma_start(k.z_rows[bass.ds(t * P, P), :], z_sb[:, s]).then_inc(z_kept[s], 16)

                tiles(pool, NTP, 2, 2, keep)
                for s in range(2):
                    pool.wait_ge(z_kept[s], 8 * NTP)

            @block.vector
            def _(dve):
                link = link_on(dve, k)
                nc.vector.memset(x_all[:, NT - 1:NTP, :], 0.0).then_inc(blank, 1)
                dve.wait_ge(w_in, 48)
                for a in range(2):
                    for h in range(2):
                        link(nc.vector.scalar_tensor_tensor(w_att[:, a, h, :], w_ext[:, a, h, 0:D], SLOPE,
                                                            att_all[:, :], ALU.mult, ALU.mult))
                        nc.vector.memset(w_ext[:, a, h, D + H:XW], 0.0)
                        link(nc.vector.tensor_reduce(w_ext[:, a, h, D:D + H],
                                                     w_att[:, a, h, :].rearrange("p (h c) -> p h c", c=C), AX.X,
                                                     ALU.add))
                nc.vector.tensor_scalar(k.att_pos[:, :], att_all[:, :], 1.0 - SLOPE, None, ALU.mult).then_inc(w_ready, 1)
                dve.wait_ge(x_in, 16 * (2 + 1))
                with dve.Fori(0, NTP // 2) as i:
                    for u in range(2):
                        nc.vector.bn_stats(stats[:, bass.ds(i * 2 + u, 1), :],
                                           x_all[:, bass.ds(i * 2 + u, 1), :]).then_inc(stat_done, 1)
                dve.wait_ge(stat_done, NTP)

                root = lambda var: ask_root(nc, k, dve, var)
                norm_scale(nc, link, stats, mean[:, :], rstd[:, :], tmp, root)

                def normalise(t, s):
                    wait_past(dve, zt_done, t - 1)
                    if not isinstance(t, int) or t >= 2:
                        dve.wait_ge(z_kept[s], (t - s) * 8)
                    nc.vector.tensor_scalar(z_sb[:, s, :], x_all[:, bass.ds(t, 1), :], mean[:, bass.ds(t, 1)],
                                            rstd[:, bass.ds(t, 1)], ALU.subtract, ALU.mult).then_inc(z_ready, 1)

                def self_logits(t, s):
                    dve.wait_ge(xr_ready, t + 1)
                    nc.vector.tensor_tensor(f_sb[:, s, :], xr_ps[:, s, 0:D], xl_sb[:, s, 0:D], ALU.add).then_inc(f_ready, 1)
                    nc.vector.tensor_tensor(lin[:, s, :], xr_ps[:, s, D:D + H], xl_sb[:, s, D:D + H],
                                            ALU.add).then_inc(lin_ready, 1)
                    dve.wait_ge(f_ready, t + 1)
                    nc.vector.scalar_tensor_tensor(g_sb[:, s, :], f_sb[:, s, :], 0.0, k.att_pos[:, :], ALU.max,
                                                   ALU.mult).then_inc(g_ready, 1)
                    dve.wait_ge(g_ready, t + 1)
                    nc.vector.tensor_reduce(red[:, s, :], g_sb[:, s, :].rearrange("p (h c) -> p h c", c=C), AX.X,
                                            ALU.add).then_inc(red_ready, 1)
                    dve.wait_ge(red_ready, t + 1)
                    dve.wait_ge(lin_ready, t + 1)
                    if not isinstance(t, int) or t >= 2:
                        dve.wait_ge(stored[s], (t - s) * 16)
                    nc.vector.tensor_tensor(xr_sb[:, s, D + H:XW], red[:, s, :], lin[:, s, :], ALU.add).then_inc(xr_full, 1)

                normalise(0, 0)
                normalise(1, 1)

                def both(t, s):
                    normalise(t + 2, s)
                    self_logits(t, s)

                dve.wait_ge(w_ready, 1)
                tiles(dve, NTP - 2, 2, 2, both)
                for t in range(NTP - 2, NTP):
                    self_logits(t, t % 2)

            @block.scalar
            def _(act):
                give_root(nc, k, act, tmp[:, 1, :], tmp[:, 0, :])

                def take_zt(t, s):
                    act.wait_ge(zt_done, t + 1)
                    wait_past(act, mm_done, t - 1)
                    nc.scalar.copy(zt_sb[:, s], zt_ps[:, s, 0:D].rearrange("p (h n) -> p h n", h=2)).then_inc(zt_taken, 1)

                def take_x(t, s):
                    act.wait_ge(mm_done, t + 1)
                    if not isinstance(t, int) or t >= 2:
                        act.wait_ge(stored[s], (t - s) * 16)
                    nc.scalar.copy(xl_sb[:, s, :], xl_ps[:, s, 0:XW]).then_inc(xl_ready, 1)
                    nc.scalar.copy(xr_sb[:, s, 0:D + H], xr_ps[:, s, 0:D + H]).then_inc(xr_ready, 1)

                take_zt(0, 0)

                def both(t, s):
                    take_zt(t + 1, 1 - s)
                    take_x(t, s)

                tiles(act, NTP - 2, 2, 2, both)
                both(NTP - 2, 0)
                take_x(NTP - 1, 1)

            @block.tensor
            def _(pe):
                def turn(t, s):
                    pe.wait_ge(z_ready, t + 1)
                    wait_past(pe, zt_taken, t - 1)
                    for h in range(2):
                        last = nc.tensor.transpose(zt_ps[:, s, h * P:(h + 1) * P], z_sb[:, s, h * P:(h + 1) * P],
                                                   k.ident[:, :])
                    last.then_inc(zt_done, 1)

                def project(t, s):
                    pe.wait_ge(zt_taken, t + 1)
                    wait_past(pe, xr_ready, t - 1)
                    wait_past(pe, lin_ready, t - 1)
                    for a, out in enumerate((xl_ps, xr_ps)):
                        for h in range(2):
                            last = nc.tensor.matmul(out[:, s, 0:XW], zt_sb[:, s, h, :], w_ext[:, a, h, :],
                                                    start=(h == 0), stop=(h == 1))
                    last.then_inc(mm_done, 1)

                pe.wait_ge(w_ready, 1)
                turn(0, 0)

                def both(t, s):
                    turn(t + 1, 1 - s)
                    project(t, s)

                tiles(pe, NTP - 2, 2, 2, both)
                both(NTP - 2, 0)
                project(NTP - 1, 1)


def load_bases(nc, k, engine, at, n):
    return nc.values_load_multi_w_load_instructions(k.bases[:, bass.ds(at, n)], engines=[engine], min_val=0, max_val=N)[1]


def attend(nc, k):
    QT = 4
    QUADS = T // QT
    PAIRS = T // 2
    LAG = 4
    LEAD = QUADS - LAG
    AHEAD = 6
    SOFT = 22
    EX = 2 * P
    assert NCH % 2 == 0
    with ExitStack() as ctx:
        sb = lambda name, shape, dt=F32: ctx.enter_context(nc.sbuf_tensor(name, shape, dt))
        pb = lambda name, shape: ctx.enter_context(nc.psum_tensor(name, shape, F32))
        sem = lambda name: ctx.enter_context(nc.semaphore(name))
        idx = sb("a_idx", [P, QUADS, QT], I32)
        xl_e = sb("a_xl_e", [P, 2 * T, XW])
        xr_w = sb("a_xr_w", [P, 2, QT, XW])
        rel_bc = sb("a_rel_bc", [P, 2, QT, P], BF16)
        far = sb("a_far", [P, QT, P])
        hot_n = sb("a_hot_n", [P, 2, QT, P])
        hot_e = sb("a_hot_e", [P, 2, QT, P])
        pos = sb("a_pos", [P, 2, D])
        red = sb("a_red", [P, 2, 2 * H])
        lg = sb("a_lg", [P, 2, 2, H, T])
        msg = sb("a_msg", [P, QT, D])
        exs = sb("a_exs", [P, 2, T, 2 * H])
        rel_r = sb("a_rel_r", [P, NCH, P], BF16)
        fresh = sb("a_fresh", [P, NCH])
        cut = sb("a_cut", [P, P + 1], BF16)
        lgr = sb("a_lgr", [P, 2, P])
        run = sb("a_run", [P, P])
        top = sb("a_top", [P, P])
        peak = sb("a_peak", [P, P])
        side = sb("a_side", [P, 2, P])
        begin = run
        expo = sb("a_expo", [P, 2, P])
        gate = sb("a_gate", [1, 2, GATES], BF16)
        carry = sb("a_carry", [1, H])
        into = sb("a_into", [1, H, T + 1])
        reach = sb("a_reach", [1, H, T + 1])
        reach_t = sb("a_reach_t", [1, H, T])
        back = sb("a_back", [1, H, T])
        reach_b = sb("a_reach_b", [1, H, T])
        fade = sb("a_fade", [1, H])
        faded = sb("a_faded", [1, H])
        f_ps = pb("a_f_ps", [P, 2, 2, 512])
        o_ps = pb("a_o_ps", [P, 2, 512])
        sm_ps = pb("a_sm_ps", [P, 2, 512])

        fixed, bases_in, masks, may_gather = sem("a_fixed"), sem("a_bases_in"), sem("a_masks"), sem("a_may_gather")
        idx_ready, far_n, hot_n_ready, far_e, hot_e_ready = (sem("a_idx_s"), sem("a_far_n"), sem("a_hot_n_s"),
                                                             sem("a_far_e"), sem("a_hot_e_s"))
        xl_in = [sem(f"a_xl_in{q}") for q in range(2 * QUADS)]
        xr_in = [sem(f"a_xr_in{q}") for q in range(2)]
        rel_in = [sem(f"a_rel_in{q}") for q in range(2)]
        gate_in = [sem(f"a_gate_in{q}") for q in range(2)]
        f_done, pos_ready, red_ready, lg_ready = sem("a_f_s"), sem("a_pos_s"), sem("a_red_s"), sem("a_lg_s")
        rows_done, rows_taken, soft, ends_done = sem("a_rows"), sem("a_rows_taken"), sem("a_soft"), sem("a_ends")
        reach_done, peak_done, expo_ready, faded_ready = sem("a_reach_c"), sem("a_peak_s"), sem("a_expo_s"), sem("a_faded_s")
        turned, exs_ready, msg_ready, sum_done, added = (sem("a_turned"), sem("a_exs_s"), sem("a_msg_s"), sem("a_sum_s"),
                                                         sem("a_added"))

        def steps(engine, step):
            late = [(2, QUADS - LAG + j) for j in range(LAG)]
            soon = [(1, j) for j in range(QUADS - LAG)]
            step(0, 0, True, [None] * QUADS)
            step(1, 1, True, [None] * LAG + soon)
            with engine.Fori(0, NCH // 2 - 2) as r:
                step(r * 2 + 2, 0, True, late + soon)
                step(r * 2 + 3, 1, True, late + soon)
            step(NCH - 2, 0, True, late + soon)
            step(NCH - 1, 1, True, late + soon)
            step(NCH, 0, False, late + soon)
            step(NCH + 1, 1, False, late)

        def softmax_in(c):
            return not isinstance(c, int) or 1 <= c <= NCH

        with nc.Block() as block:

            @block.gpsimd
            def _(pool):
                def gather(c, p, j):
                    pool.wait_ge(idx_ready, c * QUADS + (j + 1))
                    pool.sem_inc(may_gather, 1)
                    for u in range(QT):
                        nc.gpsimd.indirect_dma_start(
                            xl_e[:, p * T + j * QT + u, :], None, k.xl_rows,
                            bass.IndirectOffsetOnAxis(ap=idx[:, j, u:u + 1], axis=0)
                        ).then_inc(xl_in[p * QUADS + j], 16)

                def messages(cc, pp, jj):
                    pool.wait_ge(exs_ready, cc + 1)
                    for g in range(2):
                        t = jj * QT + 2 * g
                        wait_past(pool, sum_done, cc * T + (t - 2))
                        nc.gpsimd.tensor_tensor(
                            msg[:, 2 * g:2 * g + 2, :].rearrange("p t (h c) -> p t h c", c=C),
                            xl_e[:, pp * T + t:pp * T + t + 2, 0:D].rearrange("p t (h c) -> p t h c", c=C),
                            exs[:, pp, t:t + 2, 0:H][:, :, :, None].to_broadcast([P, 2, H, C]),
                            ALU.mult).then_inc(msg_ready, 1)

                def step(c, p, logits, sums):
                    for j in range(QUADS):
                        if sums[j:j + 1] and sums[j]:
                            b, jj = sums[j]
                            messages(c - b, (p + b) % 2, jj)
                        more = j + LEAD >= QUADS
                        at = c + more
                        if logits and not (isinstance(at, int) and at >= NCH):
                            wait_past(pool, msg_ready, c * PAIRS + (2 * (j + LEAD + 1) - 2 * PAIRS))
                            gather(at, (p + more) % 2, (j + LEAD) % QUADS)

                for j in range(LEAD):
                    gather(0, 0, j)
                steps(pool, step)

            @block.sync
            def _(sp):
                with nc.allow_non_contiguous_dma(reason="one number of each tile"):
                    sp.dma_start(k.bases[:, :], k.base_rows[:, 0:ETL]).then_inc(bases_in, 16)
                    for h in range(H):
                        sp.dma_start(rel_r[h * T:(h + 1) * T], k.rel_rows[0:ETL * P].rearrange(
                            "(c t e) -> t c e", t=T, e=P)).then_inc(fixed, 16)
                        sp.dma_start(fresh[h * T:(h + 1) * T], k.go_on_rows.rearrange("c t -> t c")).then_inc(fixed, 16)

                def loads(c, p):
                    if not isinstance(c, int) or c >= 2:
                        sp.wait_ge(soft, (c - 1) * SOFT)
                    sp.dma_start(gate[:, p], k.gate_rows[bass.ds(c, 1), :]).then_inc(gate_in[p], 16)
                    for j in range(QUADS):
                        at = c * T + j * QT
                        if j % 2 == 0:
                            bases = load_bases(nc, k, mybir.EngineType.SP, at, 2 * QT)
                        wait_past(sp, far_n, c * QUADS + (j - 1))
                        sp.dma_start(rel_bc[:, j % 2].rearrange("p t e -> p (t e)"),
                                     k.rel_rows[bass.ds(at * P, QT * P)].partition_broadcast(P)).then_inc(rel_in[j % 2], 16)
                        wait_past(sp, f_done, c * PAIRS + (2 * (j - 1)))
                        for u in range(QT):
                            sp.dma_start(xr_w[:, j % 2, u, :], k.xr_rows[bass.ds(bases[j % 2 * QT + u], P), :]).then_inc(xr_in[j % 2], 16)

                sp.wait_ge(bases_in, 16)
                loads(0, 0)
                loads(1, 1)
                with sp.Fori(0, NCH // 2 - 1) as r:
                    loads(r * 2 + 2, 0)
                    loads(r * 2 + 3, 1)

            @block.scalar
            def _(act):
                def indices(q, slot):
                    nc.scalar.copy(idx[:, slot, :], k.src_e[:, bass.ds(q * QT, QT)]).then_inc(idx_ready, 1)

                for q in range(AHEAD):
                    indices(q, q)

                def hot_nodes(c, j):
                    quad = c * QUADS + j
                    act.wait_ge(rel_in[j % 2], c * (8 * QUADS) + (j // 2 + 1) * 16)
                    nc.scalar.activation(far[:, :, :], rel_bc[:, j % 2], ACT.Abs, bias=k.neg_col[:, 0:1]).then_inc(far_n, 1)
                    act.wait_ge(far_n, quad + 1)
                    wait_past(act, f_done, c * PAIRS + 2 * (j - 1))
                    nc.scalar.activation(hot_n[:, j % 2], far[:, :, :], ACT.Relu, scale=-1.0,
                                         bias=k.one[:, 0:1]).then_inc(hot_n_ready, 1)
                    act.wait_ge(hot_n_ready, quad + 1)

                def hot_edges(c, j):
                    for u in range(QT):
                        nc.scalar.activation(far[:, u, :], k.iota_row[:, :], ACT.Abs,
                                             bias=k.neg_rel[:, bass.ds(c * T + (j * QT + u), 1)]).then_inc(far_e, 1)
                    act.wait_ge(far_e, c * T + (j + 1) * QT)
                    wait_past(act, sum_done, c * T + (j - 1) * QT)
                    nc.scalar.activation(hot_e[:, j % 2], far[:, :, :], ACT.Relu, scale=-1.0,
                                         bias=k.one[:, 0:1]).then_inc(hot_e_ready, 1)
                    act.wait_ge(hot_e_ready, c * QUADS + (j + 1))

                def step(c, p, logits, sums):
                    for j in range(QUADS):
                        quad = c * QUADS + j
                        if logits:
                            if not isinstance(c, int) or c * QUADS + j >= 2:
                                cc, pp, jj = (c, p, j - 2) if j >= 2 else (c - 1, 1 - p, j - 2 + QUADS)
                                act.wait_ge(xl_in[pp * QUADS + jj], (cc - pp) * (8 * QT) + 16 * QT)
                            indices(quad + AHEAD, (j + AHEAD) % QUADS)
                        following = c + (j + 1 == QUADS)
                        if logits and not (isinstance(following, int) and following >= NCH):
                            hot_nodes(following, (j + 1) % QUADS)
                        back = following - (2 if (j + 1) % QUADS < LAG else 1)
                        if not isinstance(back, int) or 0 <= back < NCH:
                            hot_edges(back, (j + 1 - LAG) % QUADS)
                        if not softmax_in(c):
                            continue
                        if j == 0:
                            act.wait_ge(rows_done, c)
                            nc.scalar.copy(lgr[:, :, :], sm_ps[:, 1 - p, 0:EX].rearrange("p (a e) -> p a e", a=2)
                                           ).then_inc(rows_taken, 1)
                        if j == 2:
                            act.wait_ge(soft, (c - 1) * SOFT + 19)
                            nc.scalar.activation(expo[:, :, :], lgr[:, :, :], ACT.Exp).then_inc(expo_ready, 1)
                        if j == 3:
                            act.wait_ge(soft, (c - 1) * SOFT + 20)
                            nc.scalar.activation(faded[:, :], fade[:, :], ACT.Exp).then_inc(faded_ready, 1)
                            act.wait_ge(turned, c)
                            wait_past(act, sum_done, (c - 2) * T + 1)
                            nc.scalar.copy(exs[:, 1 - p].rearrange("p t k -> p k t"),
                                           sm_ps[:, 1 - p, EX:EX + 2 * P].rearrange("p (k t) -> p k t", t=T)
                                           ).then_inc(exs_ready, 1)

                hot_nodes(0, 0)
                steps(act, step)

            @block.vector
            def _(dve):
                dve.wait_ge(fixed, 32 * H)
                nc.vector.memset(cut[:, 0:1], -NEG)
                nc.vector.memset(cut[:, P:P + 1], -NEG)
                nc.vector.memset(red[:, :, :], 0.0)
                nc.vector.memset(carry[:, :], -NEG)
                nc.vector.memset(back[:, :, :], -NEG)
                nc.vector.memset(o_ps[:, :, :], 0.0)
                nc.vector.tensor_scalar(fresh[:, :], fresh[:, :], -1.0, 1.0, ALU.mult, ALU.add).then_inc(masks, 1)
                dve.wait_ge(masks, 1)

                att = k.att_pos[:, None, :].to_broadcast([P, 2, D])

                def logits_of(c, p, j, g, between):
                    n = c * PAIRS + (2 * j + g + 1)
                    at = slice(j * QT + 2 * g, j * QT + 2 * g + 2)
                    dve.wait_ge(f_done, n)
                    nc.vector.scalar_tensor_tensor(pos[:, :, :], f_ps[:, g, :, 0:D], 0.0, att, ALU.max,
                                                   ALU.mult).then_inc(pos_ready, 1)
                    between(0)
                    dve.wait_ge(pos_ready, n)
                    nc.vector.tensor_reduce(red[:, :, 0:H], pos[:, :, :].rearrange("p t (h c) -> p t h c", c=C), AX.X,
                                            ALU.add).then_inc(red_ready, 1)
                    between(1)
                    dve.wait_ge(red_ready, n)
                    nc.vector.tensor_tensor(lg[:, p, :, :, at].rearrange("p a h t -> p t (a h)"), red[:, :, :],
                                            f_ps[:, g, :, D:XW], ALU.add).then_inc(lg_ready, 1)

                def add_up(cc, jj, u, base):
                    n = cc * T + (jj * QT + u)
                    dve.wait_ge(sum_done, n + 1)
                    if jj == 0 and u == 0:
                        dve.wait_ge(soft, (cc + 1) * SOFT)
                    wait_past(dve, added, n)
                    window = k.acc[:, :, bass.ds(base, P)]
                    nc.vector.tensor_tensor(window, o_ps[:, u % 2, 0:3 * P].rearrange("p (b n) -> p b n", b=3), window,
                                            ALU.add).then_inc(added, 1)

                def softmax(cc, pp, part, node=None):
                    did = cc * SOFT

                    def done(i, ins):
                        ins.then_inc(soft, 1)

                    def after(i):
                        wait_past(dve, soft, did + i)

                    g_in, g_pass, b_in, b_pass = gate_views(gate[:, pp])
                    rel = rel_r[:, bass.ds(cc, 1), :].rearrange("p o e -> p (o e)")
                    if part == 0:
                        done(1, nc.vector.tensor_tensor(cut[:, 1:P], rel[:, 1:P], rel[:, 0:P - 1], ALU.not_equal))
                        after(1)
                        done(2, nc.vector.tensor_scalar(cut[:, 1:P], cut[:, 1:P], -NEG, None, ALU.mult))
                        done(3, nc.vector.tensor_scalar(side[:, 0], rel, rel[:, 0:1], -NEG, ALU.not_equal, ALU.mult))
                        done(4, nc.vector.tensor_scalar(side[:, 1], rel, rel[:, P - 1:P], -NEG, ALU.not_equal, ALU.mult))
                        dve.wait_ge(rows_taken, cc + 1)
                        done(5, nc.vector.tensor_tensor(peak[:, :], lgr[:, 0], lgr[:, 1], ALU.max))
                        after(5)
                        done(6, nc.vector.tensor_tensor_scan(run[:, :], cut[:, 0:P], peak[:, :], -NEG, ALU.add, ALU.max))
                        after(6)
                        done(7, nc.vector.tensor_tensor_scan(top[:, ::-1], cut[:, P:0:-1], run[:, ::-1], -NEG, ALU.add,
                                                             ALU.max))
                        after(7)
                        done(8, nc.vector.tensor_scalar(begin[:, :], cut[:, 0:P], -1.0 / NEG, None, ALU.mult))
                        after(8)
                        done(9, nc.vector.tensor_copy(begin[:, 0:1], fresh[:, bass.ds(cc, 1)]))
                    if part == 1:
                        dve.wait_ge(ends_done, cc + 1)
                        dve.wait_ge(gate_in[pp], (cc - pp) * 8 + 16)
                        ends = sm_ps[0:1, pp, 0:EX].rearrange("p (a h t) -> p a h t", a=2, t=T)
                        done(10, nc.vector.tensor_tensor(into[:, :, 1:T + 1], ends[:, 1], g_in[:, :, 1:T + 1], ALU.add))
                        after(10)
                        done(11, nc.vector.tensor_tensor(into[:, :, 0], carry[:, :], g_in[:, :, 0], ALU.add))
                        done(12, nc.vector.tensor_tensor(back[:, :, 0:T - 1], ends[:, 0, :, 1:T], b_in[:, :, 0:T - 1],
                                                         ALU.add))
                        after(12)
                        flat = lambda a: a.rearrange("p h t -> p (h t)")
                        done(13, nc.vector.tensor_tensor_scan(flat(reach[:, :, :]), flat(g_pass), flat(into[:, :, :]),
                                                              -NEG, ALU.add, ALU.max))
                        done(14, nc.vector.tensor_tensor_scan(flat(reach_b[:, :, :])[:, ::-1], flat(b_pass)[:, ::-1],
                                                              flat(back[:, :, :])[:, ::-1], -NEG, ALU.add, ALU.max))
                        after(14)
                        done(15, nc.vector.tensor_copy(reach_t[:, :, :], reach[:, :, 0:T]))
                        done(16, nc.vector.tensor_copy(carry[:, :], reach[:, :, T]))
                    if part == 2:
                        dve.wait_ge(reach_done, cc + 1)
                        done(17, nc.vector.scalar_tensor_tensor(peak[:, :], side[:, 0], sm_ps[:, pp, 0:1], top[:, :],
                                                                ALU.add, ALU.max))
                        after(17)
                        done(18, nc.vector.scalar_tensor_tensor(peak[:, :], side[:, 1], sm_ps[:, pp, 1:2], peak[:, :],
                                                                ALU.add, ALU.max))
                        after(18)
                        done(19, nc.vector.tensor_tensor(lgr[:, :, :], lgr[:, :, :],
                                                         peak[:, None, :].to_broadcast([P, 2, P]), ALU.subtract))
                    if part == 3:
                        dve.wait_ge(peak_done, cc + 1)
                        first = sm_ps[0:1, pp, P:2 * P].rearrange("p (h t) -> p h t", t=T)[:, :, 0]
                        done(20, nc.vector.tensor_tensor(fade[:, :], into[:, :, 0], first, ALU.subtract))
                        dve.wait_ge(expo_ready, cc + 1)
                        done(21, nc.vector.tensor_tensor(expo[:, 1], expo[:, 1], begin[:, :], ALU.mult))
                    if part == 4:
                        dve.wait_ge(exs_ready, cc + 1)
                        wait_past(dve, added, cc * T)
                        column = k.acc[:, :, bass.ds(node, 1)]
                        done(22, nc.vector.tensor_tensor(column, column, sm_ps[:, pp, 2:5][:, :, None], ALU.mult))

                def step(c, p, logits, sums):
                    def soften(parts, j):
                        if softmax_in(c) and j in parts:
                            softmax(c - 1, 1 - p, parts[j])

                    for j in range(QUADS):
                        b, jj = sums[j] if sums[j:j + 1] and sums[j] else (0, 0)
                        if b:
                            bases = load_bases(nc, k, mybir.EngineType.DVE, (c - b) * T + jj * QT, QT)
                        if j == LAG and softmax_in(c):
                            softmax(c - 1, 1 - p, 4, bases[0])
                        soften({1: 0, 2: 1, 3: 3}, j)
                        for g in range(2):
                            def between(u):
                                if b:
                                    add_up(c - b, jj, 2 * g + u, bases[2 * g + u])

                            if logits:
                                logits_of(c, p, j, g, between)
                            else:
                                between(0)
                                between(1)
                            if g == 0:
                                soften({2: 2}, j)

                steps(dve, step)

            @block.tensor
            def _(pe):
                def logits_of(c, p, j, g):
                    if g == 0:
                        pe.wait_ge(hot_n_ready, c * QUADS + (j + 1))
                        pe.wait_ge(xr_in[j % 2], c * (QUADS * 8 * QT) + (j // 2 + 1) * (16 * QT))
                        pe.wait_ge(xl_in[p * QUADS + j], (c - p) * (8 * QT) + 16 * QT)
                    wait_past(pe, lg_ready, c * PAIRS + (2 * j + g - 1))
                    for u in range(2 * g, 2 * g + 2):
                        out = f_ps[:, g, u % 2, 0:XW]
                        nc.tensor.matmul(out, hot_n[:, j % 2, u, :], xr_w[:, j % 2, u, :], start=True, stop=False)
                        last = nc.tensor.matmul(out, k.ident[:, :], xl_e[:, p * T + j * QT + u, :], start=False, stop=True)
                    last.then_inc(f_done, 1)

                def sums_of(cc, pp, jj, g):
                    if g == 0:
                        pe.wait_ge(hot_e_ready, cc * QUADS + (jj + 1))
                    pe.wait_ge(msg_ready, cc * PAIRS + (2 * jj + g + 1))
                    for u in range(2 * g, 2 * g + 2):
                        t = jj * QT + u
                        wait_past(pe, added, cc * T + (t - 1))
                        one_hot = hot_e[:, jj % 2, u, :]
                        for h in range(2):
                            nc.tensor.matmul(o_ps[:, u % 2, h * P:(h + 1) * P], msg[:, u, h * P:(h + 1) * P], one_hot,
                                             start=True, stop=True)
                        nc.tensor.matmul(o_ps[0:2 * H, u % 2, 2 * P:3 * P], exs[:, pp, t, :], one_hot,
                                         start=True, stop=True).then_inc(sum_done, 1)

                def softmax(cc, pp, part):
                    did = cc * SOFT
                    sm = sm_ps[:, pp]
                    if part == 0:
                        pe.wait_ge(lg_ready, (cc + 1) * PAIRS)
                        for a in range(2):
                            last = nc.tensor.transpose(sm[:, a * P:(a + 1) * P], lg[:, pp, a].rearrange("p h t -> p (h t)"),
                                                       k.ident[:, :])
                        last.then_inc(rows_done, 1)
                    if part == 1:
                        pe.wait_ge(soft, did + 7)
                        nc.tensor.transpose(sm[0:1, 0:P], top[:, 0:1], k.ident[:, :])
                        nc.tensor.transpose(sm[0:1, P:2 * P], top[:, P - 1:P], k.ident[:, :]).then_inc(ends_done, 1)
                    if part == 2:
                        pe.wait_ge(soft, did + 15)
                        nc.tensor.matmul(sm[:, 0:1], reach_t[:, :, :].rearrange("p h t -> p (h t)"), k.one[0:1, 0:1], start=True, stop=True)
                        nc.tensor.matmul(sm[:, 1:2], reach_b[:, :, :].rearrange("p h t -> p (h t)"), k.one[0:1, 0:1], start=True,
                                         stop=True).then_inc(reach_done, 1)
                    if part == 3:
                        pe.wait_ge(soft, did + 18)
                        nc.tensor.transpose(sm[0:1, P:2 * P], peak[:, 0:1], k.ident[:, :]).then_inc(peak_done, 1)
                    if part == 4:
                        pe.wait_ge(soft, did + 21)
                        for a in range(2):
                            nc.tensor.transpose(sm[:, EX + a * P:EX + (a + 1) * P], expo[:, a], k.ident[:, :])
                        pe.wait_ge(faded_ready, cc + 1)
                        for b, heads in enumerate(((0, 1), (2, 3), range(H))):
                            for h in heads:
                                last = nc.tensor.matmul(sm[:, 2 + b:3 + b], k.head_rows[:, h if b == 2 else H + h % 2, :],
                                                        faded[0:1, h:h + 1], start=(h == heads[0]), stop=(h == heads[-1]))
                        last.then_inc(turned, 1)

                def step(c, p, logits, sums):
                    def soften(parts, j):
                        if softmax_in(c) and j in parts:
                            softmax(c - 1, 1 - p, parts[j])

                    for j in range(QUADS):
                        b, jj = sums[j] if sums[j:j + 1] and sums[j] else (0, 0)
                        for g in range(2):
                            if logits:
                                logits_of(c, p, j, g)
                            soften(({2: 2}, {0: 0, 1: 1, 2: 3, 3: 4})[g], j)
                            if b:
                                sums_of(c - b, (p + b) % 2, jj, g)

                pe.wait_ge(masks, 1)
                steps(pe, step)


def batch_scale(nc, link, stats, par, scale, tmp, root):
    for h in range(DH):
        link(nc.vector.bn_aggr(tmp[:, h, 0:2], stats[:, h]))
    link(nc.vector.tensor_copy(tmp[:, :, 2], tmp[:, :, 1]))
    root(tmp[:, :, 2])
    inverse_root(nc, link, tmp[:, :, 1], tmp[:, :, 2], tmp[:, :, 3])
    link(nc.vector.tensor_tensor(scale[:, 0], par[:, 0], tmp[:, :, 1], ALU.mult))
    link(nc.vector.tensor_tensor(tmp[:, :, 0], tmp[:, :, 0], scale[:, 0], ALU.mult))
    link(nc.vector.tensor_tensor(scale[:, 1], par[:, 1], tmp[:, :, 0], ALU.subtract))


def join_heads(nc, k):
    with ExitStack() as ctx:
        sb = lambda name, shape, dt=F32: ctx.enter_context(nc.sbuf_tensor(name, shape, dt))
        pb = lambda name, shape: ctx.enter_context(nc.psum_tensor(name, shape, F32))
        sem = lambda name: ctx.enter_context(nc.semaphore(name))
        par = sb("j_par", [P, 2, DH])
        bias = sb("j_bias", [P, DH])
        heads = sb("j_heads", [P, 2, W])
        over = sb("j_over", [R, TILES, H])
        share = sb("j_share", [R, TILES, H])
        over_f = sb("j_over_f", [R, 2, 2, D])
        xl = sb("j_xl", [R, 2, 2, D])
        z = sb("j_z", [R, 2, 2, D])
        own = sb("j_own", [R, 2, 2, D])
        stats = sb("j_stats", [P, DH, CHUNKS, 6])
        tmp = sb("j_tmp", [P, DH, 4])
        sums_ps = pb("j_sums_ps", [R, TILES, 2 * H])
        over_ps = pb("j_over_ps", [P, 2, 2, 256])
        own_ps = pb("j_own_ps", [P, 2, 2, 256])
        par_in = sem("j_par_in")
        heads_ready, heads_turned, share_ready = sem("j_heads_s"), sem("j_heads_turned"), sem("j_share_s")
        xl_in = [sem("j_xl_in0"), sem("j_xl_in1")]
        z_in = [sem("j_z_in0"), sem("j_z_in1")]
        over_ready, own_scaled, own_ready, turned, did = (sem("j_over_s"), sem("j_own_scaled"), sem("j_own_s"),
                                                          sem("j_turned"), sem("j_did"))
        STEPS = 5

        with nc.Block() as block:

            @block.sync
            def _(sp):
                with nc.allow_non_contiguous_dma(reason="one number of each feature"):
                    for i, v in enumerate((k.gamma1, k.beta1)):
                        sp.dma_start(par[:, i], v.rearrange("(h p) -> p h", p=P)).then_inc(par_in, 16)
                    sp.dma_start(bias[:, :], k.bias.rearrange("(h p) -> p h", p=P)).then_inc(par_in, 16)

                def load(c, s):
                    wait_past(sp, own_ready, c - 1)
                    sp.dma_start(xl[:, s], k.xl_rows[bass.ds(c * W, W), 0:D].rearrange("(u p) d -> p u d", p=R)
                                 ).then_inc(xl_in[s], 16)
                    sp.dma_start(z[:, s], k.z_rows[bass.ds(c * W, W), :].rearrange("(u p) d -> p u d", p=R)
                                 ).then_inc(z_in[s], 16)

                tiles(sp, CHUNKS, 2, 2, load)

            @block.gpsimd
            def _(pool):
                pool.wait_ge(share_ready, 1)

                def own_messages(c, s):
                    pool.wait_ge(xl_in[s], (c - s) * 8 + 16)
                    wait_past(pool, turned, c - 1)
                    split_heads = lambda a: a.rearrange("p u (h c) -> p u h c", c=C)
                    nc.gpsimd.tensor_tensor(split_heads(own[:, s]), split_heads(xl[:, s]),
                                            share[:, bass.ds(c * 2, 2), :][:, :, :, None].to_broadcast([R, 2, H, C]),
                                            ALU.mult).then_inc(own_scaled, 1)
                    pool.wait_ge(z_in[s], (c - s) * 8 + 16)
                    pool.wait_ge(own_scaled, c + 1)
                    nc.gpsimd.tensor_tensor(own[:, s], own[:, s], z[:, s], ALU.add).then_inc(own_ready, 1)

                tiles(pool, CHUNKS, 2, 2, own_messages)

            @block.vector
            def _(dve):
                link = link_on(dve, k)
                dve.wait_ge(heads_turned, CHUNKS)
                link(nc.vector.tensor_copy(share[:, :, :], sums_ps[:, :, H:2 * H]))
                link(nc.vector.tensor_tensor(over[:, :, :], sums_ps[:, :, 0:H], share[:, :, :], ALU.add))
                link(nc.vector.tensor_scalar(over[:, :, :], over[:, :, :], SEG_EPS, None, ALU.add))
                link(nc.vector.reciprocal(over[:, :, :], over[:, :, :]))
                nc.vector.tensor_tensor(share[:, :, :], share[:, :, :], over[:, :, :], ALU.mult).then_inc(share_ready, 1)
                dve.wait_ge(par_in, 48)

                def join(c, s):
                    def step(i, ins):
                        ins.then_inc(did, 1)

                    acc = k.acc[:, 0:DH, bass.ds(c * W, W)]
                    half = lambda h: k.acc[:, h, bass.ds(c * W, W)]
                    dve.wait_ge(turned, c + 1)
                    step(1, nc.vector.tensor_tensor(acc, over_ps[:, s, :, 0:W], acc, ALU.mult))
                    dve.wait_ge(did, c * STEPS + 1)
                    for h in range(DH):
                        step(2 + h, nc.vector.scalar_tensor_tensor(half(h), own_ps[:, s, h, 0:W], bias[:, h:h + 1], half(h),
                                                                   ALU.add, ALU.add))
                    for h in range(DH):
                        dve.wait_ge(did, c * STEPS + (2 + h))
                        step(4 + h, nc.vector.bn_stats(stats[:, h, bass.ds(c, 1), :], half(h)))

                tiles(dve, CHUNKS, 2, 2, join)
                dve.wait_ge(did, CHUNKS * STEPS)

                root = lambda var: ask_root(nc, k, dve, var)
                batch_scale(nc, link, stats, par, k.norm1, tmp, root)

            @block.scalar
            def _(act):
                def take_heads(c, s):
                    wait_past(act, heads_turned, c - 1)
                    nc.scalar.copy(heads[:, s], k.acc[:, DH, bass.ds(c * W, W)]).then_inc(heads_ready, 1)

                tiles(act, CHUNKS, 2, 2, take_heads)
                act.wait_ge(share_ready, 1)

                def spread(c, s):
                    wait_past(act, turned, c - 1)
                    nc.scalar.copy(over_f[:, s].rearrange("p u (h c) -> p u h c", c=C),
                                   over[:, bass.ds(c * 2, 2), :][:, :, :, None].to_broadcast([R, 2, H, C])
                                   ).then_inc(over_ready, 1)

                tiles(act, CHUNKS, 2, 2, spread)
                give_root(nc, k, act, tmp[:, :, 3], tmp[:, :, 2])

            @block.tensor
            def _(pe):
                def turn_heads(c, s):
                    pe.wait_ge(heads_ready, c + 1)
                    for u in range(2):
                        last = nc.tensor.matmul(sums_ps[:, bass.ds(c * 2 + u, 1), :].rearrange("p o k -> p (o k)"),
                                                heads[:, s, u * R:(u + 1) * R], k.ident[:, 0:2 * H], start=True, stop=True)
                    last.then_inc(heads_turned, 1)

                tiles(pe, CHUNKS, 2, 2, turn_heads)

                def turn(c, s):
                    wait_past(pe, did, (c - 2) * STEPS + 3)
                    for rows, out, ready in ((over_f, over_ps, over_ready), (own, own_ps, own_ready)):
                        pe.wait_ge(ready, c + 1)
                        for h in range(DH):
                            for u in range(2):
                                last = nc.tensor.transpose(out[:, s, h, u * R:(u + 1) * R], rows[:, s, u, h * P:(h + 1) * P],
                                                           k.ident[0:R, 0:R])
                    last.then_inc(turned, 1)

                tiles(pe, CHUNKS, 2, 2, turn)


def feed_forward(nc, k):
    with ExitStack() as ctx:
        sb = lambda name, shape, dt=F32: ctx.enter_context(nc.sbuf_tensor(name, shape, dt))
        pb = lambda name, shape: ctx.enter_context(nc.psum_tensor(name, shape, F32))
        sem = lambda name: ctx.enter_context(nc.semaphore(name))
        w1 = sb("f_w1", [P, DH, D])
        w2 = sb("f_w2", [P, DH, D])
        b1 = sb("f_b1", [P, DH])
        b2 = sb("f_b2", [P, DH])
        par = sb("f_par", [P, 2, DH])
        hid = sb("f_hid", [P, 2, DH, W])
        stats = sb("f_stats", [P, DH, CHUNKS, 6])
        tmp = sb("f_tmp", [P, DH, 4])
        up_ps = pb("f_up_ps", [P, 2, 2, 256])
        down_ps = pb("f_down_ps", [P, 2, 2, 256])
        w_in = sem("f_w_in")
        normed, up_done, hid_ready, down_done, summed, measured = (sem("f_normed"), sem("f_up"), sem("f_hid_s"), sem("f_down"),
                                                                   sem("f_summed"), sem("f_measured"))

        with nc.Block() as block:

            @block.sync
            def _(sp):
                for w, v in ((w1, k.W1), (w2, k.W2)):
                    sp.dma_start(w[:, :, :], v.rearrange("(h p) n -> p h n", p=P)).then_inc(w_in, 16)
                with nc.allow_non_contiguous_dma(reason="one number of each feature"):
                    for out, v in ((b1[:, :], k.b1), (b2[:, :], k.b2), (par[:, 0], k.gamma2), (par[:, 1], k.beta2)):
                        sp.dma_start(out, v.rearrange("(h p) -> p h", p=P)).then_inc(w_in, 16)
                for e in range(E):
                    sp.dma_start(k.we1[:, e], k.We1[e].rearrange("(h p) n -> p h n", p=P)).then_inc(k.experts_in, 16)
                    sp.dma_start(k.we2[:, e], k.We2[e].rearrange("(h p) n -> p h n", p=P)).then_inc(k.experts_in, 16)

            @block.vector
            def _(dve):
                link = link_on(dve, k)
                dve.wait_ge(w_in, 96)

                def add(c, s):
                    dve.wait_ge(down_done, c + 1)
                    dve.wait_ge(normed, 2 * c + 2)
                    for h in range(DH):
                        at = k.acc[:, h, bass.ds(c * W, W)]
                        nc.vector.scalar_tensor_tensor(at, down_ps[:, s, h, 0:W], b2[:, h:h + 1], at, ALU.add,
                                                       ALU.add).then_inc(summed, 1)
                    for h in range(DH):
                        dve.wait_ge(summed, 2 * c + (h + 1))
                        nc.vector.bn_stats(stats[:, h, bass.ds(c, 1), :],
                                           k.acc[:, h, bass.ds(c * W, W)]).then_inc(measured, 1)

                tiles(dve, CHUNKS, 2, 2, add)
                dve.wait_ge(measured, 2 * CHUNKS)

                root = lambda var: ask_root(nc, k, dve, var)
                batch_scale(nc, link, stats, par, k.norm2, tmp, root)

            @block.scalar
            def _(act):
                act.wait_ge(w_in, 96)

                def norm(c, s):
                    for h in range(DH):
                        at = k.acc[:, h, bass.ds(c * W, W)]
                        nc.scalar.activation(at, at, ACT.Identity, scale=k.norm1[:, 0, h:h + 1],
                                             bias=k.norm1[:, 1, h:h + 1]).then_inc(normed, 1)

                def act_up(c, s):
                    act.wait_ge(up_done, c + 1)
                    wait_past(act, down_done, c - 1)
                    for h in range(DH):
                        nc.scalar.activation(hid[:, s, h], up_ps[:, s, h, 0:W], ACT.Relu,
                                             bias=b1[:, h:h + 1]).then_inc(hid_ready, 1)

                norm(0, 0)
                norm(1, 1)

                def both(c, s):
                    norm(c + 2, s)
                    act_up(c, s)

                tiles(act, CHUNKS - 2, 3, 2, both)
                for c in range(CHUNKS - 2, CHUNKS):
                    act_up(c, c % 2)
                give_root(nc, k, act, tmp[:, :, 3], tmp[:, :, 2])

            @block.tensor
            def _(pe):
                def up(c, s):
                    pe.wait_ge(normed, 2 * c + 2)
                    wait_past(pe, hid_ready, 2 * c - 2)
                    for o in range(DH):
                        for h in range(DH):
                            last = nc.tensor.matmul(up_ps[:, s, o, 0:W], w1[:, h, o * P:(o + 1) * P],
                                                    k.acc[:, h, bass.ds(c * W, W)], start=(h == 0), stop=(h == DH - 1))
                    last.then_inc(up_done, 1)

                def down(c, s):
                    pe.wait_ge(hid_ready, 2 * c + 2)
                    wait_past(pe, summed, 2 * c - 2)
                    for o in range(DH):
                        for h in range(DH):
                            last = nc.tensor.matmul(down_ps[:, s, o, 0:W], w2[:, h, o * P:(o + 1) * P], hid[:, s, h],
                                                    start=(h == 0), stop=(h == DH - 1))
                    last.then_inc(down_done, 1)

                pe.wait_ge(w_in, 96)
                up(0, 0)

                def both(c, s):
                    up(c + 1, 1 - s)
                    down(c, s)

                tiles(pe, CHUNKS - 1, 2, 2, both)
                down(CHUNKS - 1, (CHUNKS - 1) % 2)


def route_tokens(nc, k):
    G = 5
    GROUPS = TILES // G
    ROWS = G * K
    assert GROUPS % 2 == 0
    with ExitStack() as ctx:
        sb = lambda name, shape, dt=F32: ctx.enter_context(nc.sbuf_tensor(name, shape, dt))
        pb = lambda name, shape: ctx.enter_context(nc.psum_tensor(name, shape, F32))
        sem = lambda name: ctx.enter_context(nc.semaphore(name))
        space = [k.acc[:, DH, :], 0]

        def work(rows, shape):
            n = int(np.prod(shape))
            at = space[0][0:rows, space[1]:space[1] + n]
            space[1] += n
            names = "abcd"[:len(shape)]
            if len(shape) == 1:
                return at
            return at.rearrange(f"p ({' '.join(names)}) -> p {' '.join(names)}", **dict(zip(names[1:], shape[1:])))

        pad = space[0][:, 0:ZW]
        x_in_sb = work(R, (2, 2, D))
        z = work(R, (2, G, D))
        zr = work(R, (ROWS, ZW))
        y = sb("r_y", [P, 2, DH, W])
        zt = sb("r_zt", [P, 2, DH, R])
        wg = sb("r_wg", [P, DH, E])
        bg = sb("r_bg", [1, E])
        ones = sb("r_ones", [P, P])
        below = sb("r_below", [R, R])
        stats = sb("r_stats", [R, TILES, 6])
        mean = sb("r_mean", [R, TILES])
        rstd = sb("r_rstd", [R, TILES])
        tmp = sb("r_tmp", [R, 2, TILES])
        left = sb("r_left", [R, G, E])
        mark = sb("r_mark", [R, G, E])
        which = sb("r_which", [R, G, E])
        chosen = sb("r_chosen", [R, K, G, E])
        either = sb("r_either", [R, G, E])
        rank = sb("r_rank", [R, G, E])
        best = sb("r_best", [R, G])
        total = sb("r_total", [P, E, G])
        before = sb("r_before", [P, E, G])
        opened = sb("r_opened", [P, E, G])
        count = sb("r_count", [P, E])
        place = sb("r_place", [R, K, G])
        ids_i = sb("r_ids_i", [R, TILES, K], I32)
        ids = sb("r_ids", [R, TILES, K])
        idx = sb("r_idx", [R, ROWS], I32)
        expert = sb("r_expert", [P, E])
        region = sb("r_region", [P, E])
        pad_f = sb("r_pad_f", [P, E])
        pad_i = sb("r_pad_i", [P, E], I32)
        nt = sb("r_nt", [1, E])
        end = sb("r_end", [1, E])
        jump = sb("r_jump", [1, E])
        steps_of = sb("r_steps_of", [1, NT])
        past = sb("r_past", [1, SLOT_TILES, E])
        slot_f = sb("r_slot_f", [1, 2, SLOT_TILES])
        y_ps = pb("r_y_ps", [R, 2, 2, D])
        zt_ps = pb("r_zt_ps", [P, 2, DH, 256])
        score_ps = pb("r_score_ps", [R, 2, 512])
        rank_ps = pb("r_rank_ps", [P, 2, 256])

        w_in, iotas = sem("r_w_in"), sem("r_iotas")
        x_in = [sem("r_x_in0"), sem("r_x_in1")]
        y_ready, y_turned, summed, measured = sem("r_y_s"), sem("r_y_turned"), sem("r_summed"), sem("r_measured")
        z_ready, z_turned, z_taken, scored = sem("r_z_s"), sem("r_z_turned"), sem("r_z_taken"), sem("r_scored")
        masked, ranked, routed = sem("r_masked"), sem("r_ranked"), sem("r_routed")
        row_ready, may_scatter = sem("r_row_s"), sem("r_may")
        scattered = [sem(f"r_scattered{q}") for q in range(ROWS)]
        pads_ready, pads_stored, blank_stored = sem("r_pads"), sem("r_pads_stored"), sem("r_blank_stored")

        with nc.Block() as block:

            @block.sync
            def _(sp):
                sp.dma_start(wg[:, :, :], k.Wg.rearrange("(h p) e -> p h e", p=P)).then_inc(w_in, 16)
                sp.dma_start(bg[:, :], k.bg.rearrange("(o e) -> o e", o=1)).then_inc(w_in, 16)

                def load(c, s):
                    wait_past(sp, summed, c - 1)
                    sp.dma_start(x_in_sb[:, s], k.x[bass.ds(c * W, W), :].rearrange("(u p) d -> p u d", p=R)
                                 ).then_inc(x_in[s], 16)

                tiles(sp, CHUNKS, 2, 2, load)
                sp.wait_ge(y_turned, CHUNKS)
                for e in range(E):
                    sp.dma_start(k.be1_all[:, e], k.be1[e].partition_broadcast(P)).then_inc(k.bias_in, 16)
                    sp.dma_start(k.be2_all[:, e], k.be2[e].partition_broadcast(P)).then_inc(k.bias_in, 16)
                sp.wait_ge(pads_ready, 1)
                sp.dma_start(k.disp_rows[E * REGION:E * REGION + P, :], pad[:, :]).then_inc(blank_stored, 16)
                sp.wait_ge(blank_stored, 16)
                sp.wait_ge(pads_stored, 16 * E)

            @block.scalar
            def _(act):
                def norm(c, s):
                    wait_past(act, y_turned, c - 1)
                    for h in range(DH):
                        nc.scalar.activation(y[:, s, h], k.acc[:, h, bass.ds(c * W, W)], ACT.Identity,
                                             scale=k.norm2[:, 0, h:h + 1], bias=k.norm2[:, 1, h:h + 1]).then_inc(y_ready, 1)

                tiles(act, CHUNKS, 2, 2, norm)
                give_root(nc, k, act, tmp[:, 1, :], tmp[:, 0, :])

                def take(t, s):
                    act.wait_ge(z_turned, t + 1)
                    wait_past(act, scored, t - 1)
                    nc.scalar.copy(zt[:, s], zt_ps[:, s, :, 0:R]).then_inc(z_taken, 1)

                tiles(act, TILES, 2, 2, take)

            @block.tensor
            def _(pe):
                def turn_y(c, s):
                    pe.wait_ge(y_ready, 2 * c + 2)
                    wait_past(pe, summed, c - 1)
                    for u in range(2):
                        for h in range(DH):
                            last = nc.tensor.transpose(y_ps[:, s, u, h * P:(h + 1) * P], y[:, s, h, u * R:(u + 1) * R],
                                                       k.ident[:, :])
                    last.then_inc(y_turned, 1)

                tiles(pe, CHUNKS, 2, 2, turn_y)
                pe.wait_ge(w_in, 32)

                def turn_z(g, s, i):
                    t, q = g * G + i, (s * G + i) % 2
                    pe.wait_ge(z_ready, t + 1)
                    wait_past(pe, z_taken, t - 1)
                    for h in range(DH):
                        last = nc.tensor.transpose(zt_ps[:, q, h, 0:R], z[:, s, i, h * P:(h + 1) * P], k.ident[0:R, 0:R])
                    last.then_inc(z_turned, 1)

                def score_of(g, s, i):
                    t, q = g * G + i, (s * G + i) % 2
                    pe.wait_ge(z_taken, t + 1)
                    wait_past(pe, masked, g - 1)
                    out = score_ps[:, s, i * E:(i + 1) * E]
                    for h in range(DH):
                        nc.tensor.matmul(out, zt[:, q, h], wg[:, h, :], start=(h == 0), stop=False)
                    nc.tensor.matmul(out, ones[0:1, 0:R], bg[:, :], start=False, stop=True).then_inc(scored, 1)

                def scores(g, s):
                    turn_z(g, s, 0)
                    for i in range(G):
                        if i + 1 < G:
                            turn_z(g, s, i + 1)
                        score_of(g, s, i)

                def ranks(g):
                    pe.wait_ge(masked, g + 1)
                    flat = either[:, :, :].rearrange("p t e -> p (t e)")
                    nc.tensor.matmul(rank_ps[0:R, 0, 0:G * E], below[:, :], flat, start=True, stop=True)
                    nc.tensor.matmul(rank_ps[:, 1, 0:G * E], ones[0:R, :], flat, start=True, stop=True).then_inc(ranked, 1)

                scores(0, 0)
                scores(1, 1)
                ranks(0)

                def both(g, s):
                    scores(g + 2, s)
                    ranks(g + 1)

                tiles(pe, GROUPS - 2, 2, 2, both)
                ranks(GROUPS - 1)

            @block.vector
            def _(dve):
                link = link_on(dve, k)
                link(nc.vector.memset(ones[:, :], 1.0))
                nc.vector.tensor_scalar(below[:, :], k.iota_row[0:R, 0:R], k.iota_col[0:R, 0:1], None, ALU.is_gt)
                nc.vector.tensor_scalar(expert[:, :], k.iota_row[:, 0:E], float(-E), None, ALU.add)
                nc.vector.tensor_scalar(region[:, :], k.iota_row[:, 0:E], float(REGION), None, ALU.mult)
                nc.vector.tensor_scalar(steps_of[:, :], k.iota_row[0:1, 0:NT], float(P), None, ALU.mult)
                nc.vector.memset(opened[:, :, :], 1.0)
                link(nc.vector.memset(count[:, :], 0.0))
                link(nc.vector.memset(opened[:, :, 0:1], 0.0))
                dve.wait_ge(iotas, 1)
                link(nc.vector.tensor_copy(ids[:, :, :], ids_i[:, :, :]))

                def add(c, s):
                    dve.wait_ge(y_turned, c + 1)
                    dve.wait_ge(x_in[s], (c - s) * 8 + 16)
                    nc.vector.tensor_tensor(k.x1[:, bass.ds(c * 2, 2), :], y_ps[:, s], x_in_sb[:, s], ALU.add).then_inc(summed, 1)
                    dve.wait_ge(summed, c + 1)
                    for u in range(2):
                        nc.vector.bn_stats(stats[:, bass.ds(c * 2 + u, 1), :],
                                           k.x1[:, bass.ds(c * 2 + u, 1), :]).then_inc(measured, 1)

                tiles(dve, CHUNKS, 2, 2, add)
                dve.wait_ge(measured, TILES)
                nc.vector.memset(pad[:, 0:D], 0.0)
                nc.vector.memset(pad[:, D:ZW], float(NO_ROW))
                norm_scale(nc, link, stats, mean[:, :], rstd[:, :], tmp, lambda var: ask_root(nc, k, dve, var))

                def normalise(out, t):
                    return nc.vector.tensor_scalar(out, k.x1[:, bass.ds(t, 1), :].rearrange("p o d -> p (o d)"),
                                                   mean[:, bass.ds(t, 1)], rstd[:, bass.ds(t, 1)], ALU.subtract, ALU.mult)

                def norm(g, s):
                    wait_past(dve, z_turned, (g - 1) * G)
                    for i in range(G):
                        normalise(z[:, s, i], g * G + i).then_inc(z_ready, 1)

                STEPS = 22
                spread_e = lambda a: a[:, :, None].to_broadcast([R, G, E])
                experts = expert[0:R, None, :].to_broadcast([R, G, E])

                def step_of(g):
                    def step(i, ins):
                        ins.then_inc(routed, 1)
                        dve.wait_ge(routed, g * STEPS + i)

                    return step

                def choose(g, s):
                    step = step_of(g)
                    dve.wait_ge(scored, g * G + G)
                    score = score_ps[:, s, 0:G * E].rearrange("p (t e) -> p t e", e=E)
                    for i in range(K):
                        step(6 * i + 1, nc.vector.tensor_reduce(best[:, :], score, AX.X, ALU.max))
                        step(6 * i + 2, nc.vector.tensor_tensor(mark[:, :, :], score, spread_e(best), ALU.is_ge))
                        step(6 * i + 3, nc.vector.tensor_tensor(which[:, :, :], mark[:, :, :], experts, ALU.mult))
                        step(6 * i + 4, nc.vector.tensor_reduce(best[:, :], which[:, :, :], AX.X, ALU.min))
                        step(6 * i + 5, nc.vector.tensor_tensor(chosen[:, i], experts, spread_e(best), ALU.is_equal))
                        if i == 0:
                            step(6, nc.vector.scalar_tensor_tensor(left[:, :, :], chosen[:, 0], -NEG, score, ALU.mult, ALU.add))
                            score = left[:, :, :]
                    step(12, nc.vector.tensor_tensor(either[:, :, :], chosen[:, 0], chosen[:, 1], ALU.add))
                    nc.vector.memset(best[:, :], 0.0).then_inc(masked, 1)

                def places(g):
                    step = step_of(g)
                    dve.wait_ge(ranked, g + 1)
                    flat = lambda a: a[:, :, :].rearrange("p e t -> p (e t)")
                    tile_first = lambda a: a.rearrange("p (t e) -> p t e", e=E)
                    step(13, nc.vector.tensor_copy(total[:, :, :], rank_ps[:, 1, 0:G * E].rearrange("p (t e) -> p e t", e=E)))
                    step(14, nc.vector.tensor_tensor_scan(flat(before), flat(opened), flat(total), 0.0, ALU.mult, ALU.add))
                    step(15, nc.vector.tensor_tensor(total[:, :, :], before[:, :, :], total[:, :, :], ALU.subtract))
                    step(16, nc.vector.tensor_tensor(rank[:, :, :], tile_first(rank_ps[0:R, 0, 0:G * E]),
                                                     total[0:R].rearrange("p e t -> p t e"), ALU.add))
                    step(17, nc.vector.tensor_tensor(rank[:, :, :], rank[:, :, :],
                                                     region[0:R, None, :].to_broadcast([R, G, E]), ALU.add))
                    step(18, nc.vector.tensor_tensor(region[:, :], region[:, :], before[:, :, G - 1], ALU.add))
                    for i in range(K):
                        step(19 + 2 * i, nc.vector.tensor_tensor(which[:, :, :], rank[:, :, :], chosen[:, i], ALU.mult))
                        step(20 + 2 * i, nc.vector.tensor_reduce(place[:, i], which[:, :, :], AX.X, ALU.add))

                def rows(g, s):
                    for i in range(G):
                        for j in range(K):
                            q = i * K + j
                            wait_past(dve, scattered[q], g * 16)
                            normalise(zr[:, q, 0:D], g * G + i)
                            nc.vector.tensor_copy(zr[:, q, D:ZW], ids[:, bass.ds(g * G + i, 1), j])
                            nc.vector.tensor_copy(idx[:, q:q + 1], place[:, j, i:i + 1]).then_inc(row_ready, 1)

                def close():
                    nc.vector.tensor_scalar(pad_i[:, :], region[:, :], k.iota_col[:, 0:1], None, ALU.add).then_inc(pads_ready, 1)
                    link(nc.vector.scalar_tensor_tensor(count[:, :], k.iota_row[:, 0:E], float(-REGION), region[:, :], ALU.mult,
                                                        ALU.add))
                    link(nc.vector.tensor_tensor(past[:, 0:NT, :], count[0:1, None, :].to_broadcast([1, NT, E]),
                                                 steps_of[:, :, None].to_broadcast([1, NT, E]), ALU.is_gt))
                    link(nc.vector.tensor_reduce(nt[:, :], past[:, 0:NT, :].rearrange("p j e -> p e j"), AX.X, ALU.add))
                    link(nc.vector.tensor_tensor_scan(end[:, :], ones[0:1, 0:E], nt[:, :], 0.0, ALU.mult, ALU.add))
                    link(nc.vector.tensor_scalar(jump[:, :], nt[:, :], float(-P), float(REGION), ALU.mult, ALU.add))
                    slots = k.iota_row[0:1, 0:SLOT_TILES]
                    spread_s = lambda a: a[:, None, :].to_broadcast([1, SLOT_TILES, E])
                    link(nc.vector.tensor_tensor(past[:, :, :], slots[:, :, None].to_broadcast([1, SLOT_TILES, E]),
                                                 spread_s(end), ALU.is_ge))
                    link(nc.vector.tensor_reduce(slot_f[:, 1], past[:, :, :], AX.X, ALU.add))
                    link(nc.vector.tensor_tensor(past[:, :, :], past[:, :, :], spread_s(jump), ALU.mult))
                    link(nc.vector.tensor_reduce(slot_f[:, 0], past[:, :, :], AX.X, ALU.add))
                    link(nc.vector.scalar_tensor_tensor(slot_f[:, 0], slots, float(P), slot_f[:, 0], ALU.mult, ALU.add))
                    link(nc.vector.tensor_scalar(k.slots[:, 0], slot_f[:, 0], float(E * REGION), None, ALU.min))
                    link(nc.vector.tensor_scalar(k.slots[:, 1], slot_f[:, 1], float(E - 1), None, ALU.min))

                norm(0, 0)
                norm(1, 1)
                choose(0, 0)
                places(0)

                def group(g, s):
                    norm(g + 2, s)
                    choose(g + 1, 1 - s)
                    rows(g, s)
                    places(g + 1)

                tiles(dve, GROUPS - 2, 2, 2, group)
                choose(GROUPS - 1, 1)
                rows(GROUPS - 2, 0)
                places(GROUPS - 1)
                close()
                rows(GROUPS - 1, 1)

            @block.gpsimd
            def _(pool):
                nc.gpsimd.iota(ids_i[:, :, :], [[2 * R, TILES], [1, K]], base=0, channel_multiplier=K).then_inc(iotas, 1)

                def scatter(g, s):
                    for q in range(ROWS):
                        pool.wait_ge(row_ready, g * ROWS + (q + 1))
                        pool.sem_inc(may_scatter, 1)
                        nc.gpsimd.indirect_dma_start(k.disp_rows, bass.IndirectOffsetOnAxis(ap=idx[:, q:q + 1], axis=0),
                                                     zr[:, q, :], None).then_inc(scattered[q], 16)

                tiles(pool, GROUPS - 1, 2, 2, scatter)
                pool.wait_ge(pads_ready, 1)
                for e in range(E):
                    nc.gpsimd.indirect_dma_start(k.disp_rows, bass.IndirectOffsetOnAxis(ap=pad_i[:, e:e + 1], axis=0),
                                                 pad[:, :], None).then_inc(pads_stored, 16)
                scatter(GROUPS - 1, 1)
                for q in range(ROWS):
                    pool.wait_ge(scattered[q], 16 * GROUPS)


def apply_experts(nc, k):
    RING = 4
    with ExitStack() as ctx:
        pb = lambda name, shape: ctx.enter_context(nc.psum_tensor(name, shape, F32))
        sb = lambda name, shape, dt=F32: ctx.enter_context(nc.sbuf_tensor(name, shape, dt))
        sem = lambda name: ctx.enter_context(nc.semaphore(name))
        space = [k.acc[:, 0:DH, :].rearrange("p h n -> p (h n)"), 0]

        def work(shape):
            n = int(np.prod(shape))
            at = space[0][:, space[1]:space[1] + n]
            space[1] += n
            names = "abcd"[:len(shape)]
            return at.rearrange(f"p ({' '.join(names)}) -> p {' '.join(names)}", **dict(zip(names[1:], shape[1:])))

        space[1] = E * (HID + D)
        be1, be2 = k.be1_all, k.be2_all
        z = work((RING, ZW))
        zt = work((2, DH, P))
        hid = work((2, HID))
        hid_t = work((2, HC, P))
        y = work((RING, D))
        idx = sb("x_idx", [P, RING], I32)
        zt_ps = pb("x_zt_ps", [P, 2, 512])
        hid_ps = pb("x_hid_ps", [P, 2, HID])
        hid_t_ps = pb("x_hid_t_ps", [P, 2, HC, P])
        y_ps = pb("x_y_ps", [P, 2, 512])
        z_in = [sem(f"x_z_in{q}") for q in range(RING)]
        stored = [sem(f"x_stored{q}") for q in range(RING)]
        z_turned, zt_ready, up_done, hid_ready, gelu_done = sem("x_z_turned"), sem("x_zt"), sem("x_up"), sem("x_hid_s"), sem("x_gelu")
        hid_turned, hid_t_ready, down_done, y_ready, may_store = (sem("x_hid_turned"), sem("x_hid_t_s"), sem("x_down"), sem("x_y_s"),
                                                                  sem("x_may"))
        n_main = SLOT_TILES - 2

        with nc.Block() as block:

            @block.sync
            def _(sp):
                def load(s, q):
                    row = nc.values_load_multi_w_load_instructions(k.slots[:, 0, bass.ds(s, 1)], engines=[mybir.EngineType.SP],
                                                                   min_val=0, max_val=E * REGION)[1][0]
                    wait_past(sp, y_ready, s - (RING - 1))
                    sp.dma_start(z[:, q], k.disp_rows[bass.ds(row, P), :]).then_inc(z_in[q], 16)

                tiles(sp, SLOT_TILES, RING, RING, load)

            @block.gpsimd
            def _(pool):
                def store(s, q):
                    pool.wait_ge(y_ready, s + 1)
                    pool.sem_inc(may_store, 1)
                    nc.gpsimd.indirect_dma_start(k.moe_rows, bass.IndirectOffsetOnAxis(ap=idx[:, q:q + 1], axis=0), y[:, q],
                                                 None, bounds_check=K * N - 1, oob_is_err=False).then_inc(stored[q], 16)

                tiles(pool, SLOT_TILES, RING, RING, store)
                for q in range(RING):
                    pool.wait_ge(stored[q], 16 * len(range(q, SLOT_TILES, RING)))

            @block.tensor
            def _(pe):
                def experts_of(s, n):
                    return nc.values_load_multi_w_load_instructions(k.slots[:, 1, bass.ds(s, n)], engines=[mybir.EngineType.PE],
                                                                    min_val=0, max_val=E - 1)[1]

                def turn_z(s, q):
                    pe.wait_ge(z_in[q % RING], (s - q % RING) * (16 // RING) + 16)
                    wait_past(pe, zt_ready, s - 1)
                    for h in range(DH):
                        last = nc.tensor.transpose(zt_ps[:, q % 2, h * P:(h + 1) * P], z[:, q % RING, h * P:(h + 1) * P],
                                                   k.ident[:, :])
                    last.then_inc(z_turned, 1)

                def up(s, q, e):
                    pe.wait_ge(zt_ready, s + 1)
                    wait_past(pe, hid_ready, s - 1)
                    for h in range(DH):
                        last = nc.tensor.matmul(hid_ps[:, q % 2], zt[:, q % 2, h], k.we1[:, bass.ds(e, 1), h, :].rearrange(
                            "p o n -> p (o n)"), start=(h == 0), stop=(h == DH - 1))
                    last.then_inc(up_done, 1)

                def turn_hid(s, q):
                    pe.wait_ge(gelu_done, s + 1)
                    wait_past(pe, hid_t_ready, s - 1)
                    for j in range(HC):
                        last = nc.tensor.transpose(hid_t_ps[:, q % 2, j], hid[:, q % 2, j * P:(j + 1) * P], k.ident[:, :])
                    last.then_inc(hid_turned, 1)

                def down(s, q, e):
                    pe.wait_ge(hid_t_ready, s + 1)
                    wait_past(pe, y_ready, s - 1)
                    for j in range(HC):
                        last = nc.tensor.matmul(y_ps[:, q % 2, 0:D], hid_t[:, q % 2, j], k.we2[:, bass.ds(e, 1), j, :].rearrange(
                            "p o n -> p (o n)"), start=(j == 0), stop=(j == HC - 1))
                    last.then_inc(down_done, 1)

                pe.wait_ge(k.experts_in, 32 * E)
                turn_z(0, 0)
                turn_z(1, 1)
                up(0, 0, experts_of(0, 1)[0])

                def step(s, q):
                    e = experts_of(s, 2)
                    turn_hid(s, q)
                    up(s + 1, q + 1, e[1])
                    turn_z(s + 2, q + 2)
                    down(s, q, e[0])

                tiles(pe, n_main, RING, RING, step)
                e = experts_of(n_main, 2)
                turn_hid(n_main, n_main % 2)
                up(n_main + 1, n_main + 1, e[1])
                down(n_main, n_main % 2, e[0])
                turn_hid(n_main + 1, n_main + 1)
                down(n_main + 1, n_main + 1, e[1])

            @block.scalar
            def _(act):
                def take_zt(s, q):
                    act.wait_ge(z_turned, s + 1)
                    wait_past(act, up_done, s - 1)
                    nc.scalar.copy(zt[:, q % 2], zt_ps[:, q % 2, 0:D].rearrange("p (h n) -> p h n", h=DH)).then_inc(zt_ready, 1)

                def gelu(s, q):
                    act.wait_ge(hid_ready, s + 1)
                    nc.scalar.activation(hid[:, q % 2], hid[:, q % 2], ACT.Gelu).then_inc(gelu_done, 1)

                take_zt(0, 0)
                take_zt(1, 1)

                def step(s, q):
                    gelu(s, q)
                    take_zt(s + 2, q)

                tiles(act, n_main, 2, 2, step)
                gelu(n_main, n_main)
                gelu(n_main + 1, n_main + 1)

            @block.vector
            def _(dve):
                def experts_of(s, n):
                    return nc.values_load_multi_w_load_instructions(k.slots[:, 1, bass.ds(s, n)], engines=[mybir.EngineType.DVE],
                                                                    min_val=0, max_val=E - 1)[1]

                def bias_up(s, q, e):
                    dve.wait_ge(up_done, s + 1)
                    wait_past(dve, hid_turned, s - 1)
                    nc.vector.tensor_tensor(hid[:, q % 2], hid_ps[:, q % 2], be1[:, bass.ds(e, 1), :].rearrange("p o n -> p (o n)"),
                                            ALU.add).then_inc(hid_ready, 1)

                def take_hid(s, q):
                    dve.wait_ge(hid_turned, s + 1)
                    wait_past(dve, down_done, s - 1)
                    nc.vector.tensor_copy(hid_t[:, q % 2], hid_t_ps[:, q % 2]).then_inc(hid_t_ready, 1)

                def bias_down(s, q, e):
                    if not isinstance(s, int) or s >= RING:
                        dve.wait_ge(stored[q % RING], (s - q % RING) * (16 // RING))
                    nc.vector.tensor_copy(idx[:, q % RING:q % RING + 1], z[:, q % RING, D:ZW])
                    dve.wait_ge(down_done, s + 1)
                    nc.vector.tensor_tensor(y[:, q % RING], y_ps[:, q % 2, 0:D], be2[:, bass.ds(e, 1), :].rearrange("p o n -> p (o n)"),
                                            ALU.add).then_inc(y_ready, 1)

                dve.wait_ge(k.bias_in, 32 * E)
                bias_up(0, 0, experts_of(0, 1)[0])

                def step(s, q):
                    e = experts_of(s, 2)
                    take_hid(s, q)
                    bias_up(s + 1, q + 1, e[1])
                    bias_down(s, q, e[0])

                tiles(dve, SLOT_TILES - 1, RING, RING, step)
                last = SLOT_TILES - 1
                e = experts_of(last, 1)
                take_hid(last, last % RING)
                bias_down(last, last % RING, e[0])


def combine(nc, k):
    STEP = 5
    ROUNDS = TILES // STEP
    with ExitStack() as ctx:
        sem = lambda name: ctx.enter_context(nc.semaphore(name))
        both = k.acc[0:R, 0:DH, :].rearrange("p h n -> p (h n)")[:, 0:2 * STEP * K * D].rearrange(
            "p (s t k d) -> p s t k d", s=2, t=STEP, k=K)
        rows_in, stored = k.results_in, k.results_stored
        first, summed = sem("c_first"), sem("c_summed")

        with nc.Block() as block:

            @block.sync
            def _(sp):
                def load(i, s):
                    wait_past(sp, summed, i - 1)
                    sp.dma_start(both[:, s], k.moe_rows[bass.ds(i * (STEP * R * K), STEP * R * K), :].rearrange(
                        "(t p k) d -> p t k d", p=R, k=K)).then_inc(rows_in[s], 16)

                tiles(sp, ROUNDS, 2, 2, load)

            @block.vector
            def _(dve):
                def add(i, s):
                    x1 = k.x1[:, bass.ds(i * STEP, STEP), :]
                    dve.wait_ge(rows_in[s], (i - s) * 8 + 16)
                    nc.vector.tensor_tensor(both[:, s, :, 0], both[:, s, :, 0], both[:, s, :, 1], ALU.add).then_inc(first, 1)
                    dve.wait_ge(first, i + 1)
                    nc.vector.tensor_tensor(x1, x1, both[:, s, :, 0], ALU.add).then_inc(summed, 1)

                tiles(dve, ROUNDS, 2, 2, add)

            @block.scalar
            def _(act):
                def store(i, s):
                    act.wait_ge(summed, i + 1)
                    act.dma_start(k.out[bass.ds(i * (STEP * R), STEP * R), :].rearrange("(t p) d -> p t d", p=R),
                                  k.x1[:, bass.ds(i * STEP, STEP), :]).then_inc(stored, 16)

                tiles(act, ROUNDS, 2, 2, store)
                act.wait_ge(stored, 16 * ROUNDS)


INS = ["x", "src", "dst", "L0_gnn_W_l", "L0_gnn_W_r", "L0_gnn_att", "L0_gnn_bias", "L0_gnn_W1", "L0_gnn_b1", "L0_gnn_W2",
       "L0_gnn_b2", "L0_gnn_gamma1", "L0_gnn_beta1", "L0_gnn_gamma2", "L0_gnn_beta2", "L0_ffn_Wg", "L0_ffn_bg", "L0_ffn_W1",
       "L0_ffn_b1", "L0_ffn_W2", "L0_ffn_b2"]


def graph_ffn_kernel(nc, *args):
    k = Program()
    *ins, k.out = args
    (k.x, k.src, k.dst, k.W_l, k.W_r, k.att, k.bias, k.W1, k.b1, k.W2, k.b2, k.gamma1, k.beta1, k.gamma2, k.beta2, k.Wg,
     k.bg, k.We1, k.be1, k.We2, k.be2) = ins
    dram = lambda name, shape, dt=F32: nc.dram_tensor(name, shape, dt).ap()
    k.first_rows = dram("first_rows", [ETP + 1])
    k.last_rows = dram("last_rows", [ETP + 1])
    k.base_rows = dram("base_rows", [1, ETP], I32)
    k.rel_rows = dram("rel_rows", [ETP * P], BF16)
    k.gate_rows = dram("gate_rows", [NCH, GATES], BF16)
    k.go_on_rows = dram("go_on_rows", [NCH, T])
    k.xl_rows = dram("xl_rows", [COLS, XW])
    k.xr_rows = dram("xr_rows", [COLS, XW])
    k.z_rows = dram("z_rows", [COLS, D])
    k.disp_rows = dram("disp_rows", [E * REGION + P, ZW])
    k.moe_rows = dram("moe_rows", [K * N, D])

    with ExitStack() as ctx:
        keep = lambda name, shape, dt=F32: ctx.enter_context(nc.sbuf_tensor(name, shape, dt))
        k.iota_row = keep("iota_row", [P, P])
        k.iota_col = keep("iota_col", [P, 1])
        k.ident = keep("ident", [P, P])
        k.norm1 = keep("norm1", [P, 2, DH])
        k.norm2 = keep("norm2", [P, 2, DH])
        k.slots = keep("slots", [1, 2, SLOT_TILES], I32)
        k.acc = keep("acc", [P, DH + 1, COLS])
        k.chain, k.linked = ctx.enter_context(nc.semaphore("chain")), 0
        k.var_ready, k.root_ready, k.asked, k.given = (ctx.enter_context(nc.semaphore("var_ready")),
                                                       ctx.enter_context(nc.semaphore("root_ready")), 0, 0)
        features = k.acc[:, 0:DH, :].rearrange("p h n -> p (h n)")
        k.be1_all = features[:, 0:E * HID].rearrange("p (e n) -> p e n", e=E)
        k.be2_all = features[:, E * HID:E * (HID + D)].rearrange("p (e n) -> p e n", e=E)
        k.bias_in = ctx.enter_context(nc.semaphore("bias_in"))
        k.experts_in = ctx.enter_context(nc.semaphore("experts_in"))
        k.results_in = [ctx.enter_context(nc.semaphore(f"results_in{s}")) for s in range(2)]
        k.results_stored = ctx.enter_context(nc.semaphore("results_stored"))
        with ExitStack() as edges:
            sb = lambda name, shape, dt=F32: edges.enter_context(nc.sbuf_tensor(name, shape, dt))
            k.neg_col = sb("neg_col", [P, 1])
            k.one = sb("one", [P, 1])
            k.head_rows = sb("head_rows", [1, H + 2, P])
            k.src_e = sb("src_e", [P, ETP], I32)
            k.neg_rel = sb("neg_rel", [P, ETP])
            k.att_pos = sb("att_pos", [P, D])
            k.bases = sb("bases", [1, ETL], I32)
            prepare_edges(nc, k)
            project_nodes(nc, k)
            attend(nc, k)
        join_heads(nc, k)
        k.we1 = keep("we1", [P, E, DH, HID])
        k.we2 = keep("we2", [P, E, HC, D])
        feed_forward(nc, k)
        k.x1 = keep("x1", [R, TILES, D])
        route_tokens(nc, k)
        apply_experts(nc, k)
        combine(nc, k)


def kernel(**inputs):
    import concourse.bacc as _bacc
    from concourse.bass_utils import run_bass_kernel_spmd as _run

    nc = _bacc.Bacc("TRN2", target_bir_lowering=False, num_devices=1)
    arrays, args = {}, []
    for name in INS:
        a = np.ascontiguousarray(inputs[name])
        arrays[f"in_{name}_dram"] = a
        args.append(nc.dram_tensor(f"in_{name}_dram", a.shape, mybir.dt.from_np(a.dtype), kind="ExternalInput").ap())
    args.append(nc.dram_tensor("out_dram", (N, D), F32, kind="ExternalOutput").ap())
    graph_ffn_kernel(nc, *args)
    r = _run(nc, [arrays], core_ids=[0])
    return r.results[0]["out_dram"]
```

```python
from contextlib import ExitStack

import concourse.bass as bass
import numpy as np
from concourse import mybir

F32 = mybir.dt.float32
BF16 = mybir.dt.bfloat16
I32 = mybir.dt.int32
ALU = mybir.AluOpType
ACT = mybir.ActivationFunctionType
AX = mybir.AxisListType

P = 128
N = 6250
D = 256
DH = D // P
H = 4
C = D // H
SLOPE = 0.2
EPS = 1e-5
SEG_EPS = 1e-16
NEG = 2.0 ** 100

EDGES = 106250
NT = (N + P - 1) // P
NTAIL = N - (NT - 1) * P
NTP = NT + 1
COLS = NTP * P
ET = (EDGES + P - 1) // P
T = 32
NCH = (ET + T - 1) // T
ETL = NCH * T
Q = (ETL + P - 1) // P
ETP = Q * P
FULLQ = EDGES // (P * P)
ROWS_LAST = (EDGES - FULLQ * P * P) // P
EDGES_LAST = EDGES - FULLQ * P * P - ROWS_LAST * P
LN_HALF = NTP // 2
GATES = 2 * H * (T + 1) + 2 * H * T
XW = D + 8

E = 8
HID = 512
HC = HID // P
K = 2
R = 125
TILES = N // R
W = 2 * R
CHUNKS = N // W
REGION = NT * P + P
SLOT_TILES = (K * N + E * (P - 1)) // P
SLOT_TILES += SLOT_TILES % 2
ZW = D + 1
NO_ROW = 4 * COLS


def link_on(dve, k):

    def link(ins):
        k.linked += 1
        ins.then_inc(k.chain, 1)
        dve.wait_ge(k.chain, k.linked)

    return link


def ask_root(nc, k, dve, var):
    k.asked += 1
    nc.vector.tensor_scalar(var, var, EPS, None, ALU.add).then_inc(k.var_ready, 1)
    dve.wait_ge(k.root_ready, k.asked)


def give_root(nc, k, act, root, var):
    k.given += 1
    act.wait_ge(k.var_ready, k.given)
    nc.scalar.activation(root, var, ACT.Sqrt).then_inc(k.root_ready, 1)


def tiles(engine, n, front, unroll, body, start=0):
    front += start
    for t in range(start, front):
        body(t, t % unroll)
    rounds = (n - front) // unroll
    if rounds:
        with engine.Fori(0, rounds) as i:
            for u in range(unroll):
                body(i * unroll + (front + u), (front + u) % unroll)
    for t in range(front + rounds * unroll, n):
        body(t, t % unroll)


def wait_past(engine, semaphore, value):
    if isinstance(value, int) and value <= 0:
        return
    engine.wait_ge(semaphore, value)


def gate_views(row):
    f, b = H * (T + 1), H * T
    cut = lambda at, n: row[:, at:at + n].rearrange("p (h t) -> p h t", h=H)
    return cut(0, f), cut(f, f), cut(2 * f, b), cut(2 * f + b, b)


class Program:
    pass


def prepare_edges(nc, k):
    with ExitStack() as ctx:
        sb = lambda name, shape, dt=F32: ctx.enter_context(nc.sbuf_tensor(name, shape, dt))
        sem = lambda name: ctx.enter_context(nc.semaphore(name))
        src_ps = ctx.enter_context(nc.psum_tensor("p_src_ps", [P, 2, 512], F32))
        rel_ps = ctx.enter_context(nc.psum_tensor("p_rel_ps", [P, 2, 512], F32))
        rows_i = sb("p_rows_i", [P, 2, Q, P], I32)
        rows_f = sb("p_rows_f", [P, 2, Q, P])
        rel = sb("p_rel", [P, Q, P])
        rel_bf = sb("p_rel_bf", [P, Q, P], BF16)
        ends = sb("p_ends", [P, 2, Q])
        ints = sb("p_ints", [P, P + 1], I32)
        first = sb("p_first", [NCH, T + 2])
        last = sb("p_last", [NCH, T + 2])
        go_on = sb("p_go_on", [NCH, T + 1])
        single = sb("p_single", [NCH, T + 1])
        gates = sb("p_gates", [NCH, GATES], BF16)
        blank = sb("p_blank", [1, 2])
        padded, loaded, iotas = sem("p_padded"), sem("p_loaded"), sem("p_iotas")
        rows_ready, rel_ready, turned = sem("p_rows"), sem("p_rel_s"), sem("p_turned")
        ends_ready, stored, ends_in, gates_ready = sem("p_ends_s"), sem("p_stored"), sem("p_ends_in"), sem("p_gates_s")

        with nc.Block() as block:

            @block.sync
            def _(sp):
                for a, name in enumerate((k.dst, k.src)):
                    sp.dma_start(rows_i[:, a, 0:FULLQ, :],
                                 name[0:FULLQ * P * P].rearrange("(q p e) -> p q e", p=P, e=P)).then_inc(loaded, 16)
                sp.wait_ge(padded, 2)
                for a, name in enumerate((k.dst, k.src)):
                    at = FULLQ * P * P
                    if ROWS_LAST:
                        sp.dma_start(rows_i[0:ROWS_LAST, a, FULLQ, :],
                                     name[at:at + ROWS_LAST * P].rearrange("(p e) -> p e", e=P)).then_inc(loaded, 16)
                        at += ROWS_LAST * P
                    if EDGES_LAST:
                        sp.dma_start(rows_i[ROWS_LAST:ROWS_LAST + 1, a, FULLQ, 0:EDGES_LAST],
                                     name[at:EDGES].rearrange("(p e) -> p e", p=1)).then_inc(loaded, 16)
                sp.wait_ge(ends_ready, 1)
                with nc.allow_non_contiguous_dma(reason="one number of each tile"):
                    sp.dma_start(k.first_rows[1:1 + ETP].rearrange("(q p) -> p q", p=P), ends[:, 0]).then_inc(stored, 16)
                    sp.dma_start(k.last_rows[1:1 + ETP].rearrange("(q p) -> p q", p=P), ends[:, 1]).then_inc(stored, 16)
                    sp.dma_start(k.base_rows[0].rearrange("(q p) -> p q", p=P),
                                 rows_i[:, 0, :, 0]).then_inc(stored, 16)
                sp.dma_start(k.first_rows[0:1], blank[0:1, 0:1]).then_inc(stored, 16)
                sp.dma_start(k.last_rows[0:1], blank[0:1, 1:2]).then_inc(stored, 16)
                sp.wait_ge(rel_ready, 2)
                sp.dma_start(k.rel_rows.rearrange("(q p e) -> p q e", p=P, e=P), rel_bf[:, :, :]).then_inc(stored, 16)
                sp.wait_ge(stored, 96)
                for rows, out in ((k.first_rows, first), (k.last_rows, last)):
                    overlapping = bass.AP(tensor=rows.tensor, offset=0, ap=[[T, NCH], [1, T + 2]])
                    sp.dma_start(out[:, :], overlapping).then_inc(ends_in, 16)
                sp.wait_ge(gates_ready, 1)
                sp.dma_start(k.gate_rows, gates[:, :]).then_inc(stored, 16)
                sp.dma_start(k.go_on_rows, go_on[:, 0:T]).then_inc(stored, 16)
                sp.wait_ge(stored, 128)

            @block.scalar
            def _(act):
                act.wait_ge(loaded, 32 * (1 + (ROWS_LAST > 0) + (EDGES_LAST > 0)))
                act.dma_start(k.att_all[:, :], k.att.rearrange("h c -> (h c)").partition_broadcast(P)).then_inc(k.w_in, 16)
                for a, w in enumerate((k.W_l, k.W_r)):
                    act.dma_start(k.w_ext[:, a, :, 0:D], w.rearrange("(h p) n -> p h n", p=P)).then_inc(k.w_in, 16)
                for i, (a, b) in enumerate(((0, LN_HALF), (LN_HALF, NT - 1))):
                    act.dma_start(k.x_all[:, a:b, :], k.x[a * P:b * P, :].rearrange("(t p) d -> p t d", p=P)
                                  ).then_inc(k.x_in[i], 16)
                act.wait_ge(padded, 3)
                act.dma_start(k.x_all[0:NTAIL, NT - 1, :], k.x[(NT - 1) * P:N, :]).then_inc(k.x_in[1], 16)

            @block.gpsimd
            def _(pool):
                nc.gpsimd.iota(ints[:, 0:P], [[1, P]], base=0, channel_multiplier=0).then_inc(iotas, 1)
                nc.gpsimd.iota(ints[:, P:P + 1], [[0, 1]], base=0, channel_multiplier=1).then_inc(iotas, 1)

            @block.vector
            def _(dve):
                link = link_on(dve, k)
                nc.vector.memset(rows_i[:, 0, FULLQ:Q, :], N).then_inc(padded, 1)
                nc.vector.memset(rows_i[:, 1, FULLQ:Q, :], 0).then_inc(padded, 1)
                nc.vector.memset(k.x_all[:, NT - 1:NTP, :], 0.0).then_inc(padded, 1)
                nc.vector.memset(blank[:, :], -1.0)
                nc.vector.memset(k.one[:, :], 1.0)
                link(nc.vector.memset(k.head_rows[:, :, :], 0.0))
                for h in range(H):
                    nc.vector.memset(k.head_rows[:, h, h:2 * H:H], 1.0)
                for h in range(2):
                    nc.vector.memset(k.head_rows[:, H + h, h * C:(h + 1) * C], 1.0)
                dve.wait_ge(iotas, 2)
                link(nc.vector.tensor_copy(k.iota_row[:, :], ints[:, 0:P]))
                link(nc.vector.tensor_copy(k.iota_col[:, :], ints[:, P:P + 1]))
                link(nc.vector.tensor_scalar(k.neg_col[:, :], k.iota_col[:, :], -1.0, None, ALU.mult))
                link(nc.vector.tensor_scalar(k.ident[:, :], k.iota_row[:, :], k.iota_col[:, 0:1], None, ALU.is_equal))
                dve.wait_ge(loaded, 32 * (1 + (ROWS_LAST > 0) + (EDGES_LAST > 0)))
                link(nc.vector.tensor_copy(rows_f[:, 0], rows_i[:, 0]))
                nc.vector.tensor_copy(rows_f[:, 1], rows_i[:, 1]).then_inc(rows_ready, 1)
                nc.vector.tensor_copy(ends[:, 0], rows_f[:, 0, :, 0])
                nc.vector.tensor_copy(ends[:, 1], rows_f[:, 0, :, P - 1]).then_inc(ends_ready, 1)
                nc.vector.tensor_tensor(rel[:, :, :], rows_f[:, 0], rows_f[:, 0, :, 0:1].to_broadcast([P, Q, P]),
                                        ALU.subtract).then_inc(rel_ready, 1)
                dve.wait_ge(rel_ready, 1)
                nc.vector.tensor_copy(rel_bf[:, :, :], rel[:, :, :]).then_inc(rel_ready, 1)
                for g in range((Q + 3) // 4):
                    n = min(4, Q - 4 * g)
                    dve.wait_ge(turned, 2 * g + 2)
                    at = slice(4 * g * P, (4 * g + n) * P)
                    nc.vector.tensor_copy(k.src_e[:, at], src_ps[:, g, 0:n * P])
                    nc.vector.tensor_scalar(k.neg_rel[:, at], rel_ps[:, g, 0:n * P], -1.0, None, ALU.mult)
                dve.wait_ge(ends_in, 32)
                j = T + 1
                link(nc.vector.tensor_tensor(go_on[:, :], first[:, 1:j + 1], last[:, 0:j], ALU.is_equal))
                link(nc.vector.tensor_tensor(single[:, :], first[:, 0:j], last[:, 0:j], ALU.is_equal))
                g_in, g_pass, b_in, b_pass = gate_views(gates[:, :])
                link(nc.vector.memset(gates[:, :], -NEG))
                for h in range(H):
                    nc.vector.tensor_scalar(g_in[:, h, 0:T], go_on[:, 0:T], 1.0, NEG, ALU.subtract, ALU.mult)
                    nc.vector.memset(g_in[:, h, T:j], 0.0)
                    nc.vector.tensor_scalar(g_pass[:, h, T:j], single[:, T:j], 1.0, NEG, ALU.subtract, ALU.mult)
                    nc.vector.tensor_scalar(b_in[:, h, 0:T - 1], go_on[:, 1:T], 1.0, NEG, ALU.subtract, ALU.mult)
                link(nc.vector.tensor_tensor(last[:, 0:T], go_on[:, 0:T], single[:, 0:T], ALU.mult))
                for h in range(H):
                    nc.vector.tensor_scalar(g_pass[:, h, 1:T], last[:, 1:T], 1.0, NEG, ALU.subtract, ALU.mult)
                link(nc.vector.tensor_tensor(first[:, 0:T - 1], go_on[:, 1:T], single[:, 2:T + 1], ALU.mult))
                for h in range(H):
                    link(nc.vector.tensor_scalar(b_pass[:, h, 0:T - 1], first[:, 0:T - 1], 1.0, NEG, ALU.subtract,
                                                 ALU.mult))
                nc.vector.memset(blank[:, :], -1.0).then_inc(gates_ready, 1)

            @block.tensor
            def _(pe):
                pe.wait_ge(rows_ready, 1)
                pe.wait_ge(k.chain, 5)
                pe.wait_ge(rel_ready, 1)
                for g in range((Q + 3) // 4):
                    for out, rows in ((src_ps, rows_f[:, 1]), (rel_ps, rel[:, :, :])):
                        for q in range(4 * g, min(4 * g + 4, Q)):
                            last = nc.tensor.transpose(out[:, g, (q % 4) * P:(q % 4 + 1) * P], rows[:, q, :],
                                                       k.ident[:, :])
                        last.then_inc(turned, 1)


def inverse_root(nc, link, out, var, root):
    link(nc.vector.reciprocal(out, root))
    link(nc.vector.tensor_tensor(root, out, out, ALU.mult))
    link(nc.vector.scalar_tensor_tensor(root, root, -0.5, var, ALU.mult, ALU.mult))
    link(nc.vector.scalar_tensor_tensor(out, root, 1.5, out, ALU.add, ALU.mult))


def norm_scale(nc, link, st, mean, rstd, tmp, root):
    half = D // 2
    link(nc.vector.tensor_tensor(tmp[:, 0, :], st[:, :, 1], st[:, :, 4], ALU.subtract))
    link(nc.vector.tensor_tensor(tmp[:, 0, :], tmp[:, 0, :], tmp[:, 0, :], ALU.mult))
    link(nc.vector.tensor_tensor(tmp[:, 1, :], st[:, :, 2], st[:, :, 5], ALU.add))
    link(nc.vector.tensor_scalar(tmp[:, 0, :], tmp[:, 0, :], 0.25, None, ALU.mult))
    link(nc.vector.scalar_tensor_tensor(tmp[:, 0, :], tmp[:, 1, :], 0.5 / half, tmp[:, 0, :], ALU.mult, ALU.add))
    link(nc.vector.tensor_tensor(mean, st[:, :, 1], st[:, :, 4], ALU.add))
    link(nc.vector.tensor_scalar(mean, mean, 0.5, None, ALU.mult))
    root(tmp[:, 0, :])
    inverse_root(nc, link, rstd, tmp[:, 0, :], tmp[:, 1, :])


def project_nodes(nc, k):
    RING = 4
    AHEAD = RING - 1
    TURN = LN_HALF - AHEAD
    STEPS = 4
    with ExitStack() as ctx:
        sb = lambda name, shape, dt=F32: ctx.enter_context(nc.sbuf_tensor(name, shape, dt))
        pb = lambda name, shape: ctx.enter_context(nc.psum_tensor(name, shape, F32))
        sem = lambda name: ctx.enter_context(nc.semaphore(name))
        x_all, w_ext = k.x_all, k.w_ext
        stats = sb("ln_stats", [P, NTP, 6])
        mean = sb("ln_mean", [P, NTP])
        rstd = sb("ln_rstd", [P, NTP])
        tmp = sb("ln_tmp", [P, 2, NTP])
        w_att = sb("w_att", [P, 2, 2, D])
        z_sb = sb("z_sb", [P, RING, D])
        zt_sb = sb("zt_sb", [P, 2, 2, P])
        xl_sb = sb("xl_sb", [P, RING, XW])
        xr_sb = sb("xr_sb", [P, RING, XW])
        f_sb = sb("f_sb", [P, 2, D])
        g_sb = sb("g_sb", [P, 2, D])
        lin = sb("lin", [P, 2, H])
        red = sb("red", [P, 2, H])
        zt_ps = pb("zt_ps", [P, 2, 512])
        xl_ps = pb("xl_ps", [P, 2, 512])
        xr_ps = pb("xr_ps", [P, 2, 512])
        stat_done, w_ready = sem("n_stat"), sem("n_w_ready")
        z_ready, zt_done, zt_taken = sem("n_z"), sem("n_zt"), sem("n_zt_taken")
        z_kept = [sem(f"n_z_kept{s}") for s in range(RING)]
        mm_done, xr_ready, xr_full, did = sem("n_mm"), sem("n_xr"), sem("n_xr_full"), sem("n_did")
        stored = [sem(f"n_stored{s}") for s in range(RING)]

        with nc.Block() as block:

            @block.sync
            def _(sp):
                def store(t, s):
                    sp.wait_ge(xr_full, t + 1)
                    row = t * P
                    sp.dma_start(k.xl_rows[bass.ds(row, P), :], xl_sb[:, s, :]).then_inc(stored[s], 16)
                    sp.dma_start(k.xr_rows[bass.ds(row, P), :], xr_sb[:, s, :]).then_inc(stored[s], 16)

                tiles(sp, NTP, RING, RING, store)
                for s in range(RING):
                    sp.wait_ge(stored[s], 32 * len(range(s, NTP, RING)))

            @block.gpsimd
            def _(pool):
                nc.gpsimd.memset(k.acc[:, :, :], 0.0)

            @block.vector
            def _(dve):
                link = link_on(dve, k)
                dve.wait_ge(k.w_in, 48)
                for a in range(2):
                    for h in range(2):
                        link(nc.vector.scalar_tensor_tensor(w_att[:, a, h, :], w_ext[:, a, h, 0:D], SLOPE,
                                                            k.att_all[:, :], ALU.mult, ALU.mult))
                        nc.vector.memset(w_ext[:, a, h, D + H:XW], 0.0)
                        link(nc.vector.tensor_reduce(w_ext[:, a, h, D:D + H],
                                                     w_att[:, a, h, :].rearrange("p (h c) -> p h c", c=C), AX.X,
                                                     ALU.add))
                nc.vector.tensor_scalar(k.att_pos[:, :], k.att_all[:, :], 1.0 - SLOPE, None, ALU.mult).then_inc(w_ready, 1)

                def measure(t):
                    nc.vector.bn_stats(stats[:, bass.ds(t, 1), :], x_all[:, bass.ds(t, 1), :]).then_inc(stat_done, 1)

                def scales(a, b):
                    dve.wait_ge(stat_done, b)
                    norm_scale(nc, link, stats[:, a:b], mean[:, a:b], rstd[:, a:b], tmp[:, :, a:b],
                               lambda var: ask_root(nc, k, dve, var))

                def normalise(t, s):
                    wait_past(dve, zt_done, t - (RING - 1))
                    if not isinstance(t, int) or t >= RING:
                        dve.wait_ge(z_kept[s], (t - s) * (16 // RING))
                    nc.vector.tensor_scalar(z_sb[:, s, :], x_all[:, bass.ds(t, 1), :], mean[:, bass.ds(t, 1)],
                                            rstd[:, bass.ds(t, 1)], ALU.subtract, ALU.mult).then_inc(z_ready, 1)

                def self_logits(t, s, between=lambda: None):
                    b = s % 2
                    dve.wait_ge(xr_ready, t + 1)
                    nc.vector.tensor_tensor(f_sb[:, b, :], xr_ps[:, b, 0:D], xl_sb[:, s, 0:D], ALU.add).then_inc(did, 1)
                    nc.vector.tensor_tensor(lin[:, b, :], xr_ps[:, b, D:D + H], xl_sb[:, s, D:D + H], ALU.add).then_inc(did, 1)
                    dve.wait_ge(did, t * STEPS + 1)
                    nc.vector.scalar_tensor_tensor(g_sb[:, b, :], f_sb[:, b, :], 0.0, k.att_pos[:, :], ALU.max,
                                                   ALU.mult).then_inc(did, 1)
                    between()
                    dve.wait_ge(did, t * STEPS + 3)
                    nc.vector.tensor_reduce(red[:, b, :], g_sb[:, b, :].rearrange("p (h c) -> p h c", c=C), AX.X,
                                            ALU.add).then_inc(did, 1)
                    dve.wait_ge(did, t * STEPS + 4)
                    if not isinstance(t, int) or t >= RING:
                        dve.wait_ge(stored[s], (t - s) * (32 // RING))
                    nc.vector.tensor_tensor(xr_sb[:, s, D + H:XW], red[:, b, :], lin[:, b, :], ALU.add).then_inc(xr_full, 1)

                dve.wait_ge(k.x_in[0], 16)
                tiles(dve, LN_HALF, 0, 5, lambda t, s: measure(t))
                scales(0, LN_HALF)
                for t in range(AHEAD):
                    normalise(t, t)
                dve.wait_ge(w_ready, 1)
                dve.wait_ge(k.x_in[1], 32)

                def first_half(t, s):
                    normalise(t + AHEAD, (s + AHEAD) % RING)
                    self_logits(t, s, lambda: measure(t + LN_HALF))

                def second_half(t, s):
                    normalise(t + AHEAD, (s + AHEAD) % RING)
                    self_logits(t, s)

                tiles(dve, TURN, RING, RING, first_half)
                for t in range(TURN + LN_HALF, NTP):
                    measure(t)
                scales(LN_HALF, NTP)
                tiles(dve, NTP - AHEAD, 0, RING, second_half, TURN)
                for t in range(NTP - AHEAD, NTP):
                    self_logits(t, t % RING)

            @block.scalar
            def _(act):
                halves = ((0, LN_HALF), (LN_HALF, NTP))
                give_root(nc, k, act, tmp[:, 1, slice(*halves[0])], tmp[:, 0, slice(*halves[0])])

                def take_zt(t, s):
                    act.wait_ge(zt_done, t + 1)
                    wait_past(act, mm_done, t - 1)
                    nc.scalar.copy(zt_sb[:, s % 2], zt_ps[:, s % 2, 0:D].rearrange("p (h n) -> p h n", h=2)
                                   ).then_inc(zt_taken, 1)
                    act.dma_start(k.z_rows[bass.ds(t * P, P), :], z_sb[:, s]).then_inc(z_kept[s], 16)

                def take_x(t, s):
                    act.wait_ge(mm_done, t + 1)
                    if not isinstance(t, int) or t >= RING:
                        act.wait_ge(stored[s], (t - s) * (32 // RING))
                    nc.scalar.copy(xl_sb[:, s, :], xl_ps[:, s % 2, 0:XW])
                    nc.scalar.copy(xr_sb[:, s, 0:D + H], xr_ps[:, s % 2, 0:D + H]).then_inc(xr_ready, 1)

                take_zt(0, 0)

                def both(t, s):
                    take_zt(t + 1, (s + 1) % RING)
                    take_x(t, s)

                tiles(act, TURN, RING, RING, both)
                give_root(nc, k, act, tmp[:, 1, slice(*halves[1])], tmp[:, 0, slice(*halves[1])])
                tiles(act, NTP - 1, 0, RING, both, TURN)
                take_x(NTP - 1, (NTP - 1) % RING)
                for s in range(RING):
                    act.wait_ge(z_kept[s], 16 * len(range(s, NTP, RING)))

            @block.tensor
            def _(pe):
                def turn(t, s):
                    pe.wait_ge(z_ready, t + 1)
                    wait_past(pe, zt_taken, t - 1)
                    for h in range(2):
                        last = nc.tensor.transpose(zt_ps[:, s % 2, h * P:(h + 1) * P], z_sb[:, s, h * P:(h + 1) * P],
                                                   k.ident[:, :])
                    last.then_inc(zt_done, 1)

                def project(t, s):
                    pe.wait_ge(zt_taken, t + 1)
                    wait_past(pe, xr_ready, t - 1)
                    wait_past(pe, did, t * STEPS - (2 * STEPS - 2))
                    for a, out in enumerate((xl_ps, xr_ps)):
                        for h in range(2):
                            last = nc.tensor.matmul(out[:, s, 0:XW], zt_sb[:, s, h, :], w_ext[:, a, h, :],
                                                    start=(h == 0), stop=(h == 1))
                    last.then_inc(mm_done, 1)

                pe.wait_ge(w_ready, 1)
                turn(0, 0)

                def both(t, s):
                    turn(t + 1, (s + 1) % RING)
                    project(t, s % 2)

                tiles(pe, NTP - 1, RING, RING, both)
                project(NTP - 1, (NTP - 1) % 2)


def load_bases(nc, k, engine, at, n):
    return nc.values_load_multi_w_load_instructions(k.bases[:, bass.ds(at, n)], engines=[engine], min_val=0, max_val=N)[1]


def attend(nc, k):
    QT = 4
    QUADS = T // QT
    PAIRS = T // 2
    LAG = 4
    LEAD = QUADS - LAG
    AHEAD = 6
    SOFT = 18
    EX = 2 * P
    assert NCH % 2 == 0
    with ExitStack() as ctx:
        sb = lambda name, shape, dt=F32: ctx.enter_context(nc.sbuf_tensor(name, shape, dt))
        pb = lambda name, shape: ctx.enter_context(nc.psum_tensor(name, shape, F32))
        sem = lambda name: ctx.enter_context(nc.semaphore(name))
        idx = sb("a_idx", [P, QUADS, QT], I32)
        xl_e = sb("a_xl_e", [P, 2 * T, XW])
        xr_w = sb("a_xr_w", [P, 2, QT, XW])
        rel_bc = sb("a_rel_bc", [P, 2, QT, P], BF16)
        far = sb("a_far", [P, QT, P])
        hot_n = sb("a_hot_n", [P, 2, QT, P])
        hot_e = sb("a_hot_e", [P, 2, QT, P])
        pos = sb("a_pos", [P, 2, D])
        red = sb("a_red", [P, 2, 2 * H])
        lg = sb("a_lg", [P, 2, 2, H, T])
        msg = sb("a_msg", [P, QT, D])
        exs = sb("a_exs", [P, 2, T, 2 * H])
        rel_r = sb("a_rel_r", [P, NCH, P], BF16)
        fresh = sb("a_fresh", [P, NCH])
        cut = sb("a_cut", [P, P + 1], BF16)
        lgr = sb("a_lgr", [P, 2, P])
        run = sb("a_run", [P, P])
        top = sb("a_top", [P, P])
        peak = sb("a_peak", [P, P])
        side = sb("a_side", [P, 2, P])
        begin = sb("a_begin", [P, P])
        ends = sb("a_ends", [P, 2, NCH])
        expo = sb("a_expo", [P, 2, P])
        gate = sb("a_gate", [1, 2, GATES], BF16)
        carry = sb("a_carry", [1, H])
        into = sb("a_into", [1, H, T + 1])
        reach = sb("a_reach", [1, H, T + 1])
        reach_t = sb("a_reach_t", [1, H, T])
        back = sb("a_back", [1, H, T])
        reach_b = sb("a_reach_b", [1, H, T])
        fade = sb("a_fade", [1, H])
        faded = sb("a_faded", [1, H])
        f_ps = pb("a_f_ps", [P, 2, 2, 512])
        o_ps = pb("a_o_ps", [P, 2, 512])
        sm_ps = pb("a_sm_ps", [P, 2, 512])

        fixed, bases_in, masks = sem("a_fixed"), sem("a_bases_in"), sem("a_masks")
        sides, sides_ready = sem("a_sides"), sem("a_sides_s")
        idx_ready, far_n, hot_n_ready, far_e, hot_e_ready = (sem("a_idx_s"), sem("a_far_n"), sem("a_hot_n_s"),
                                                             sem("a_far_e"), sem("a_hot_e_s"))
        xl_in = [sem(f"a_xl_in{q}") for q in range(2 * QUADS)]
        xr_in = [sem(f"a_xr_in{q}") for q in range(2)]
        rel_in = [sem(f"a_rel_in{q}") for q in range(2)]
        gate_in = [sem(f"a_gate_in{q}") for q in range(2)]
        f_done, settled, lg_ready = sem("a_f_s"), sem("a_settled"), sem("a_lg_s")
        rows_done, rows_taken, soft, ends_done = sem("a_rows"), sem("a_rows_taken"), sem("a_soft"), sem("a_ends")
        reach_done, peak_done, expo_ready, faded_ready = sem("a_reach_c"), sem("a_peak_s"), sem("a_expo_s"), sem("a_faded_s")
        turned, exs_ready, msg_ready, sum_done, added = (sem("a_turned"), sem("a_exs_s"), sem("a_msg_s"), sem("a_sum_s"),
                                                         sem("a_added"))

        def steps(engine, step):
            late = [(2, QUADS - LAG + j) for j in range(LAG)]
            soon = [(1, j) for j in range(QUADS - LAG)]
            step(0, 0, True, [None] * QUADS)
            step(1, 1, True, [None] * LAG + soon)
            with engine.Fori(0, NCH // 2 - 2) as r:
                step(r * 2 + 2, 0, True, late + soon)
                step(r * 2 + 3, 1, True, late + soon)
            step(NCH - 2, 0, True, late + soon)
            step(NCH - 1, 1, True, late + soon)
            step(NCH, 0, False, late + soon)
            step(NCH + 1, 1, False, late)

        def softmax_in(c):
            return not isinstance(c, int) or 1 <= c <= NCH

        with nc.Block() as block:

            @block.gpsimd
            def _(pool):
                def gather(c, p, j):
                    pool.wait_ge(idx_ready, c * QUADS + (j + 1))
                    pool.sem_inc(k.taken, 1)
                    for u in range(QT):
                        nc.gpsimd.indirect_dma_start(
                            xl_e[:, p * T + j * QT + u, :], None, k.xl_rows,
                            bass.IndirectOffsetOnAxis(ap=idx[:, j, u:u + 1], axis=0)
                        ).then_inc(xl_in[p * QUADS + j], 16)

                def messages(cc, pp, jj):
                    pool.wait_ge(exs_ready, cc + 1)
                    for g in range(2):
                        t = jj * QT + 2 * g
                        wait_past(pool, sum_done, cc * T + (t - 2))
                        nc.gpsimd.tensor_tensor(
                            msg[:, 2 * g:2 * g + 2, :].rearrange("p t (h c) -> p t h c", c=C),
                            xl_e[:, pp * T + t:pp * T + t + 2, 0:D].rearrange("p t (h c) -> p t h c", c=C),
                            exs[:, pp, t:t + 2, 0:H][:, :, :, None].to_broadcast([P, 2, H, C]),
                            ALU.mult).then_inc(msg_ready, 1)

                def step(c, p, logits, sums):
                    for j in range(QUADS):
                        if sums[j:j + 1] and sums[j]:
                            b, jj = sums[j]
                            messages(c - b, (p + b) % 2, jj)
                        more = j + LEAD >= QUADS
                        at = c + more
                        if logits and not (isinstance(at, int) and at >= NCH):
                            wait_past(pool, msg_ready, c * PAIRS + (2 * (j + LEAD + 1) - 2 * PAIRS))
                            gather(at, (p + more) % 2, (j + LEAD) % QUADS)

                for j in range(LEAD):
                    gather(0, 0, j)
                steps(pool, step)

            @block.sync
            def _(sp):
                with nc.allow_non_contiguous_dma(reason="one number of each tile"):
                    sp.dma_start(k.bases[:, :], k.base_rows[:, 0:ETL]).then_inc(bases_in, 16)
                    for h in range(H):
                        sp.dma_start(rel_r[h * T:(h + 1) * T], k.rel_rows[0:ETL * P].rearrange(
                            "(c t e) -> t c e", t=T, e=P)).then_inc(fixed, 16)
                        sp.dma_start(fresh[h * T:(h + 1) * T], k.go_on_rows.rearrange("c t -> t c")).then_inc(fixed, 16)

                def loads(c, p):
                    if not isinstance(c, int) or c >= 2:
                        sp.wait_ge(soft, (c - 1) * SOFT)
                    sp.dma_start(gate[:, p], k.gate_rows[bass.ds(c, 1), :]).then_inc(gate_in[p], 16)
                    for j in range(QUADS):
                        at = c * T + j * QT
                        if j % 2 == 0:
                            bases = load_bases(nc, k, mybir.EngineType.SP, at, 2 * QT)
                        wait_past(sp, far_n, c * QUADS + (j - 1))
                        sp.dma_start(rel_bc[:, j % 2].rearrange("p t e -> p (t e)"),
                                     k.rel_rows[bass.ds(at * P, QT * P)].partition_broadcast(P)).then_inc(rel_in[j % 2], 16)
                        wait_past(sp, f_done, c * PAIRS + (2 * (j - 1)))
                        for u in range(QT):
                            sp.dma_start(xr_w[:, j % 2, u, :], k.xr_rows[bass.ds(bases[j % 2 * QT + u], P), :]
                                         ).then_inc(xr_in[j % 2], 16)

                sp.wait_ge(bases_in, 16)
                loads(0, 0)
                loads(1, 1)
                with sp.Fori(0, NCH // 2 - 1) as r:
                    loads(r * 2 + 2, 0)
                    loads(r * 2 + 3, 1)

            @block.scalar
            def _(act):
                def indices(q, slot):
                    nc.scalar.copy(idx[:, slot, :], k.src_e[:, bass.ds(q * QT, QT)]).then_inc(idx_ready, 1)

                for q in range(AHEAD):
                    indices(q, q)

                def hot_nodes(c, j):
                    quad = c * QUADS + j
                    act.wait_ge(rel_in[j % 2], c * (8 * QUADS) + (j // 2 + 1) * 16)
                    nc.scalar.activation(far[:, :, :], rel_bc[:, j % 2], ACT.Abs, bias=k.neg_col[:, 0:1]).then_inc(far_n, 1)
                    act.wait_ge(far_n, quad + 1)
                    wait_past(act, f_done, c * PAIRS + 2 * (j - 1))
                    nc.scalar.activation(hot_n[:, j % 2], far[:, :, :], ACT.Relu, scale=-1.0,
                                         bias=k.one[:, 0:1]).then_inc(hot_n_ready, 1)
                    act.wait_ge(hot_n_ready, quad + 1)

                def hot_edges(c, j):
                    for u in range(QT):
                        nc.scalar.activation(far[:, u, :], k.iota_row[:, :], ACT.Abs,
                                             bias=k.neg_rel[:, bass.ds(c * T + (j * QT + u), 1)]).then_inc(far_e, 1)
                    act.wait_ge(far_e, c * T + (j + 1) * QT)
                    wait_past(act, sum_done, c * T + (j - 1) * QT)
                    nc.scalar.activation(hot_e[:, j % 2], far[:, :, :], ACT.Relu, scale=-1.0,
                                         bias=k.one[:, 0:1]).then_inc(hot_e_ready, 1)
                    act.wait_ge(hot_e_ready, c * QUADS + (j + 1))

                def step(c, p, logits, sums):
                    for j in range(QUADS):
                        quad = c * QUADS + j
                        if logits:
                            if not isinstance(c, int) or c * QUADS + j >= 2:
                                cc, pp, jj = (c, p, j - 2) if j >= 2 else (c - 1, 1 - p, j - 2 + QUADS)
                                act.wait_ge(xl_in[pp * QUADS + jj], (cc - pp) * (8 * QT) + 16 * QT)
                            indices(quad + AHEAD, (j + AHEAD) % QUADS)
                        following = c + (j + 1 == QUADS)
                        if logits and not (isinstance(following, int) and following >= NCH):
                            hot_nodes(following, (j + 1) % QUADS)
                        back = following - (2 if (j + 1) % QUADS < LAG else 1)
                        if not isinstance(back, int) or 0 <= back < NCH:
                            hot_edges(back, (j + 1 - LAG) % QUADS)
                        if not softmax_in(c):
                            continue
                        if j == 0:
                            act.wait_ge(rows_done, c)
                            nc.scalar.copy(lgr[:, :, :], sm_ps[:, 1 - p, 0:EX].rearrange("p (a e) -> p a e", a=2)
                                           ).then_inc(rows_taken, 1)
                            for i in range(2):
                                nc.scalar.activation(side[:, i], rel_r[:, bass.ds(c - 1, 1), :].rearrange("p o e -> p (o e)"),
                                                     ACT.Abs, scale=-1.0, bias=ends[:, i, bass.ds(c - 1, 1)]).then_inc(sides, 1)
                            act.wait_ge(sides, 3 * c - 1)
                            nc.scalar.activation(side[:, :, :], side[:, :, :], ACT.Copy, scale=-NEG).then_inc(sides_ready, 1)
                        if j == 1:
                            act.wait_ge(soft, (c - 1) * SOFT + 2)
                            nc.scalar.activation(begin[:, :], cut[:, 0:P], ACT.Copy, scale=-1.0 / NEG).then_inc(sides, 1)
                            act.wait_ge(sides, 3 * c)
                            nc.scalar.copy(begin[:, 0:1], fresh[:, bass.ds(c - 1, 1)]).then_inc(sides_ready, 1)
                        if j == 2:
                            act.wait_ge(soft, (c - 1) * SOFT + 15)
                            nc.scalar.activation(expo[:, :, :], lgr[:, :, :], ACT.Exp).then_inc(expo_ready, 1)
                        if j == 3:
                            act.wait_ge(soft, (c - 1) * SOFT + 16)
                            nc.scalar.activation(faded[:, :], fade[:, :], ACT.Exp).then_inc(faded_ready, 1)
                            act.wait_ge(turned, c)
                            wait_past(act, sum_done, (c - 2) * T + 1)
                            nc.scalar.copy(exs[:, 1 - p].rearrange("p t k -> p k t"),
                                           sm_ps[:, 1 - p, EX:EX + 2 * P].rearrange("p (k t) -> p k t", t=T)
                                           ).then_inc(exs_ready, 1)

                hot_nodes(0, 0)
                steps(act, step)

            @block.vector
            def _(dve):
                dve.wait_ge(fixed, 32 * H)
                for i, e in enumerate((0, P - 1)):
                    nc.vector.tensor_copy(ends[:, i], rel_r[:, :, e])
                nc.vector.memset(cut[:, 0:1], -NEG)
                nc.vector.memset(cut[:, P:P + 1], -NEG)
                nc.vector.memset(red[:, :, :], 0.0)
                nc.vector.memset(carry[:, :], -NEG)
                nc.vector.memset(back[:, :, :], -NEG)
                nc.vector.memset(o_ps[:, :, :], 0.0)
                nc.vector.tensor_scalar(fresh[:, :], fresh[:, :], -1.0, 1.0, ALU.mult, ALU.add).then_inc(masks, 1)
                dve.wait_ge(masks, 1)

                att = k.att_pos[:, None, :].to_broadcast([P, 2, D])

                def logits_of(c, p, j, g, between):
                    n = c * PAIRS + (2 * j + g + 1)
                    at = slice(j * QT + 2 * g, j * QT + 2 * g + 2)
                    dve.wait_ge(f_done, n)
                    nc.vector.scalar_tensor_tensor(pos[:, :, :], f_ps[:, g, :, 0:D], 0.0, att, ALU.max,
                                                   ALU.mult).then_inc(settled, 1)
                    between(0)
                    dve.wait_ge(settled, 2 * n - 1)
                    nc.vector.tensor_reduce(red[:, :, 0:H], pos[:, :, :].rearrange("p t (h c) -> p t h c", c=C), AX.X,
                                            ALU.add).then_inc(settled, 1)
                    between(1)
                    dve.wait_ge(settled, 2 * n)
                    nc.vector.tensor_tensor(lg[:, p, :, :, at].rearrange("p a h t -> p t (a h)"), red[:, :, :],
                                            f_ps[:, g, :, D:XW], ALU.add).then_inc(lg_ready, 1)

                def add_up(cc, jj, u, base):
                    n = cc * T + (jj * QT + u)
                    dve.wait_ge(sum_done, n + 1)
                    if jj == 0 and u == 0:
                        dve.wait_ge(soft, (cc + 1) * SOFT)
                    wait_past(dve, added, n)
                    window = k.acc[:, :, bass.ds(base, P)]
                    nc.vector.tensor_tensor(window, o_ps[:, u % 2, 0:3 * P].rearrange("p (b n) -> p b n", b=3), window,
                                            ALU.add).then_inc(added, 1)

                def softmax(cc, pp, part, node=None):
                    did = cc * SOFT

                    def done(i, ins):
                        ins.then_inc(soft, 1)

                    def after(i):
                        wait_past(dve, soft, did + i)

                    g_in, g_pass, b_in, b_pass = gate_views(gate[:, pp])
                    rel = rel_r[:, bass.ds(cc, 1), :].rearrange("p o e -> p (o e)")
                    if part == 0:
                        done(1, nc.vector.tensor_tensor(cut[:, 1:P], rel[:, 1:P], rel[:, 0:P - 1], ALU.not_equal))
                        after(1)
                        done(2, nc.vector.tensor_scalar(cut[:, 1:P], cut[:, 1:P], -NEG, None, ALU.mult))
                        dve.wait_ge(rows_taken, cc + 1)
                        done(3, nc.vector.tensor_tensor(peak[:, :], lgr[:, 0], lgr[:, 1], ALU.max))
                        after(3)
                        done(4, nc.vector.tensor_tensor_scan(run[:, :], cut[:, 0:P], peak[:, :], -NEG, ALU.add, ALU.max))
                        after(4)
                        done(5, nc.vector.tensor_tensor_scan(top[:, ::-1], cut[:, P:0:-1], run[:, ::-1], -NEG, ALU.add,
                                                             ALU.max))
                    if part == 1:
                        dve.wait_ge(ends_done, cc + 1)
                        dve.wait_ge(gate_in[pp], (cc - pp) * 8 + 16)
                        ends = sm_ps[0:1, pp, 0:EX].rearrange("p (a h t) -> p a h t", a=2, t=T)
                        done(6, nc.vector.tensor_tensor(into[:, :, 1:T + 1], ends[:, 1], g_in[:, :, 1:T + 1], ALU.add))
                        after(6)
                        done(7, nc.vector.tensor_tensor(into[:, :, 0], carry[:, :], g_in[:, :, 0], ALU.add))
                        done(8, nc.vector.tensor_tensor(back[:, :, 0:T - 1], ends[:, 0, :, 1:T], b_in[:, :, 0:T - 1],
                                                         ALU.add))
                        after(8)
                        flat = lambda a: a.rearrange("p h t -> p (h t)")
                        done(9, nc.vector.tensor_tensor_scan(flat(reach[:, :, :]), flat(g_pass), flat(into[:, :, :]),
                                                              -NEG, ALU.add, ALU.max))
                        done(10, nc.vector.tensor_tensor_scan(flat(reach_b[:, :, :])[:, ::-1], flat(b_pass)[:, ::-1],
                                                              flat(back[:, :, :])[:, ::-1], -NEG, ALU.add, ALU.max))
                        after(10)
                        done(11, nc.vector.tensor_copy(reach_t[:, :, :], reach[:, :, 0:T]))
                        done(12, nc.vector.tensor_copy(carry[:, :], reach[:, :, T]))
                    if part == 2:
                        dve.wait_ge(sides_ready, 2 * cc + 1)
                        dve.wait_ge(reach_done, cc + 1)
                        done(13, nc.vector.scalar_tensor_tensor(peak[:, :], side[:, 0], sm_ps[:, pp, 0:1], top[:, :],
                                                                ALU.add, ALU.max))
                        after(13)
                        done(14, nc.vector.scalar_tensor_tensor(peak[:, :], side[:, 1], sm_ps[:, pp, 1:2], peak[:, :],
                                                                ALU.add, ALU.max))
                        after(14)
                        done(15, nc.vector.tensor_tensor(lgr[:, :, :], lgr[:, :, :],
                                                         peak[:, None, :].to_broadcast([P, 2, P]), ALU.subtract))
                    if part == 3:
                        dve.wait_ge(peak_done, cc + 1)
                        first = sm_ps[0:1, pp, P:2 * P].rearrange("p (h t) -> p h t", t=T)[:, :, 0]
                        done(16, nc.vector.tensor_tensor(fade[:, :], into[:, :, 0], first, ALU.subtract))
                        dve.wait_ge(expo_ready, cc + 1)
                        dve.wait_ge(sides_ready, 2 * cc + 2)
                        done(17, nc.vector.tensor_tensor(expo[:, 1], expo[:, 1], begin[:, :], ALU.mult))
                    if part == 4:
                        dve.wait_ge(exs_ready, cc + 1)
                        wait_past(dve, added, cc * T)
                        column = k.acc[:, :, bass.ds(node, 1)]
                        done(18, nc.vector.tensor_tensor(column, column, sm_ps[:, pp, 2:5][:, :, None], ALU.mult))

                def step(c, p, logits, sums):
                    def soften(parts, j):
                        if softmax_in(c) and j in parts:
                            softmax(c - 1, 1 - p, parts[j])

                    for j in range(QUADS):
                        b, jj = sums[j] if sums[j:j + 1] and sums[j] else (0, 0)
                        soften({1: 0, 2: 1, 3: 3}, j)
                        if b:
                            bases = load_bases(nc, k, mybir.EngineType.DVE, (c - b) * T + jj * QT, QT)
                        if j == LAG and softmax_in(c):
                            softmax(c - 1, 1 - p, 4, bases[0])
                        for g in range(2):
                            def between(u):
                                if b:
                                    add_up(c - b, jj, 2 * g + u, bases[2 * g + u])

                            if logits:
                                logits_of(c, p, j, g, between)
                            else:
                                between(0)
                                between(1)
                            if g == 0:
                                soften({2: 2}, j)

                steps(dve, step)

            @block.tensor
            def _(pe):
                def logits_of(c, p, j, g):
                    if g == 0:
                        pe.wait_ge(hot_n_ready, c * QUADS + (j + 1))
                        pe.wait_ge(xr_in[j % 2], c * (QUADS * 8 * QT) + (j // 2 + 1) * (16 * QT))
                        pe.wait_ge(xl_in[p * QUADS + j], (c - p) * (8 * QT) + 16 * QT)
                    wait_past(pe, lg_ready, c * PAIRS + (2 * j + g - 1))
                    for u in range(2 * g, 2 * g + 2):
                        out = f_ps[:, g, u % 2, 0:XW]
                        nc.tensor.matmul(out, hot_n[:, j % 2, u, :], xr_w[:, j % 2, u, :], start=True, stop=False)
                        last = nc.tensor.matmul(out, k.ident[:, :], xl_e[:, p * T + j * QT + u, :], start=False, stop=True)
                    last.then_inc(f_done, 1)

                def sums_of(cc, pp, jj, g):
                    if g == 0:
                        pe.wait_ge(hot_e_ready, cc * QUADS + (jj + 1))
                    pe.wait_ge(msg_ready, cc * PAIRS + (2 * jj + g + 1))
                    for u in range(2 * g, 2 * g + 2):
                        t = jj * QT + u
                        wait_past(pe, added, cc * T + (t - 1))
                        one_hot = hot_e[:, jj % 2, u, :]
                        for h in range(2):
                            nc.tensor.matmul(o_ps[:, u % 2, h * P:(h + 1) * P], msg[:, u, h * P:(h + 1) * P], one_hot,
                                             start=True, stop=True)
                        nc.tensor.matmul(o_ps[0:2 * H, u % 2, 2 * P:3 * P], exs[:, pp, t, :], one_hot,
                                         start=True, stop=True).then_inc(sum_done, 1)

                def softmax(cc, pp, part):
                    did = cc * SOFT
                    sm = sm_ps[:, pp]
                    if part == 0:
                        pe.wait_ge(lg_ready, (cc + 1) * PAIRS)
                        for a in range(2):
                            last = nc.tensor.transpose(sm[:, a * P:(a + 1) * P], lg[:, pp, a].rearrange("p h t -> p (h t)"),
                                                       k.ident[:, :])
                        last.then_inc(rows_done, 1)
                    if part == 1:
                        pe.wait_ge(soft, did + 5)
                        nc.tensor.transpose(sm[0:1, 0:P], top[:, 0:1], k.ident[:, :])
                        nc.tensor.transpose(sm[0:1, P:2 * P], top[:, P - 1:P], k.ident[:, :]).then_inc(ends_done, 1)
                    if part == 2:
                        pe.wait_ge(soft, did + 11)
                        nc.tensor.matmul(sm[:, 0:1], reach_t[:, :, :].rearrange("p h t -> p (h t)"), k.one[0:1, 0:1], start=True,
                                         stop=True)
                        nc.tensor.matmul(sm[:, 1:2], reach_b[:, :, :].rearrange("p h t -> p (h t)"), k.one[0:1, 0:1], start=True,
                                         stop=True).then_inc(reach_done, 1)
                    if part == 3:
                        pe.wait_ge(soft, did + 14)
                        nc.tensor.transpose(sm[0:1, P:2 * P], peak[:, 0:1], k.ident[:, :]).then_inc(peak_done, 1)
                    if part == 4:
                        pe.wait_ge(soft, did + 17)
                        for a in range(2):
                            nc.tensor.transpose(sm[:, EX + a * P:EX + (a + 1) * P], expo[:, a], k.ident[:, :])
                        pe.wait_ge(faded_ready, cc + 1)
                        for b, heads in enumerate(((0, 1), (2, 3), range(H))):
                            for h in heads:
                                last = nc.tensor.matmul(sm[:, 2 + b:3 + b], k.head_rows[:, h if b == 2 else H + h % 2, :],
                                                        faded[0:1, h:h + 1], start=(h == heads[0]), stop=(h == heads[-1]))
                        last.then_inc(turned, 1)

                def step(c, p, logits, sums):
                    def soften(parts, j):
                        if softmax_in(c) and j in parts:
                            softmax(c - 1, 1 - p, parts[j])

                    for j in range(QUADS):
                        b, jj = sums[j] if sums[j:j + 1] and sums[j] else (0, 0)
                        for g in range(2):
                            if logits:
                                logits_of(c, p, j, g)
                            if g == 1:
                                soften({0: 0, 1: 1, 2: 3, 3: 4}, j)
                            if b:
                                sums_of(c - b, (p + b) % 2, jj, g)
                            if g == 0:
                                soften({2: 2}, j)

                pe.wait_ge(masks, 1)
                steps(pe, step)


def batch_scale(nc, link, stats, par, scale, tmp, root):
    for h in range(DH):
        link(nc.vector.bn_aggr(tmp[:, h, 0:2], stats[:, h]))
    link(nc.vector.tensor_copy(tmp[:, :, 2], tmp[:, :, 1]))
    root(tmp[:, :, 2])
    inverse_root(nc, link, tmp[:, :, 1], tmp[:, :, 2], tmp[:, :, 3])
    link(nc.vector.tensor_tensor(scale[:, 0], par[:, 0], tmp[:, :, 1], ALU.mult))
    link(nc.vector.tensor_tensor(tmp[:, :, 0], tmp[:, :, 0], scale[:, 0], ALU.mult))
    link(nc.vector.tensor_tensor(scale[:, 1], par[:, 1], tmp[:, :, 0], ALU.subtract))


def join_heads(nc, k):
    with ExitStack() as ctx:
        sb = lambda name, shape, dt=F32: ctx.enter_context(nc.sbuf_tensor(name, shape, dt))
        pb = lambda name, shape: ctx.enter_context(nc.psum_tensor(name, shape, F32))
        sem = lambda name: ctx.enter_context(nc.semaphore(name))
        par = sb("j_par", [P, 2, DH])
        bias = sb("j_bias", [P, DH])
        heads = sb("j_heads", [P, 2, W])
        over = sb("j_over", [R, TILES, H])
        share = sb("j_share", [R, TILES, H])
        over_f = sb("j_over_f", [R, 2, 2, D])
        xl = sb("j_xl", [R, 2, 2, D])
        z = sb("j_z", [R, 2, 2, D])
        own = sb("j_own", [R, 2, 2, D])
        stats = sb("j_stats", [P, DH, CHUNKS, 6])
        tmp = sb("j_tmp", [P, DH, 4])
        sums_ps = pb("j_sums_ps", [R, TILES, 2 * H])
        over_ps = pb("j_over_ps", [P, 2, 2, 256])
        own_ps = pb("j_own_ps", [P, 2, 2, 256])
        par_in = sem("j_par_in")
        heads_ready, heads_turned, share_ready = sem("j_heads_s"), sem("j_heads_turned"), sem("j_share_s")
        xl_in = [sem("j_xl_in0"), sem("j_xl_in1")]
        z_in = [sem("j_z_in0"), sem("j_z_in1")]
        over_ready, own_scaled, own_ready, turned, did = (sem("j_over_s"), sem("j_own_scaled"), sem("j_own_s"),
                                                          sem("j_turned"), sem("j_did"))
        STEPS = 5

        with nc.Block() as block:

            @block.sync
            def _(sp):
                with nc.allow_non_contiguous_dma(reason="one number of each feature"):
                    for i, v in enumerate((k.gamma1, k.beta1)):
                        sp.dma_start(par[:, i], v.rearrange("(h p) -> p h", p=P)).then_inc(par_in, 16)
                    sp.dma_start(bias[:, :], k.bias.rearrange("(h p) -> p h", p=P)).then_inc(par_in, 16)

                def load(c, s):
                    wait_past(sp, own_ready, c - 1)
                    sp.dma_start(xl[:, s], k.xl_rows[bass.ds(c * W, W), 0:D].rearrange("(u p) d -> p u d", p=R)
                                 ).then_inc(xl_in[s], 16)
                    sp.dma_start(z[:, s], k.z_rows[bass.ds(c * W, W), :].rearrange("(u p) d -> p u d", p=R)
                                 ).then_inc(z_in[s], 16)

                tiles(sp, CHUNKS, 2, 2, load)

            @block.gpsimd
            def _(pool):
                pool.wait_ge(share_ready, 1)

                def own_messages(c, s):
                    pool.wait_ge(xl_in[s], (c - s) * 8 + 16)
                    wait_past(pool, turned, c - 1)
                    split_heads = lambda a: a.rearrange("p u (h c) -> p u h c", c=C)
                    nc.gpsimd.tensor_tensor(split_heads(own[:, s]), split_heads(xl[:, s]),
                                            share[:, bass.ds(c * 2, 2), :][:, :, :, None].to_broadcast([R, 2, H, C]),
                                            ALU.mult).then_inc(own_scaled, 1)
                    pool.wait_ge(z_in[s], (c - s) * 8 + 16)
                    pool.wait_ge(own_scaled, c + 1)
                    nc.gpsimd.tensor_tensor(own[:, s], own[:, s], z[:, s], ALU.add).then_inc(own_ready, 1)

                tiles(pool, CHUNKS, 2, 2, own_messages)

            @block.vector
            def _(dve):
                link = link_on(dve, k)
                dve.wait_ge(heads_turned, CHUNKS)
                link(nc.vector.tensor_copy(share[:, :, :], sums_ps[:, :, H:2 * H]))
                link(nc.vector.tensor_tensor(over[:, :, :], sums_ps[:, :, 0:H], share[:, :, :], ALU.add))
                link(nc.vector.tensor_scalar(over[:, :, :], over[:, :, :], SEG_EPS, None, ALU.add))
                link(nc.vector.reciprocal(over[:, :, :], over[:, :, :]))
                nc.vector.tensor_tensor(share[:, :, :], share[:, :, :], over[:, :, :], ALU.mult).then_inc(share_ready, 1)
                dve.wait_ge(par_in, 48)

                def join(c, s):
                    def step(i, ins):
                        ins.then_inc(did, 1)

                    acc = k.acc[:, 0:DH, bass.ds(c * W, W)]
                    half = lambda h: k.acc[:, h, bass.ds(c * W, W)]
                    dve.wait_ge(turned, c + 1)
                    step(1, nc.vector.tensor_tensor(acc, over_ps[:, s, :, 0:W], acc, ALU.mult))
                    dve.wait_ge(did, c * STEPS + 1)
                    for h in range(DH):
                        step(2 + h, nc.vector.scalar_tensor_tensor(half(h), own_ps[:, s, h, 0:W], bias[:, h:h + 1], half(h),
                                                                   ALU.add, ALU.add))
                    for h in range(DH):
                        dve.wait_ge(did, c * STEPS + (2 + h))
                        step(4 + h, nc.vector.bn_stats(stats[:, h, bass.ds(c, 1), :], half(h)))

                tiles(dve, CHUNKS, 2, 2, join)
                dve.wait_ge(did, CHUNKS * STEPS)

                root = lambda var: ask_root(nc, k, dve, var)
                batch_scale(nc, link, stats, par, k.norm1, tmp, root)

            @block.scalar
            def _(act):
                def take_heads(c, s):
                    wait_past(act, heads_turned, c - 1)
                    nc.scalar.copy(heads[:, s], k.acc[:, DH, bass.ds(c * W, W)]).then_inc(heads_ready, 1)

                tiles(act, CHUNKS, 2, 2, take_heads)
                act.wait_ge(share_ready, 1)

                def spread(c, s):
                    wait_past(act, turned, c - 1)
                    nc.scalar.copy(over_f[:, s].rearrange("p u (h c) -> p u h c", c=C),
                                   over[:, bass.ds(c * 2, 2), :][:, :, :, None].to_broadcast([R, 2, H, C])
                                   ).then_inc(over_ready, 1)

                tiles(act, CHUNKS, 2, 2, spread)
                give_root(nc, k, act, tmp[:, :, 3], tmp[:, :, 2])

            @block.tensor
            def _(pe):
                def turn_heads(c, s):
                    pe.wait_ge(heads_ready, c + 1)
                    for u in range(2):
                        last = nc.tensor.matmul(sums_ps[:, bass.ds(c * 2 + u, 1), :].rearrange("p o k -> p (o k)"),
                                                heads[:, s, u * R:(u + 1) * R], k.ident[:, 0:2 * H], start=True, stop=True)
                    last.then_inc(heads_turned, 1)

                tiles(pe, CHUNKS, 2, 2, turn_heads)

                def turn(c, s):
                    wait_past(pe, did, (c - 2) * STEPS + 3)
                    for rows, out, ready in ((over_f, over_ps, over_ready), (own, own_ps, own_ready)):
                        pe.wait_ge(ready, c + 1)
                        for h in range(DH):
                            for u in range(2):
                                last = nc.tensor.transpose(out[:, s, h, u * R:(u + 1) * R], rows[:, s, u, h * P:(h + 1) * P],
                                                           k.ident[0:R, 0:R])
                    last.then_inc(turned, 1)

                tiles(pe, CHUNKS, 2, 2, turn)


def feed_forward(nc, k):
    with ExitStack() as ctx:
        sb = lambda name, shape, dt=F32: ctx.enter_context(nc.sbuf_tensor(name, shape, dt))
        pb = lambda name, shape: ctx.enter_context(nc.psum_tensor(name, shape, F32))
        sem = lambda name: ctx.enter_context(nc.semaphore(name))
        w1 = sb("f_w1", [P, DH, D])
        w2 = sb("f_w2", [P, DH, D])
        b1 = sb("f_b1", [P, DH])
        b2 = sb("f_b2", [P, DH])
        par = sb("f_par", [P, 2, DH])
        hid = sb("f_hid", [P, 2, DH, W])
        stats = sb("f_stats", [P, DH, CHUNKS, 6])
        tmp = sb("f_tmp", [P, DH, 4])
        up_ps = pb("f_up_ps", [P, 2, 2, 256])
        down_ps = pb("f_down_ps", [P, 2, 2, 256])
        w_in = sem("f_w_in")
        normed, up_done, hid_ready, down_done, summed, measured = (sem("f_normed"), sem("f_up"), sem("f_hid_s"), sem("f_down"),
                                                                   sem("f_summed"), sem("f_measured"))

        with nc.Block() as block:

            @block.sync
            def _(sp):
                for w, v in ((w1, k.W1), (w2, k.W2)):
                    sp.dma_start(w[:, :, :], v.rearrange("(h p) n -> p h n", p=P)).then_inc(w_in, 16)
                with nc.allow_non_contiguous_dma(reason="one number of each feature"):
                    for out, v in ((b1[:, :], k.b1), (b2[:, :], k.b2), (par[:, 0], k.gamma2), (par[:, 1], k.beta2)):
                        sp.dma_start(out, v.rearrange("(h p) -> p h", p=P)).then_inc(w_in, 16)
                for e in range(E):
                    sp.dma_start(k.we1[:, e], k.We1[e].rearrange("(h p) n -> p h n", p=P)).then_inc(k.experts_in, 16)
                    sp.dma_start(k.we2[:, e], k.We2[e].rearrange("(h p) n -> p h n", p=P)).then_inc(k.experts_in, 16)

            @block.vector
            def _(dve):
                link = link_on(dve, k)
                dve.wait_ge(w_in, 96)

                def add(c, s):
                    dve.wait_ge(down_done, c + 1)
                    dve.wait_ge(normed, 2 * c + 2)
                    for h in range(DH):
                        at = k.acc[:, h, bass.ds(c * W, W)]
                        nc.vector.scalar_tensor_tensor(at, down_ps[:, s, h, 0:W], b2[:, h:h + 1], at, ALU.add,
                                                       ALU.add).then_inc(summed, 1)
                    for h in range(DH):
                        dve.wait_ge(summed, 2 * c + (h + 1))
                        nc.vector.bn_stats(stats[:, h, bass.ds(c, 1), :],
                                           k.acc[:, h, bass.ds(c * W, W)]).then_inc(measured, 1)

                tiles(dve, CHUNKS, 2, 2, add)
                dve.wait_ge(measured, 2 * CHUNKS)

                root = lambda var: ask_root(nc, k, dve, var)
                batch_scale(nc, link, stats, par, k.norm2, tmp, root)

            @block.scalar
            def _(act):
                act.wait_ge(w_in, 96)

                def norm(c, s):
                    for h in range(DH):
                        at = k.acc[:, h, bass.ds(c * W, W)]
                        nc.scalar.activation(at, at, ACT.Identity, scale=k.norm1[:, 0, h:h + 1],
                                             bias=k.norm1[:, 1, h:h + 1]).then_inc(normed, 1)

                def act_up(c, s):
                    act.wait_ge(up_done, c + 1)
                    wait_past(act, down_done, c - 1)
                    for h in range(DH):
                        nc.scalar.activation(hid[:, s, h], up_ps[:, s, h, 0:W], ACT.Relu,
                                             bias=b1[:, h:h + 1]).then_inc(hid_ready, 1)

                norm(0, 0)
                norm(1, 1)

                def both(c, s):
                    norm(c + 2, s)
                    act_up(c, s)

                tiles(act, CHUNKS - 2, 3, 2, both)
                for c in range(CHUNKS - 2, CHUNKS):
                    act_up(c, c % 2)
                give_root(nc, k, act, tmp[:, :, 3], tmp[:, :, 2])

            @block.tensor
            def _(pe):
                def up(c, s):
                    pe.wait_ge(normed, 2 * c + 2)
                    wait_past(pe, hid_ready, 2 * c - 2)
                    for o in range(DH):
                        for h in range(DH):
                            last = nc.tensor.matmul(up_ps[:, s, o, 0:W], w1[:, h, o * P:(o + 1) * P],
                                                    k.acc[:, h, bass.ds(c * W, W)], start=(h == 0), stop=(h == DH - 1))
                    last.then_inc(up_done, 1)

                def down(c, s):
                    pe.wait_ge(hid_ready, 2 * c + 2)
                    wait_past(pe, summed, 2 * c - 2)
                    for o in range(DH):
                        for h in range(DH):
                            last = nc.tensor.matmul(down_ps[:, s, o, 0:W], w2[:, h, o * P:(o + 1) * P], hid[:, s, h],
                                                    start=(h == 0), stop=(h == DH - 1))
                    last.then_inc(down_done, 1)

                pe.wait_ge(w_in, 96)
                up(0, 0)

                def both(c, s):
                    up(c + 1, 1 - s)
                    down(c, s)

                tiles(pe, CHUNKS - 1, 2, 2, both)
                down(CHUNKS - 1, (CHUNKS - 1) % 2)


def route_tokens(nc, k):
    G = 5
    GROUPS = TILES // G
    ROWS = G * K
    assert GROUPS % 2 == 0
    with ExitStack() as ctx:
        sb = lambda name, shape, dt=F32: ctx.enter_context(nc.sbuf_tensor(name, shape, dt))
        pb = lambda name, shape: ctx.enter_context(nc.psum_tensor(name, shape, F32))
        sem = lambda name: ctx.enter_context(nc.semaphore(name))
        space = [k.acc[:, DH, :], 0]

        def work(rows, shape):
            n = int(np.prod(shape))
            at = space[0][0:rows, space[1]:space[1] + n]
            space[1] += n
            names = "abcd"[:len(shape)]
            if len(shape) == 1:
                return at
            return at.rearrange(f"p ({' '.join(names)}) -> p {' '.join(names)}", **dict(zip(names[1:], shape[1:])))

        pad = space[0][:, 0:ZW]
        x_in_sb = work(R, (2, 2, D))
        z = work(R, (2, G, D))
        zr = k.acc[0:R, 0:DH, :].rearrange("p h n -> p (h n)")[:, E * (HID + D):E * (HID + D) + 2 * ROWS * ZW].rearrange(
            "p (s q d) -> p s q d", s=2, q=ROWS)
        y = sb("r_y", [P, 2, DH, W])
        zt = sb("r_zt", [P, 2, DH, R])
        wg = sb("r_wg", [P, DH, E])
        bg = sb("r_bg", [1, E])
        ones = sb("r_ones", [P, P])
        below = sb("r_below", [R, R])
        stats = sb("r_stats", [R, TILES, 6])
        mean = sb("r_mean", [R, TILES])
        rstd = sb("r_rstd", [R, TILES])
        tmp = sb("r_tmp", [R, 2, TILES])
        left = sb("r_left", [R, G, E])
        mark = sb("r_mark", [R, G, E])
        which = sb("r_which", [R, G, E])
        chosen = sb("r_chosen", [R, K, G, E])
        either = sb("r_either", [R, G, E])
        rank = sb("r_rank", [R, G, E])
        best = sb("r_best", [R, G])
        total = sb("r_total", [P, E, G])
        before = sb("r_before", [P, E, G])
        opened = sb("r_opened", [P, E, G])
        count = sb("r_count", [P, E])
        place = sb("r_place", [R, K, G])
        ids_i = sb("r_ids_i", [R, TILES, K], I32)
        ids = sb("r_ids", [R, TILES * K])
        idx = sb("r_idx", [R, 2, ROWS], I32)
        expert = sb("r_expert", [P, E])
        region = sb("r_region", [P, E])
        pad_at = sb("r_pad_at", [1, E], I32)
        nt = sb("r_nt", [1, E])
        end = sb("r_end", [1, E])
        jump = sb("r_jump", [1, E])
        steps_of = sb("r_steps_of", [1, NT])
        past = sb("r_past", [1, SLOT_TILES, E])
        slot_f = sb("r_slot_f", [1, 2, SLOT_TILES])
        y_ps = pb("r_y_ps", [R, 2, 2, D])
        zt_ps = pb("r_zt_ps", [P, 2, DH, 256])
        score_ps = pb("r_score_ps", [R, 2, 512])
        rank_ps = pb("r_rank_ps", [P, 2, 256])

        w_in, iotas = sem("r_w_in"), sem("r_iotas")
        x_in = [sem("r_x_in0"), sem("r_x_in1")]
        y_ready, y_turned, summed, measured = sem("r_y_s"), sem("r_y_turned"), sem("r_summed"), sem("r_measured")
        z_ready, z_turned, z_taken, scored = sem("r_z_s"), sem("r_z_turned"), sem("r_z_taken"), sem("r_scored")
        masked, ranked, routed = sem("r_masked"), sem("r_ranked"), sem("r_routed")
        copied, rows_ready = sem("r_copied"), sem("r_rows_s")
        scattered = [sem("r_scattered0"), sem("r_scattered1")]
        pads_ready, pads_stored = sem("r_pads"), sem("r_pads_stored")

        with nc.Block() as block:

            @block.sync
            def _(sp):
                sp.dma_start(wg[:, :, :], k.Wg.rearrange("(h p) e -> p h e", p=P)).then_inc(w_in, 16)
                sp.dma_start(bg[:, :], k.bg.rearrange("(o e) -> o e", o=1)).then_inc(w_in, 16)

                def load(c, s):
                    wait_past(sp, summed, c - 1)
                    sp.dma_start(x_in_sb[:, s], k.x[bass.ds(c * W, W), :].rearrange("(u p) d -> p u d", p=R)
                                 ).then_inc(x_in[s], 16)

                tiles(sp, CHUNKS, 2, 2, load)
                sp.wait_ge(y_turned, CHUNKS)
                for e in range(E):
                    sp.dma_start(k.be1_all[:, e], k.be1[e].partition_broadcast(P)).then_inc(k.bias_in, 16)
                    sp.dma_start(k.be2_all[:, e], k.be2[e].partition_broadcast(P)).then_inc(k.bias_in, 16)
                sp.wait_ge(pads_ready, 1)
                rows = nc.values_load_multi_w_load_instructions(pad_at[:, 0:E], engines=[mybir.EngineType.SP], min_val=0,
                                                                max_val=E * REGION - P)[1]
                for row in (*rows, E * REGION):
                    sp.dma_start(k.disp_rows[bass.ds(row, P), :], pad[:, :]).then_inc(pads_stored, 16)
                sp.wait_ge(pads_stored, 16 * (E + 1))

            @block.scalar
            def _(act):
                def norm(c, s):
                    wait_past(act, y_turned, c - 1)
                    for h in range(DH):
                        nc.scalar.activation(y[:, s, h], k.acc[:, h, bass.ds(c * W, W)], ACT.Identity,
                                             scale=k.norm2[:, 0, h:h + 1], bias=k.norm2[:, 1, h:h + 1]).then_inc(y_ready, 1)

                tiles(act, CHUNKS, 2, 2, norm)
                give_root(nc, k, act, tmp[:, 1, :], tmp[:, 0, :])

                def take(g, s):
                    for i in range(G):
                        t, q = g * G + i, (s * G + i) % 2
                        act.wait_ge(z_turned, t + 1)
                        wait_past(act, scored, t - 1)
                        nc.scalar.copy(zt[:, q], zt_ps[:, q, :, 0:R]).then_inc(z_taken, 1)

                def copy(g, s):
                    act.wait_ge(z_ready, g * G + G)
                    if not isinstance(g, int) or g >= 2:
                        act.wait_ge(scattered[s], (g - s) * (8 * ROWS))
                    for i in range(G):
                        nc.scalar.copy(zr[:, s, i * K:(i + 1) * K, 0:D],
                                       z[:, s, i:i + 1, :].to_broadcast([R, K, D])).then_inc(copied, 1)

                take(0, 0)
                copy(0, 0)
                take(1, 1)

                def both(g, s):
                    copy(g + 1, 1 - s)
                    take(g + 2, s)

                tiles(act, GROUPS - 2, 2, 2, both)
                copy(GROUPS - 1, 1)

            @block.tensor
            def _(pe):
                def turn_y(c, s):
                    pe.wait_ge(y_ready, 2 * c + 2)
                    wait_past(pe, summed, c - 1)
                    for u in range(2):
                        for h in range(DH):
                            last = nc.tensor.transpose(y_ps[:, s, u, h * P:(h + 1) * P], y[:, s, h, u * R:(u + 1) * R],
                                                       k.ident[:, :])
                    last.then_inc(y_turned, 1)

                tiles(pe, CHUNKS, 2, 2, turn_y)
                pe.wait_ge(w_in, 32)

                def turn_z(g, s, i):
                    t, q = g * G + i, (s * G + i) % 2
                    pe.wait_ge(z_ready, t + 1)
                    wait_past(pe, z_taken, t - 1)
                    for h in range(DH):
                        last = nc.tensor.transpose(zt_ps[:, q, h, 0:R], z[:, s, i, h * P:(h + 1) * P], k.ident[0:R, 0:R])
                    last.then_inc(z_turned, 1)

                def score_of(g, s, i):
                    t, q = g * G + i, (s * G + i) % 2
                    pe.wait_ge(z_taken, t + 1)
                    wait_past(pe, masked, g - 1)
                    out = score_ps[:, s, i * E:(i + 1) * E]
                    for h in range(DH):
                        nc.tensor.matmul(out, zt[:, q, h], wg[:, h, :], start=(h == 0), stop=False)
                    nc.tensor.matmul(out, ones[0:1, 0:R], bg[:, :], start=False, stop=True).then_inc(scored, 1)

                def scores(g, s, between=lambda: None):
                    turn_z(g, s, 0)
                    for i in range(G):
                        if i + 1 < G:
                            turn_z(g, s, i + 1)
                        score_of(g, s, i)
                        if i == 0:
                            between()

                def ranks(g):
                    pe.wait_ge(masked, g + 1)
                    flat = either[:, :, :].rearrange("p t e -> p (t e)")
                    nc.tensor.matmul(rank_ps[0:R, 0, 0:G * E], below[:, :], flat, start=True, stop=True)
                    nc.tensor.matmul(rank_ps[:, 1, 0:G * E], ones[0:R, :], flat, start=True, stop=True).then_inc(ranked, 1)

                scores(0, 0)
                ranks(0)
                scores(1, 1)

                def both(g, s):
                    scores(g + 2, s, lambda: ranks(g + 1))

                tiles(pe, GROUPS - 2, 2, 2, both)
                ranks(GROUPS - 1)

            @block.vector
            def _(dve):
                link = link_on(dve, k)
                link(nc.vector.memset(ones[:, :], 1.0))
                nc.vector.tensor_scalar(below[:, :], k.iota_row[0:R, 0:R], k.iota_col[0:R, 0:1], None, ALU.is_gt)
                nc.vector.tensor_scalar(expert[:, :], k.iota_row[:, 0:E], float(-E), None, ALU.add)
                nc.vector.tensor_scalar(region[:, :], k.iota_row[:, 0:E], float(REGION), None, ALU.mult)
                nc.vector.tensor_scalar(steps_of[:, :], k.iota_row[0:1, 0:NT], float(P), None, ALU.mult)
                nc.vector.memset(opened[:, :, :], 1.0)
                link(nc.vector.memset(count[:, :], 0.0))
                link(nc.vector.memset(opened[:, :, 0:1], 0.0))
                dve.wait_ge(iotas, 1)
                link(nc.vector.tensor_copy(ids[:, :], ids_i[:, :, :].rearrange("p t j -> p (t j)")))

                def add(c, q):
                    s = q % 2
                    dve.wait_ge(y_turned, c + 1)
                    dve.wait_ge(x_in[s], (c - s) * 8 + 16)
                    nc.vector.tensor_tensor(k.x1[:, bass.ds(c * 2, 2), :], y_ps[:, s], x_in_sb[:, s], ALU.add
                                            ).then_inc(summed, 1)
                    dve.wait_ge(summed, c + 1)
                    for u in range(2):
                        nc.vector.bn_stats(stats[:, bass.ds(c * 2 + u, 1), :],
                                           k.x1[:, bass.ds(c * 2 + u, 1), :]).then_inc(measured, 1)

                tiles(dve, CHUNKS, 2, 4, add)
                dve.wait_ge(measured, TILES)
                nc.vector.memset(pad[:, 0:D], 0.0)
                nc.vector.memset(pad[:, D:ZW], float(NO_ROW))
                norm_scale(nc, link, stats, mean[:, :], rstd[:, :], tmp, lambda var: ask_root(nc, k, dve, var))

                def norm(g, s):
                    wait_past(dve, z_turned, (g - 1) * G)
                    wait_past(dve, copied, (g - 1) * G)
                    for i in range(G):
                        t = bass.ds(g * G + i, 1)
                        nc.vector.tensor_scalar(z[:, s, i], k.x1[:, t, :].rearrange("p o d -> p (o d)"), mean[:, t],
                                                rstd[:, t], ALU.subtract, ALU.mult).then_inc(z_ready, 1)

                STEPS = 22
                spread_e = lambda a: a[:, :, None].to_broadcast([R, G, E])
                experts = expert[0:R, None, :].to_broadcast([R, G, E])

                def step_of(g):
                    def step(i, ins):
                        ins.then_inc(routed, 1)
                        dve.wait_ge(routed, g * STEPS + i)

                    return step

                def choose(g, s):
                    step = step_of(g)
                    dve.wait_ge(scored, g * G + G)
                    score = score_ps[:, s, 0:G * E].rearrange("p (t e) -> p t e", e=E)
                    for i in range(K):
                        step(6 * i + 1, nc.vector.tensor_reduce(best[:, :], score, AX.X, ALU.max))
                        step(6 * i + 2, nc.vector.tensor_tensor(mark[:, :, :], score, spread_e(best), ALU.is_ge))
                        step(6 * i + 3, nc.vector.tensor_tensor(which[:, :, :], mark[:, :, :], experts, ALU.mult))
                        step(6 * i + 4, nc.vector.tensor_reduce(best[:, :], which[:, :, :], AX.X, ALU.min))
                        step(6 * i + 5, nc.vector.tensor_tensor(chosen[:, i], experts, spread_e(best), ALU.is_equal))
                        if i == 0:
                            step(6, nc.vector.scalar_tensor_tensor(left[:, :, :], chosen[:, 0], -NEG, score, ALU.mult, ALU.add))
                            score = left[:, :, :]
                    step(12, nc.vector.tensor_tensor(either[:, :, :], chosen[:, 0], chosen[:, 1], ALU.add))
                    nc.vector.memset(best[:, :], 0.0).then_inc(masked, 1)

                def places(g):
                    step = step_of(g)
                    dve.wait_ge(ranked, g + 1)
                    flat = lambda a: a[:, :, :].rearrange("p e t -> p (e t)")
                    tile_first = lambda a: a.rearrange("p (t e) -> p t e", e=E)
                    step(13, nc.vector.tensor_copy(total[:, :, :], rank_ps[:, 1, 0:G * E].rearrange("p (t e) -> p e t", e=E)))
                    step(14, nc.vector.tensor_tensor_scan(flat(before), flat(opened), flat(total), 0.0, ALU.mult, ALU.add))
                    step(15, nc.vector.tensor_tensor(total[:, :, :], before[:, :, :], total[:, :, :], ALU.subtract))
                    step(16, nc.vector.tensor_tensor(rank[:, :, :], tile_first(rank_ps[0:R, 0, 0:G * E]),
                                                     total[0:R].rearrange("p e t -> p t e"), ALU.add))
                    step(17, nc.vector.tensor_tensor(rank[:, :, :], rank[:, :, :],
                                                     region[0:R, None, :].to_broadcast([R, G, E]), ALU.add))
                    step(18, nc.vector.tensor_tensor(region[:, :], region[:, :], before[:, :, G - 1], ALU.add))
                    for i in range(K):
                        step(19 + 2 * i, nc.vector.tensor_tensor(which[:, :, :], rank[:, :, :], chosen[:, i], ALU.mult))
                        step(20 + 2 * i, nc.vector.tensor_reduce(place[:, i], which[:, :, :], AX.X, ALU.add))

                def rows(g, s):
                    if not isinstance(g, int) or g >= 2:
                        dve.wait_ge(scattered[s], (g - s) * (8 * ROWS))
                    nc.vector.tensor_copy(zr[:, s, :, D:ZW], ids[:, bass.ds(g * ROWS, ROWS)][:, :, None])
                    nc.vector.tensor_copy(idx[:, s].rearrange("p (t j) -> p j t", j=K), place[:, :, :]).then_inc(rows_ready, 1)

                def close():
                    nc.vector.tensor_copy(pad_at[:, :], region[0:1, :]).then_inc(pads_ready, 1)
                    link(nc.vector.scalar_tensor_tensor(count[:, :], k.iota_row[:, 0:E], float(-REGION), region[:, :], ALU.mult,
                                                        ALU.add))
                    link(nc.vector.tensor_tensor(past[:, 0:NT, :], count[0:1, None, :].to_broadcast([1, NT, E]),
                                                 steps_of[:, :, None].to_broadcast([1, NT, E]), ALU.is_gt))
                    link(nc.vector.tensor_reduce(nt[:, :], past[:, 0:NT, :].rearrange("p j e -> p e j"), AX.X, ALU.add))
                    link(nc.vector.tensor_tensor_scan(end[:, :], ones[0:1, 0:E], nt[:, :], 0.0, ALU.mult, ALU.add))
                    link(nc.vector.tensor_scalar(jump[:, :], nt[:, :], float(-P), float(REGION), ALU.mult, ALU.add))
                    slots = k.iota_row[0:1, 0:SLOT_TILES]
                    spread_s = lambda a: a[:, None, :].to_broadcast([1, SLOT_TILES, E])
                    link(nc.vector.tensor_tensor(past[:, :, :], slots[:, :, None].to_broadcast([1, SLOT_TILES, E]),
                                                 spread_s(end), ALU.is_ge))
                    link(nc.vector.tensor_reduce(slot_f[:, 1], past[:, :, :], AX.X, ALU.add))
                    link(nc.vector.tensor_tensor(past[:, :, :], past[:, :, :], spread_s(jump), ALU.mult))
                    link(nc.vector.tensor_reduce(slot_f[:, 0], past[:, :, :], AX.X, ALU.add))
                    link(nc.vector.scalar_tensor_tensor(slot_f[:, 0], slots, float(P), slot_f[:, 0], ALU.mult, ALU.add))
                    link(nc.vector.tensor_scalar(k.slots[:, 0], slot_f[:, 0], float(E * REGION), None, ALU.min))
                    link(nc.vector.tensor_scalar(k.slots[:, 1], slot_f[:, 1], float(E - 1), None, ALU.min))

                norm(0, 0)
                choose(0, 0)
                norm(1, 1)
                places(0)

                def group(g, s):
                    rows(g, s)
                    norm(g + 2, s)
                    choose(g + 1, 1 - s)
                    places(g + 1)

                tiles(dve, GROUPS - 2, 2, 2, group)
                rows(GROUPS - 2, 0)
                choose(GROUPS - 1, 1)
                places(GROUPS - 1)
                rows(GROUPS - 1, 1)
                close()

            @block.gpsimd
            def _(pool):
                nc.gpsimd.iota(ids_i[:, :, :], [[2 * R, TILES], [1, K]], base=0, channel_multiplier=K).then_inc(iotas, 1)

                def scatter(g, s):
                    pool.wait_ge(rows_ready, g + 1)
                    for i in range(G):
                        pool.wait_ge(copied, g * G + (i + 1))
                        pool.sem_inc(k.taken, 1)
                        for q in range(i * K, (i + 1) * K):
                            nc.gpsimd.indirect_dma_start(k.disp_rows, bass.IndirectOffsetOnAxis(ap=idx[:, s, q:q + 1], axis=0),
                                                         zr[:, s, q, :], None).then_inc(scattered[s], 16)

                tiles(pool, GROUPS, 2, 2, scatter)
                for s in range(2):
                    pool.wait_ge(scattered[s], 8 * ROWS * GROUPS)


def apply_experts(nc, k):
    RING = 4
    with ExitStack() as ctx:
        pb = lambda name, shape: ctx.enter_context(nc.psum_tensor(name, shape, F32))
        sb = lambda name, shape, dt=F32: ctx.enter_context(nc.sbuf_tensor(name, shape, dt))
        sem = lambda name: ctx.enter_context(nc.semaphore(name))
        space = [k.acc[:, 0:DH, :].rearrange("p h n -> p (h n)"), 0]

        def work(shape):
            n = int(np.prod(shape))
            at = space[0][:, space[1]:space[1] + n]
            space[1] += n
            names = "abcd"[:len(shape)]
            return at.rearrange(f"p ({' '.join(names)}) -> p {' '.join(names)}", **dict(zip(names[1:], shape[1:])))

        space[1] = E * (HID + D)
        be1, be2 = k.be1_all, k.be2_all
        z = work((RING, ZW))
        zt = work((2, DH, P))
        hid = work((2, HID))
        hid_t = work((2, HC, P))
        y = work((RING, D))
        idx = sb("x_idx", [P, RING], I32)
        zt_ps = pb("x_zt_ps", [P, 2, 512])
        hid_ps = pb("x_hid_ps", [P, 2, HID])
        hid_t_ps = pb("x_hid_t_ps", [P, 2, HC, P])
        y_ps = pb("x_y_ps", [P, 2, 512])
        z_in = [sem(f"x_z_in{q}") for q in range(RING)]
        stored = [sem(f"x_stored{q}") for q in range(RING)]
        z_turned, zt_ready, up_done, hid_ready, gelu_done = sem("x_z_turned"), sem("x_zt"), sem("x_up"), sem("x_hid_s"), sem("x_gelu")
        hid_turned, hid_t_ready, down_done, y_ready = sem("x_hid_turned"), sem("x_hid_t_s"), sem("x_down"), sem("x_y_s")
        n_main = SLOT_TILES - 2

        with nc.Block() as block:

            @block.sync
            def _(sp):
                def load(s, q):
                    row = nc.values_load_multi_w_load_instructions(k.slots[:, 0, bass.ds(s, 1)],
                                                                    engines=[mybir.EngineType.SP], min_val=0, max_val=E * REGION)[1][0]
                    wait_past(sp, y_ready, s - (RING - 1))
                    sp.dma_start(z[:, q], k.disp_rows[bass.ds(row, P), :]).then_inc(z_in[q], 16)

                tiles(sp, SLOT_TILES, RING, RING, load)

            @block.gpsimd
            def _(pool):
                def store(s, q):
                    pool.wait_ge(y_ready, s + 1)
                    pool.sem_inc(k.taken, 1)
                    nc.gpsimd.indirect_dma_start(k.moe_rows, bass.IndirectOffsetOnAxis(ap=idx[:, q:q + 1], axis=0), y[:, q],
                                                 None, bounds_check=K * N - 1, oob_is_err=False).then_inc(stored[q], 16)

                tiles(pool, SLOT_TILES, RING, RING, store)
                for q in range(RING):
                    pool.wait_ge(stored[q], 16 * len(range(q, SLOT_TILES, RING)))

            @block.tensor
            def _(pe):
                def experts_of(s, n):
                    return nc.values_load_multi_w_load_instructions(
                        k.slots[:, 1, bass.ds(s, n)], engines=[mybir.EngineType.PE], min_val=0, max_val=E - 1)[1]

                def turn_z(s, q):
                    pe.wait_ge(z_in[q % RING], (s - q % RING) * (16 // RING) + 16)
                    wait_past(pe, zt_ready, s - 1)
                    for h in range(DH):
                        last = nc.tensor.transpose(zt_ps[:, q % 2, h * P:(h + 1) * P], z[:, q % RING, h * P:(h + 1) * P],
                                                   k.ident[:, :])
                    last.then_inc(z_turned, 1)

                def up(s, q, e):
                    pe.wait_ge(zt_ready, s + 1)
                    wait_past(pe, hid_ready, s - 1)
                    for h in range(DH):
                        last = nc.tensor.matmul(hid_ps[:, q % 2], zt[:, q % 2, h], k.we1[:, bass.ds(e, 1), h, :].rearrange(
                            "p o n -> p (o n)"), start=(h == 0), stop=(h == DH - 1))
                    last.then_inc(up_done, 1)

                def turn_hid(s, q):
                    pe.wait_ge(gelu_done, s + 1)
                    wait_past(pe, hid_t_ready, s - 1)
                    for j in range(HC):
                        last = nc.tensor.transpose(hid_t_ps[:, q % 2, j], hid[:, q % 2, j * P:(j + 1) * P], k.ident[:, :])
                    last.then_inc(hid_turned, 1)

                def down(s, q, e):
                    pe.wait_ge(hid_t_ready, s + 1)
                    wait_past(pe, y_ready, s - 1)
                    for j in range(HC):
                        last = nc.tensor.matmul(y_ps[:, q % 2, 0:D], hid_t[:, q % 2, j], k.we2[:, bass.ds(e, 1), j, :].rearrange(
                            "p o n -> p (o n)"), start=(j == 0), stop=(j == HC - 1))
                    last.then_inc(down_done, 1)

                pe.wait_ge(k.experts_in, 32 * E)
                turn_z(0, 0)
                turn_z(1, 1)
                up(0, 0, experts_of(0, 1)[0])

                def step(s, q):
                    e = experts_of(s, 2)
                    turn_hid(s, q)
                    up(s + 1, q + 1, e[1])
                    turn_z(s + 2, q + 2)
                    down(s, q, e[0])

                tiles(pe, n_main, RING, RING, step)
                e = experts_of(n_main, 2)
                turn_hid(n_main, n_main % 2)
                up(n_main + 1, n_main + 1, e[1])
                down(n_main, n_main % 2, e[0])
                turn_hid(n_main + 1, n_main + 1)
                down(n_main + 1, n_main + 1, e[1])

            @block.scalar
            def _(act):
                def take_zt(s, q):
                    act.wait_ge(z_turned, s + 1)
                    wait_past(act, up_done, s - 1)
                    nc.scalar.copy(zt[:, q % 2], zt_ps[:, q % 2, 0:D].rearrange("p (h n) -> p h n", h=DH)).then_inc(zt_ready, 1)

                def gelu(s, q):
                    act.wait_ge(hid_ready, s + 1)
                    nc.scalar.activation(hid[:, q % 2], hid[:, q % 2], ACT.Gelu).then_inc(gelu_done, 1)

                take_zt(0, 0)
                take_zt(1, 1)

                def step(s, q):
                    gelu(s, q)
                    take_zt(s + 2, q)

                tiles(act, n_main, 2, 2, step)
                gelu(n_main, n_main)
                gelu(n_main + 1, n_main + 1)

            @block.vector
            def _(dve):
                def experts_of(s, n):
                    return nc.values_load_multi_w_load_instructions(
                        k.slots[:, 1, bass.ds(s, n)], engines=[mybir.EngineType.DVE], min_val=0, max_val=E - 1)[1]

                def bias_up(s, q, e):
                    dve.wait_ge(up_done, s + 1)
                    wait_past(dve, hid_turned, s - 1)
                    nc.vector.tensor_tensor(hid[:, q % 2], hid_ps[:, q % 2],
                                            be1[:, bass.ds(e, 1), :].rearrange("p o n -> p (o n)"), ALU.add).then_inc(hid_ready, 1)

                def take_hid(s, q):
                    dve.wait_ge(hid_turned, s + 1)
                    wait_past(dve, down_done, s - 1)
                    nc.vector.tensor_copy(hid_t[:, q % 2], hid_t_ps[:, q % 2]).then_inc(hid_t_ready, 1)

                def bias_down(s, q, e):
                    if not isinstance(s, int) or s >= RING:
                        dve.wait_ge(stored[q % RING], (s - q % RING) * (16 // RING))
                    nc.vector.tensor_copy(idx[:, q % RING:q % RING + 1], z[:, q % RING, D:ZW])
                    dve.wait_ge(down_done, s + 1)
                    nc.vector.tensor_tensor(y[:, q % RING], y_ps[:, q % 2, 0:D],
                                            be2[:, bass.ds(e, 1), :].rearrange("p o n -> p (o n)"), ALU.add).then_inc(y_ready, 1)

                dve.wait_ge(k.bias_in, 32 * E)
                bias_up(0, 0, experts_of(0, 1)[0])

                def step(s, q):
                    e = experts_of(s, 2)
                    take_hid(s, q)
                    bias_up(s + 1, q + 1, e[1])
                    bias_down(s, q, e[0])

                tiles(dve, SLOT_TILES - 1, RING, RING, step)
                last = SLOT_TILES - 1
                e = experts_of(last, 1)
                take_hid(last, last % RING)
                bias_down(last, last % RING, e[0])


def combine(nc, k):
    STEP = 5
    ROUNDS = TILES // STEP
    with ExitStack() as ctx:
        sem = lambda name: ctx.enter_context(nc.semaphore(name))
        both = k.acc[0:R, 0:DH, :].rearrange("p h n -> p (h n)")[:, 0:2 * STEP * K * D].rearrange(
            "p (s t k d) -> p s t k d", s=2, t=STEP, k=K)
        rows_in, stored = k.results_in, k.results_stored
        first, summed = sem("c_first"), sem("c_summed")

        with nc.Block() as block:

            @block.sync
            def _(sp):
                def load(i, s):
                    wait_past(sp, summed, i - 1)
                    sp.dma_start(both[:, s], k.moe_rows[bass.ds(i * (STEP * R * K), STEP * R * K), :].rearrange(
                        "(t p k) d -> p t k d", p=R, k=K)).then_inc(rows_in[s], 16)

                tiles(sp, ROUNDS, 2, 2, load)

            @block.vector
            def _(dve):
                def add(i, s):
                    x1 = k.x1[:, bass.ds(i * STEP, STEP), :]
                    dve.wait_ge(rows_in[s], (i - s) * 8 + 16)
                    nc.vector.tensor_tensor(both[:, s, :, 0], both[:, s, :, 0], both[:, s, :, 1], ALU.add).then_inc(first, 1)
                    dve.wait_ge(first, i + 1)
                    nc.vector.tensor_tensor(x1, x1, both[:, s, :, 0], ALU.add).then_inc(summed, 1)

                tiles(dve, ROUNDS, 2, 2, add)

            @block.scalar
            def _(act):
                def store(i, s):
                    act.wait_ge(summed, i + 1)
                    act.dma_start(k.out[bass.ds(i * (STEP * R), STEP * R), :].rearrange("(t p) d -> p t d", p=R),
                                  k.x1[:, bass.ds(i * STEP, STEP), :]).then_inc(stored, 16)

                tiles(act, ROUNDS, 2, 2, store)
                act.wait_ge(stored, 16 * ROUNDS)


INS = ["x", "src", "dst", "L0_gnn_W_l", "L0_gnn_W_r", "L0_gnn_att", "L0_gnn_bias", "L0_gnn_W1", "L0_gnn_b1", "L0_gnn_W2",
       "L0_gnn_b2", "L0_gnn_gamma1", "L0_gnn_beta1", "L0_gnn_gamma2", "L0_gnn_beta2", "L0_ffn_Wg", "L0_ffn_bg", "L0_ffn_W1",
       "L0_ffn_b1", "L0_ffn_W2", "L0_ffn_b2"]


def graph_ffn_kernel(nc, *args):
    k = Program()
    *ins, k.out = args
    (k.x, k.src, k.dst, k.W_l, k.W_r, k.att, k.bias, k.W1, k.b1, k.W2, k.b2, k.gamma1, k.beta1, k.gamma2, k.beta2, k.Wg,
     k.bg, k.We1, k.be1, k.We2, k.be2) = ins
    dram = lambda name, shape, dt=F32: nc.dram_tensor(name, shape, dt).ap()
    k.first_rows = dram("first_rows", [ETP + 1])
    k.last_rows = dram("last_rows", [ETP + 1])
    k.base_rows = dram("base_rows", [1, ETP], I32)
    k.rel_rows = dram("rel_rows", [ETP * P], BF16)
    k.gate_rows = dram("gate_rows", [NCH, GATES], BF16)
    k.go_on_rows = dram("go_on_rows", [NCH, T])
    k.xl_rows = dram("xl_rows", [COLS, XW])
    k.xr_rows = dram("xr_rows", [COLS, XW])
    k.z_rows = dram("z_rows", [COLS, D])
    k.disp_rows = dram("disp_rows", [E * REGION + P, ZW])
    k.moe_rows = dram("moe_rows", [K * N, D])

    with ExitStack() as ctx:
        keep = lambda name, shape, dt=F32: ctx.enter_context(nc.sbuf_tensor(name, shape, dt))
        k.iota_row = keep("iota_row", [P, P])
        k.iota_col = keep("iota_col", [P, 1])
        k.ident = keep("ident", [P, P])
        k.norm1 = keep("norm1", [P, 2, DH])
        k.norm2 = keep("norm2", [P, 2, DH])
        k.slots = keep("slots", [1, 2, SLOT_TILES], I32)
        k.acc = keep("acc", [P, DH + 1, COLS])
        k.chain, k.linked = ctx.enter_context(nc.semaphore("chain")), 0
        k.var_ready, k.root_ready, k.asked, k.given = (ctx.enter_context(nc.semaphore("var_ready")),
                                                       ctx.enter_context(nc.semaphore("root_ready")), 0, 0)
        features = k.acc[:, 0:DH, :].rearrange("p h n -> p (h n)")
        k.be1_all = features[:, 0:E * HID].rearrange("p (e n) -> p e n", e=E)
        k.be2_all = features[:, E * HID:E * (HID + D)].rearrange("p (e n) -> p e n", e=E)
        k.bias_in = ctx.enter_context(nc.semaphore("bias_in"))
        k.taken = ctx.enter_context(nc.semaphore("taken"))
        k.experts_in = ctx.enter_context(nc.semaphore("experts_in"))
        k.results_in = [ctx.enter_context(nc.semaphore(f"results_in{s}")) for s in range(2)]
        k.results_stored = ctx.enter_context(nc.semaphore("results_stored"))
        with ExitStack() as edges:
            sb = lambda name, shape, dt=F32: edges.enter_context(nc.sbuf_tensor(name, shape, dt))
            k.neg_col = sb("neg_col", [P, 1])
            k.one = sb("one", [P, 1])
            k.head_rows = sb("head_rows", [1, H + 2, P])
            k.src_e = sb("src_e", [P, ETP], I32)
            k.neg_rel = sb("neg_rel", [P, ETP])
            k.att_pos = sb("att_pos", [P, D])
            k.bases = sb("bases", [1, ETL], I32)
            with ExitStack() as nodes:
                sb = lambda name, shape, dt=F32: nodes.enter_context(nc.sbuf_tensor(name, shape, dt))
                k.x_all = sb("x_all", [P, NTP, D])
                k.w_ext = sb("w_ext", [P, 2, 2, XW])
                k.att_all = sb("att_all", [P, D])
                k.x_in = [nodes.enter_context(nc.semaphore(f"x_in{s}")) for s in range(2)]
                k.w_in = nodes.enter_context(nc.semaphore("w_in"))
                prepare_edges(nc, k)
                project_nodes(nc, k)
            attend(nc, k)
        join_heads(nc, k)
        k.we1 = keep("we1", [P, E, DH, HID])
        k.we2 = keep("we2", [P, E, HC, D])
        feed_forward(nc, k)
        k.x1 = keep("x1", [R, TILES, D])
        route_tokens(nc, k)
        apply_experts(nc, k)
        combine(nc, k)


def kernel(**inputs):
    import concourse.bacc as _bacc
    from concourse.bass_utils import run_bass_kernel_spmd as _run

    nc = _bacc.Bacc("TRN2", target_bir_lowering=False, num_devices=1)
    arrays, args = {}, []
    for name in INS:
        a = np.ascontiguousarray(inputs[name])
        arrays[f"in_{name}_dram"] = a
        args.append(nc.dram_tensor(f"in_{name}_dram", a.shape, mybir.dt.from_np(a.dtype), kind="ExternalInput").ap())
    args.append(nc.dram_tensor("out_dram", (N, D), F32, kind="ExternalOutput").ap())
    graph_ffn_kernel(nc, *args)
    r = _run(nc, [arrays], core_ids=[0])
    return r.results[0]["out_dram"]
```
